# Optimizing a Trainium2 kernel written in Bass

```python
import numpy as np
import jax
import jax.numpy as jnp

def _softmax(x, axis=-1):
    return jax.nn.softmax(x, axis=axis)

def _gelu(x):
    return jax.nn.gelu(x, approximate=True)

def _silu(x):
    return jax.nn.silu(x)

def _sigmoid(x):
    return jax.nn.sigmoid(x)

def _layernorm(x, axis=-1, eps=1e-05):
    m = jnp.mean(x, axis=axis, keepdims=True)
    v = jnp.var(x, axis=axis, keepdims=True)
    return (x - m) / jnp.sqrt(v + eps)

def _scatter_add(tgt, idx, src, axis=0):
    return tgt.at[idx].add(src)

def _segment_sum(src, seg, n):
    return jax.ops.segment_sum(src, seg, n)
kernel_name = 'mk_hybrid_d1_jaxref_r8_8151ef'

def setup_inputs(seed: int=0):
    np.random.seed(seed)
    _w = jnp.asarray

    def _L0_attn_a_setup():
        import jax, jax.numpy as jnp
        import numpy as np
        EMB_DIM = 256
        NUM_HEADS = 16
        HEAD_DIM = EMB_DIM // NUM_HEADS
        B, T = (4, 256)
        key = jax.random.key(seed)
        ks = jax.random.split(key, 6)
        s = lambda fan_in: 1.0 / np.sqrt(fan_in)
        return {'x': jax.random.normal(ks[0], (B, T, EMB_DIM), dtype=jnp.float32), 'Wq': jax.random.normal(ks[1], (EMB_DIM, EMB_DIM), dtype=jnp.float32) * s(EMB_DIM), 'Wk': jax.random.normal(ks[2], (EMB_DIM, HEAD_DIM), dtype=jnp.float32) * s(EMB_DIM), 'Wv': jax.random.normal(ks[3], (EMB_DIM, HEAD_DIM), dtype=jnp.float32) * s(EMB_DIM), 'Wo': jax.random.normal(ks[4], (EMB_DIM, EMB_DIM), dtype=jnp.float32) * s(EMB_DIM), 'bo': jax.random.normal(ks[5], (EMB_DIM,), dtype=jnp.float32) * 0.01}
    _L0_attn_a_in = _L0_attn_a_setup()

    def _L0_attn_b_setup():
        import jax, jax.numpy as jnp
        import numpy as np
        N_HEADS = 16
        N_KV_HEADS = 4
        HEAD_DIM = 128
        D_MODEL = 256
        WINDOW = 128
        THETA = 10000.0
        EPS = 1e-06

        def _rmsnorm(x, w):
            var = jnp.mean(x * x, axis=-1, keepdims=True)
            return x * jax.lax.rsqrt(var + EPS) * w

        def _rope(x, pos):
            d2 = HEAD_DIM // 2
            inv_freq = 1.0 / THETA ** (jnp.arange(0, HEAD_DIM, 2, dtype=jnp.float32) / HEAD_DIM)
            ang = pos[:, None].astype(jnp.float32) * inv_freq[None, :]
            cos = jnp.cos(ang)[None, None]
            sin = jnp.sin(ang)[None, None]
            x1, x2 = (x[..., :d2], x[..., d2:])
            return jnp.concatenate([x1 * cos - x2 * sin, x1 * sin + x2 * cos], axis=-1)
        key = jax.random.key(seed)
        ks = jax.random.split(key, 7)
        B, S = (1, 256)
        s = 0.02
        return {'x': jax.random.normal(ks[0], (B, S, D_MODEL), jnp.float32), 'wq': jax.random.normal(ks[1], (N_HEADS * HEAD_DIM, D_MODEL), jnp.float32) * s, 'wk': jax.random.normal(ks[2], (N_KV_HEADS * HEAD_DIM, D_MODEL), jnp.float32) * s, 'wv': jax.random.normal(ks[3], (N_KV_HEADS * HEAD_DIM, D_MODEL), jnp.float32) * s, 'wo': jax.random.normal(ks[4], (D_MODEL, N_HEADS * HEAD_DIM), jnp.float32) * s, 'q_norm_w': jnp.ones((HEAD_DIM,), jnp.float32), 'k_norm_w': jnp.ones((HEAD_DIM,), jnp.float32)}
    _L0_attn_b_in = _L0_attn_b_setup()

    def _L0_ffn_setup():
        import jax, jax.numpy as jnp
        import numpy as np
        BLOCK_SIZE = 32
        HIDDEN_SIZE = 256
        MLP_DIM = 2048
        NVFP4_LUT = jnp.array([0.0, 0.5, 1.0, 1.5, 2.0, 3.0, 4.0, 6.0, 0.0, -0.5, -1.0, -1.5, -2.0, -3.0, -4.0, -6.0], dtype=jnp.float32)

        def dequant_nvfp4(W_packed, scales, block=BLOCK_SIZE):
            N = W_packed.shape[0]
            low = W_packed & 15
            high = W_packed >> 4 & 15
            idx = jnp.stack([low, high], axis=-1).reshape(N, -1)
            vals = NVFP4_LUT[idx]
            K = vals.shape[1]
            vals = vals.reshape(N, K // block, block) * scales[:, :, None]
            return vals.reshape(N, K)
        key = jax.random.key(seed)
        ks = jax.random.split(key, 7)
        x = jax.random.normal(ks[0], (4, 32, HIDDEN_SIZE), dtype=jnp.float32)
        gate_W_packed = jax.random.randint(ks[1], (MLP_DIM, HIDDEN_SIZE // 2), 0, 32, dtype=jnp.int32)
        gate_scales = jax.random.uniform(ks[2], (MLP_DIM, HIDDEN_SIZE // BLOCK_SIZE), dtype=jnp.float32) * 0.1 + 0.001
        up_W_packed = jax.random.randint(ks[3], (MLP_DIM, HIDDEN_SIZE // 2), 0, 32, dtype=jnp.int32)
        up_scales = jax.random.uniform(ks[4], (MLP_DIM, HIDDEN_SIZE // BLOCK_SIZE), dtype=jnp.float32) * 0.1 + 0.001
        down_W_packed = jax.random.randint(ks[5], (HIDDEN_SIZE, MLP_DIM // 2), 0, 32, dtype=jnp.int32)
        down_scales = jax.random.uniform(ks[6], (HIDDEN_SIZE, MLP_DIM // BLOCK_SIZE), dtype=jnp.float32) * 0.1 + 0.001
        return {'x': x, 'gate_W_packed': gate_W_packed, 'gate_scales': gate_scales, 'up_W_packed': up_W_packed, 'up_scales': up_scales, 'down_W_packed': down_W_packed, 'down_scales': down_scales}
    _L0_ffn_in = _L0_ffn_setup()
    _d = {'L0_attn_a_x': _L0_attn_a_in['x'], 'L0_attn_a_Wq': _L0_attn_a_in['Wq'], 'L0_attn_a_Wk': _L0_attn_a_in['Wk'], 'L0_attn_a_Wv': _L0_attn_a_in['Wv'], 'L0_attn_a_Wo': _L0_attn_a_in['Wo'], 'L0_attn_a_bo': _L0_attn_a_in['bo'], 'L0_attn_b_wq': _L0_attn_b_in['wq'], 'L0_attn_b_wk': _L0_attn_b_in['wk'], 'L0_attn_b_wv': _L0_attn_b_in['wv'], 'L0_attn_b_wo': _L0_attn_b_in['wo'], 'L0_attn_b_q_norm_w': _L0_attn_b_in['q_norm_w'], 'L0_attn_b_k_norm_w': _L0_attn_b_in['k_norm_w'], 'L0_ffn_gate_W_packed': _L0_ffn_in['gate_W_packed'], 'L0_ffn_gate_scales': _L0_ffn_in['gate_scales'], 'L0_ffn_up_W_packed': _L0_ffn_in['up_W_packed'], 'L0_ffn_up_scales': _L0_ffn_in['up_scales'], 'L0_ffn_down_W_packed': _L0_ffn_in['down_W_packed'], 'L0_ffn_down_scales': _L0_ffn_in['down_scales']}
    _x0 = _d['L0_attn_a_x']
    _d['L0_attn_a_x'] = jax.random.normal(jax.random.fold_in(jax.random.key(seed), 1), (2, 1024, 256), dtype=_x0.dtype)
    del _x0
    return _d

def reference(L0_attn_a_x, L0_attn_a_Wq, L0_attn_a_Wk, L0_attn_a_Wv, L0_attn_a_Wo, L0_attn_a_bo, L0_attn_b_wq, L0_attn_b_wk, L0_attn_b_wv, L0_attn_b_wo, L0_attn_b_q_norm_w, L0_attn_b_k_norm_w, L0_ffn_gate_W_packed, L0_ffn_gate_scales, L0_ffn_up_W_packed, L0_ffn_up_scales, L0_ffn_down_W_packed, L0_ffn_down_scales):

    def _L0_attn_a_ref(x, Wq, Wk, Wv, Wo, bo):
        import jax, jax.numpy as jnp
        import numpy as np
        EMB_DIM = 256
        NUM_HEADS = 16
        HEAD_DIM = EMB_DIM // NUM_HEADS
        B, T = (4, 256)
        Bsz, Tlen, C = x.shape
        H, D = (NUM_HEADS, HEAD_DIM)
        q = (x @ Wq).reshape(Bsz, Tlen, H, D)
        k = x @ Wk
        v = x @ Wv
        scores = jnp.einsum('bihd,bjd->bhij', q, k) / jnp.sqrt(jnp.float32(D))
        i = jnp.arange(Tlen)[:, None]
        j = jnp.arange(Tlen)[None, :]
        causal = j <= i
        scores = jnp.where(causal, scores, -jnp.inf)
        attn = jax.nn.softmax(scores, axis=-1)
        out = jnp.einsum('bhij,bjd->bihd', attn, v).reshape(Bsz, Tlen, C)
        return out @ Wo + bo

    def _L0_attn_b_ref(x, wq, wk, wv, wo, q_norm_w, k_norm_w):
        import jax, jax.numpy as jnp
        import numpy as np
        N_HEADS = 16
        N_KV_HEADS = 4
        HEAD_DIM = 128
        D_MODEL = 256
        WINDOW = 128
        THETA = 10000.0
        EPS = 1e-06

        def _rmsnorm(x, w):
            var = jnp.mean(x * x, axis=-1, keepdims=True)
            return x * jax.lax.rsqrt(var + EPS) * w

        def _rope(x, pos):
            d2 = HEAD_DIM // 2
            inv_freq = 1.0 / THETA ** (jnp.arange(0, HEAD_DIM, 2, dtype=jnp.float32) / HEAD_DIM)
            ang = pos[:, None].astype(jnp.float32) * inv_freq[None, :]
            cos = jnp.cos(ang)[None, None]
            sin = jnp.sin(ang)[None, None]
            x1, x2 = (x[..., :d2], x[..., d2:])
            return jnp.concatenate([x1 * cos - x2 * sin, x1 * sin + x2 * cos], axis=-1)
        B, S, _ = x.shape
        past_length = 0
        scale = HEAD_DIM ** (-0.5)
        n_rep = N_HEADS // N_KV_HEADS
        q = (x @ wq.T).reshape(B, S, N_HEADS, HEAD_DIM).transpose(0, 2, 1, 3)
        k = (x @ wk.T).reshape(B, S, N_KV_HEADS, HEAD_DIM).transpose(0, 2, 1, 3)
        v = (x @ wv.T).reshape(B, S, N_KV_HEADS, HEAD_DIM).transpose(0, 2, 1, 3)
        q = _rmsnorm(q, q_norm_w)
        k = _rmsnorm(k, k_norm_w)
        pos = jnp.arange(S) + past_length
        q = _rope(q, pos)
        k = _rope(k, pos)
        k_rep = jnp.repeat(k, n_rep, axis=1)
        v_rep = jnp.repeat(v, n_rep, axis=1)
        q_idx = jnp.arange(S)[:, None] + past_length
        k_idx = jnp.arange(S)[None, :]
        mask = (q_idx >= k_idx) & (q_idx - k_idx < WINDOW)
        scores = jnp.einsum('bhqd,bhkd->bhqk', q, k_rep) * scale
        scores = jnp.where(mask[None, None], scores, jnp.float32(-jnp.inf))
        attn = jax.nn.softmax(scores, axis=-1)
        out = jnp.einsum('bhqk,bhkd->bhqd', attn, v_rep)
        out = out.transpose(0, 2, 1, 3).reshape(B, S, N_HEADS * HEAD_DIM)
        return out @ wo.T

    def _L0_ffn_ref(x, gate_W_packed, gate_scales, up_W_packed, up_scales, down_W_packed, down_scales):
        import jax, jax.numpy as jnp
        import numpy as np
        BLOCK_SIZE = 32
        HIDDEN_SIZE = 256
        MLP_DIM = 2048
        NVFP4_LUT = jnp.array([0.0, 0.5, 1.0, 1.5, 2.0, 3.0, 4.0, 6.0, 0.0, -0.5, -1.0, -1.5, -2.0, -3.0, -4.0, -6.0], dtype=jnp.float32)

        def dequant_nvfp4(W_packed, scales, block=BLOCK_SIZE):
            N = W_packed.shape[0]
            low = W_packed & 15
            high = W_packed >> 4 & 15
            idx = jnp.stack([low, high], axis=-1).reshape(N, -1)
            vals = NVFP4_LUT[idx]
            K = vals.shape[1]
            vals = vals.reshape(N, K // block, block) * scales[:, :, None]
            return vals.reshape(N, K)
        B, S, H = x.shape
        xt = x.reshape(B * S, H)
        Wg = dequant_nvfp4(gate_W_packed, gate_scales)
        Wu = dequant_nvfp4(up_W_packed, up_scales)
        Wd = dequant_nvfp4(down_W_packed, down_scales)
        gate = jnp.einsum('th,nh->tn', xt, Wg)
        up = jnp.einsum('th,nh->tn', xt, Wu)
        gelu = jnp.tanh(0.7978845608028654 * (gate + 0.044715 * gate ** 3)) * gate * 0.5 + gate * 0.5
        inter = gelu * up
        out = jnp.einsum('tn,hn->th', inter, Wd)
        return out.reshape(B, S, H)
    x = L0_attn_a_x
    x = x + _L0_attn_a_ref(_layernorm(x, axis=-1), L0_attn_a_Wq, L0_attn_a_Wk, L0_attn_a_Wv, L0_attn_a_Wo, L0_attn_a_bo)
    x = x + _L0_ffn_ref(_layernorm(x, axis=-1), L0_ffn_gate_W_packed, L0_ffn_gate_scales, L0_ffn_up_W_packed, L0_ffn_up_scales, L0_ffn_down_W_packed, L0_ffn_down_scales)
    x = x + _L0_attn_b_ref(_layernorm(x, axis=-1), L0_attn_b_wq, L0_attn_b_wk, L0_attn_b_wv, L0_attn_b_wo, L0_attn_b_q_norm_w, L0_attn_b_k_norm_w)
    x = x + _L0_ffn_ref(_layernorm(x, axis=-1), L0_ffn_gate_W_packed, L0_ffn_gate_scales, L0_ffn_up_W_packed, L0_ffn_up_scales, L0_ffn_down_W_packed, L0_ffn_down_scales)
    return x

_drawn_inputs = setup_inputs


def setup_inputs(seed=0):
    import zlib

    import numpy as np

    out = dict(_drawn_inputs(seed))
    spreads = {'L0_attn_b_q_norm_w': (1.0, 0.6), 'L0_attn_b_k_norm_w': (1.0, 0.6)}
    factors = {'L0_attn_a_bo': 3.202,
     'L0_attn_b_wq': 8.0,
     'L0_attn_b_wk': 8.0,
     'L0_attn_b_wv': 8.0,
     'L0_attn_b_wo': 8.0}
    for name, (base, spread) in spreads.items():
        noise = np.random.default_rng([zlib.crc32(name.encode()), seed]).standard_normal(out[name].shape)
        drawn = base * np.exp(spread * noise) if base else spread * noise
        out[name] = jnp.asarray(drawn.astype(out[name].dtype))
    for name, factor in factors.items():
        out[name] = (out[name] * factor).astype(out[name].dtype)
    return out
```

```python
import concourse.bass as bass
from concourse import mybir
from concourse.alu_op_type import AluOpType as ALU
from contextlib import ExitStack

F32 = mybir.dt.float32
F32R = mybir.dt.float32r
BF16 = mybir.dt.bfloat16
I32 = mybir.dt.int32
ACT = mybir.ActivationFunctionType
AX = mybir.AxisListType

P = 128
E = 256
B, T = 2, 1024
TILES = B * T // P
TB = T // P
CT = 4
CHUNKS = TILES // CT
C = CT * P
HA, DA = 16, 16
QKV = E + 2 * DA
QUADS = HA // 4
HB, KVB, DB = 16, 4, 128
MLP = 2048
NT = MLP // P
BIG = -1.0e30
LN_EPS, RMS_EPS = 1e-5, 1e-6
RSQRT_SEED = float(0x5F3759DF)
POOL_CONST = 19
MAXES = [(i, h, 2) for i in range(CT) for h in (0, 2)] + [(i, h, 1) for i in range(CT, TB) for h in range(4)]
STEPS = CT + TB
EXPS = 2 * STEPS
RSQRT_LINKS = 2 + 3 * 3


class Chain:

    def __init__(self, eng, sem):
        self.eng, self.sem, self.base, self.k = eng, sem, 0, 0

    def at(self, base):
        self.base, self.k = base, 0

    def link(self, ins):
        self.k += 1
        ins.then_inc(self.sem, 1)
        self.eng.wait_ge(self.sem, self.base + self.k)


def build(nc, x, Wq, Wk, Wv, Wo, bo, wq, wk, wv, wo, qw, kw, gW, gS, uW, uS, dW, dS, cos, sin, out, stop=9, dbg=None):
    ctx = ExitStack()
    with ctx:
        def sb(name, shape, dt, stack=ctx):
            return stack.enter_context(nc.sbuf_tensor(name, shape, dt))

        sems = {}

        def sem(name):
            if name not in sems:
                sems[name] = ctx.enter_context(nc.semaphore(name))
            return sems[name]

        X = sb("X", [P, TILES, E], F32)
        wgh = sb("wgh", [P, 2, MLP], F32R)
        wgl = sb("wgl", [P, 2, MLP], F32R)
        wuh = sb("wuh", [P, 2, MLP], F32R)
        wul = sb("wul", [P, 2, MLP], F32R)
        ident = sb("ident", [P, P], F32)
        identb = sb("identb", [P, P], BF16)
        causal = sb("causal", [P, P], BF16)
        causalT = sb("causalT", [P, P], BF16)
        window = sb("window", [P, 3, E], BF16)
        stats = sb("stats", [P, CT, 6], F32)
        mv = sb("mv", [P, CT, 2], F32)
        var = sb("var", [P, CT], F32)
        rstd = sb("rstd", [P, CT], F32)
        rtmp = sb("rtmp", [P, CT], F32)
        xn = sb("xn", [P, CT, E], F32)
        s = ExitStack()
        wdh = sb("wdh", [P, NT, E], F32R, s)
        wdl = sb("wdl", [P, NT, E], F32R, s)
        mid = ExitStack()
        raw = [sb(f"raw{i}", [P, MLP], I32, mid) for i in range(3)]
        scl = [sb(f"scl{i}", [P, P], F32, mid) for i in range(3)]
        mag = sb("mag", [P, MLP], I32, mid)
        sgn = sb("sgn", [P, MLP], F32, mid)
        val = sb("val", [P, MLP], F32, mid)
        deq = [sb(f"deq{i}", [P, MLP], F32, mid) for i in range(2)]
        mid.close()
        mid = ExitStack()
        wqr = sb("wqr", [P, HB, E], F32, mid)
        wkvr = sb("wkvr", [P, 2, KVB, E], F32, mid)
        wor = sb("wor", [P, 2, HB, P], F32, mid)
        wTs = sb("wTs", [P, 10240], F32, mid)
        mid.close()
        mid = ExitStack()
        wah = sb("wah", [P, 2, QKV], F32R, mid)
        wal = sb("wal", [P, 2, QKV], F32R, mid)
        woah = sb("woah", [P, 2, E], F32R, mid)
        woal = sb("woal", [P, 2, E], F32R, mid)
        bob = sb("bob", [P, E], F32, mid)
        qkv = sb("qkv", [P, TB, QKV], F32, mid)
        qpad = sb("qpad", [P, TB, 4, P], F32, mid)
        qTa = sb("qTa", [P, 4, T], F32R, mid)
        kTa = sb("kTa", [P, T], F32R, mid)
        kpad = sb("kpad", [P, TB, P], F32, mid)
        vpad = sb("vpad", [P, TB, 32], F32, mid)
        nmax = sb("nmax", [P, TB, 4], F32, mid)
        OT = sb("OT", [P, C], F32, mid)
        rec = sb("rec", [P, CT, 4], F32, mid)
        att = sb("att", [P, TB, E], F32, mid)
        both = ExitStack()
        prob = sb("prob", [P, 2, 4, C], F32, both)
        both.close()
        xTh1 = sb("xTh1", [P, 2, C], F32R, mid)
        xTl1 = sb("xTl1", [P, 2, C], F32R, mid)
        sa = sb("sa", [P, 2, QKV], F32, mid)
        so = sb("so", [P, 2, E], F32, mid)
        mid.close()
        s2 = ExitStack()
        wTb = sb("wTb", [P, 10240], F32, s2)
        mid = ExitStack()
        xTh2 = sb("xTh2", [P, 2, C], F32R, mid)
        xTl2 = sb("xTl2", [P, 2, C], F32R, mid)
        gel = sb("gel", [P, 2, C], F32, mid)
        prod = sb("prod", [P, 2, C], F32, mid)
        inh = sb("inh", [P, 2, C], F32R, mid)
        inl = sb("inl", [P, 2, C], F32R, mid)
        yT = sb("yT", [P, 2, C], F32, mid)
        mid.close()
        mid = ExitStack()
        xTf = sb("xTf", [P, 2, C], F32, mid)
        qk = sb("qk", [P, 20, DB], F32, mid)
        rot = sb("rot", [P, 20, DB], F32, mid)
        qTb = sb("qTb", [P, HB, P], F32, mid)
        kTb = sb("kTb", [P, 2, KVB, P], F32, mid)
        prb = sb("prb", [P, 2, 4, E], F32, mid)
        sqb = sb("sqb", [P, 2, C], F32, mid)
        ssb = sb("ssb", [P, 20], F32, mid)
        rqk = sb("rqk", [P, 20], F32, mid)
        rqt = sb("rqt", [P, 20], F32, mid)
        nmb = sb("nmb", [P, 2, 4], F32, mid)
        rsb = sb("rsb", [P, 2, 4], F32, mid)
        rcb = sb("rcb", [P, 2, 4], F32, mid)
        mid.close()
        s2.close()
        s.close()
        mid = ExitStack()
        tabs = sb("tabs", [P, 4, TB, DB], F32, mid)
        PT = sb("PT", [P, 2, C], F32, mid)
        vb = sb("vb", [P, 2, C], F32, mid)
        oT = sb("oT", [P, HB, P], F32, mid)
        mid.close()

        wqT = wTb[:, 0:4096].rearrange("p (r n) -> p r n", r=2)
        wkvT = wTb[:, 4096:6144].rearrange("p (r n) -> p r n", r=2)
        woT = wTb[:, 6144:10240].rearrange("p (h n) -> p h n", h=HB)

        ps = ctx.enter_context(nc.psum_tensor("ps", [P, 8, 512], F32))
        TP = [ps[:, 0, :], ps[:, 1, :]]

        wb_keep = nc.dram_tensor("wb_keep", (P, 10240), F32, kind="Internal").ap()
        wd_keep = nc.dram_tensor("wd_keep", (P, 2 * NT * E), F32, kind="Internal").ap()

        w_mats = [(wgh, wgl), (wuh, wul), (wdh, wdl)]

        def wb_slot(n):
            return wTs[:, n * 512:(n + 1) * 512]

        def w_slot(i, part, nib, k):
            m = w_mats[i][part]
            return m[:, nib, k * 512:(k + 1) * 512] if i < 2 else m[:, 4 * k + nib:4 * k + nib + 3:2, :]

        def w_psum(i, n):
            return TP[n % 2] if i < 2 else TP[n % 2].rearrange("p (a e) -> p a e", a=2)

        block = ctx.enter_context(nc.Block())

        @block.sync
        def _(sp):
            sp.dma_start(wqr[:, :, :], wq.rearrange("(h p) k -> p h k", p=P)).then_inc(sem("wq_in"), 16)
            sp.dma_start(wkvr[:, 0, :, :], wk.rearrange("(h p) k -> p h k", p=P)).then_inc(sem("wkv_in"), 16)
            sp.dma_start(wkvr[:, 1, :, :], wv.rearrange("(h p) k -> p h k", p=P)).then_inc(sem("wkv_in"), 16)
            sp.dma_start(wor[:, :, :, :], wo.rearrange("(u p) (h d) -> p u h d", p=P, d=P)).then_inc(sem("wo_in"), 16)
            sp.dma_start(X[:, :, :], x.rearrange("b (t p) e -> p (b t) e", p=P)).then_inc(sem("x_in"), 16)
            sp.wait_ge(sem("wb_ready"), 20)
            sp.dma_start(wb_keep, wTs[:, :]).then_inc(sem("wb_kept"), 16)
            sp.wait_ge(sem("wb_kept"), 16)
            for i, (w, sc) in enumerate([(gW, gS), (uW, uS)]):
                sp.dma_start(raw[i][:, :].rearrange("p (t c) -> p t c", c=E),
                             w.rearrange("(t p r) c -> p t (r c)", p=P, r=2)).then_inc(sem(f"raw{i}_in"), 16)
                sp.dma_start(scl[i][:, :].rearrange("p (t c) -> p t c", c=16),
                             sc.rearrange("(t p r) c -> p t (r c)", p=P, r=2)).then_inc(sem(f"raw{i}_in"), 16)
            sp.dma_start(raw[2][:, :].rearrange("p (u c) -> p u c", u=2),
                         dW.rearrange("(u p) c -> p u c", u=2)).then_inc(sem("raw2_in"), 16)
            sp.dma_start(scl[2][:, :].rearrange("p (u c) -> p u c", u=2),
                         dS.rearrange("(u p) c -> p u c", u=2)).then_inc(sem("raw2_in"), 16)
            sp.wait_ge(sem("lo_ready"), 24)
            sp.dma_start(wd_keep[:, 0:NT * E], wdh[:, :, :].rearrange("p a b -> p (a b)").bitcast(F32)).then_inc(sem("wd_kept"), 16)
            sp.dma_start(wd_keep[:, NT * E:], wdl[:, :, :].rearrange("p a b -> p (a b)").bitcast(F32)).then_inc(sem("wd_kept"), 16)
            sp.dma_start(sa[:, :, 0:E], Wq.rearrange("(p r) n -> p r n", r=2)).then_inc(sem("wa_in"), 16)
            sp.dma_start(sa[:, :, E:E + DA], Wk.rearrange("(p r) n -> p r n", r=2)).then_inc(sem("wa_in"), 16)
            sp.dma_start(sa[:, :, E + DA:], Wv.rearrange("(p r) n -> p r n", r=2)).then_inc(sem("wa_in"), 16)
            sp.dma_start(so[:, :, :], Wo.rearrange("(p r) n -> p r n", r=2)).then_inc(sem("wa_in"), 16)
            sp.dma_start(bob[:, :], bo.rearrange("(a n) -> a n", a=1).broadcast_to([P, E])).then_inc(sem("wa_in"), 16)
            if stop >= 3:
                sp.wait_ge(sem("x_updated"), 16)
                sp.dma_start(wTb[:, :], wb_keep).then_inc(sem("wb_back"), 16)
                sp.wait_ge(sem("x_updated"), 16 + 2 * CHUNKS)
                for n in range(2):
                    sp.dma_start(tabs[:, n, :, 0:64], cos.rearrange("(t p) d -> p t d", p=P)).then_inc(sem("tab_in"), 16)
                    sp.dma_start(tabs[:, n, :, 64:128], sin.rearrange("(t p) d -> p t d", p=P)).then_inc(sem("tab_in"), 16)
                sp.dma_start(vb[:, 0, 0:DB], qw.rearrange("(a n) -> a n", a=1).broadcast_to([P, DB])).then_inc(sem("tab_in"), 16)
                sp.dma_start(vb[:, 0, DB:2 * DB], kw.rearrange("(a n) -> a n", a=1).broadcast_to([P, DB])).then_inc(sem("tab_in"), 16)
            if stop >= 4:
                sp.wait_ge(sem("x_updated"), 16 + 2 * CHUNKS + TILES)
                sp.wait_ge(sem("wd_kept"), 32)
                sp.dma_start(wdh[:, :, :].rearrange("p a b -> p (a b)").bitcast(F32), wd_keep[:, 0:NT * E]).then_inc(sem("wd_back"), 16)
                sp.dma_start(wdl[:, :, :].rearrange("p a b -> p (a b)").bitcast(F32), wd_keep[:, NT * E:]).then_inc(sem("wd_back"), 16)
            done = {0: 0, 1: 16, 2: 16 + 2 * CHUNKS, 3: 16 + 2 * CHUNKS + TILES}.get(stop)
            for c in range(CHUNKS):
                sp.wait_ge(sem("x_updated"), done if done is not None else 16 + 2 * CHUNKS + TILES + 2 * (c + 1))
                if stop == 0:
                    sp.wait_ge(sem("x_in"), 16)
                b, a = divmod(c, CHUNKS // B)
                sp.dma_start(out[b, a * C:(a + 1) * C, :].rearrange("(t p) e -> p t e", p=P),
                             X[:, c * CT:(c + 1) * CT, :]).then_inc(sem("out_written"), 16)
            sp.wait_ge(sem("out_written"), 16 * CHUNKS)

        @block.gpsimd
        def _(pool):
            def diagonal(m):
                pool.memset(m, 0.0).then_inc(sem("pool"), 1)
                pool.wait_ge(sem("pool"), diagonal.n + 1)
                pool.affine_select(out=m, in_=m, compare_op=ALU.not_equal, fill=1.0, base=0,
                                   pattern=[[-1, P]], channel_multiplier=1).then_inc(sem("pool"), 1)
                diagonal.n += 2
            diagonal.n = 0
            diagonal(ident[:, :])
            diagonal(identb[:, :])

            def mask(m, keep_where, base, step, per_partition):
                pool.memset(m, 0.0).then_inc(sem("pool"), 1)
                pool.wait_ge(sem("pool"), diagonal.n + 1)
                pool.affine_select(out=m, in_=m, compare_op=keep_where, fill=BIG, base=base,
                                   pattern=[[step, P]], channel_multiplier=per_partition).then_inc(sem("pool"), 1)
                diagonal.n += 2
            mask(causal[:, :], ALU.is_ge, 0, -1, 1)
            mask(causalT[:, :], ALU.is_ge, 0, 1, -1)
            mask(window[:, 0, 0:P], ALU.is_ge, 0, -1, 1)
            mask(window[:, 0, P:E], ALU.is_gt, 0, 1, -1)
            mask(window[:, 1, 0:P], ALU.is_ge, 0, -1, 1)
            pool.memset(window[:, 1, P:E], BIG).then_inc(sem("pool"), 1)
            diagonal.n += 1
            mask(window[:, 2, 0:P], ALU.is_gt, 0, 1, -1)
            mask(window[:, 2, P:E], ALU.is_ge, 0, -1, 1)
            assert diagonal.n == POOL_CONST
            if stop >= 1:
                pool.wait_ge(sem("wa_in"), 80)
                for b in range(B):
                    pool.wait_ge(sem("ln_ready"), 2 * (b + 1))
                    v = X[:, b * TB:(b + 1) * TB, :]
                    pool.tensor_tensor(v, v, bob[:, :].rearrange("p (a e) -> p a e", a=1).broadcast_to([P, TB, E]),
                                       ALU.add).then_inc(sem("bias_added"), 1)
            if stop >= 3:
                with pool.Fori(0, TILES) as t:
                    pool.wait_ge(sem("rope_parts"), t + 1)
                    pool.tensor_tensor(qk[:, :, :], qk[:, :, :], rot[:, :, :], ALU.add).then_inc(sem("rope_sum"), 1)

        @block.scalar
        def _(act):
            def copy(o, i, s):
                act.activation(o, i, ACT.Copy).then_inc(sem(s), 1)

            for n in range(20):
                act.wait_ge(sem("wb_tp"), n + 1)
                copy(wb_slot(n), TP[n % 2], "wb_ready")
            for i in range(3):
                for nib in range(2):
                    for k in range(4):
                        n = (i * 2 + nib) * 4 + k
                        act.wait_ge(sem("w_tp"), n + 1)
                        copy(w_slot(i, 0, nib, k), w_psum(i, n), "hi_ready")

            def split_x(n, hi):
                for r in range(2):
                    act.wait_ge(sem("xn_tp"), 2 * n + r + 1)
                    copy(hi[:, r, :], TP[r], "xT_hi")

            if stop >= 1:
                act.wait_ge(sem("wa_in"), 80)
                copy(wah[:, :, :], sa[:, :, :], "wa_hi")
                copy(woah[:, :, :], so[:, :, :], "wa_hi")
                with act.Fori(0, B) as b:
                    for a in range(2):
                        act_c = b * 2 + a
                        split_x(act_c, xTh1)
                        for t in range(CT):
                            act.wait_ge(sem("qkv_mm"), act_c * CT + t + 1)
                            copy(qkv[:, a * CT + t, :], ps[:, 6 + t % 2, 0:QKV], "qkv_ready")
                    for h in range(2):
                        act.wait_ge(sem("k_tp"), b * 2 + h + 1)
                        copy(kTa[:, h * C:(h + 1) * C], TP[h], "k_ready")
                    with act.Fori(0, QUADS) as qd:
                        u = b * QUADS + qd
                        for i in range(TB):
                            act.wait_ge(sem("q_tp"), u * 2 * TB + i + 1)
                            copy(qTa[:, :, i * P:(i + 1) * P], TP[i % 2].rearrange("p (h q) -> p h q", h=4), "q_ready")
                        for i in range(TB):
                            act.wait_ge(sem("q_tp"), u * 2 * TB + TB + i + 1)
                            copy(qTa[0:32, :, i * P:(i + 1) * P],
                                 TP[i % 2][0:32, :].rearrange("p (h q) -> p h q", h=4), "q_ready")
                        n = 0
                        for cc in range(2):
                            for j in range(CT * (cc + 1)):
                                step = 4 * cc + j
                                w = C - P * max(0, j - CT * cc)
                                for v in range(2):
                                    act.wait_ge(sem("sT_mm"), u * EXPS + n + 1)
                                    if v == 0 and step >= 2:
                                        act.wait_ge(sem("pv"), u * STEPS + step - 1)
                                    act.activation(prob[:, step % 2, 2 * v:2 * v + 2, 0:w],
                                                   ps[:, 2 + 2 * (n % 2):4 + 2 * (n % 2), 0:w], ACT.Exp)\
                                       .then_inc(sem("exp"), 1)
                                    n += 1
                            act.wait_ge(sem("pv"), u * STEPS + (CT if cc == 0 else STEPS))
                            act.wait_ge(sem("o_tp"), u * 2 + cc)
                            copy(OT[:, :], ps[:, 6 + cc, :], "o_ready")
                    for a in range(2):
                        for r in range(2):
                            act.wait_ge(sem("att_tp"), b * 4 + a * 2 + r + 1)
                            copy(xTh1[:, r, :], TP[r], "att_hi")

            def ffn(base, f):
                with act.Fori(0, CHUNKS) as c:
                    split_x(c + base, xTh2)
                    g = (c + f * CHUNKS) * NT
                    for t in range(NT + 1):
                        if t < NT:
                            act.wait_ge(sem("gate_mm"), g + t + 1)
                            if t >= 2:
                                act.wait_ge(sem("prod"), g + t - 1)
                            act.activation(gel[:, t % 2, :], ps[:, 2 + t % 2, :], ACT.Gelu_apprx_tanh)\
                               .then_inc(sem("gelu"), 1)
                        if t >= 1:
                            act.wait_ge(sem("prod"), g + t)
                            if t >= 3:
                                act.wait_ge(sem("down_mm"), g + t - 2)
                            copy(inh[:, (t - 1) % 2, :], prod[:, (t - 1) % 2, :], "in_hi")
                    act.wait_ge(sem("down_mm"), g + NT)
                    act.wait_ge(sem("y_tp"), (c + f * CHUNKS) * 2)
                    copy(yT[:, :, :], ps[:, 6:8, :], "y_ready")

            if stop >= 2:
                ffn(CHUNKS, 0)
            if stop >= 3:
                with act.Fori(0, CHUNKS) as c:
                    for r in range(2):
                        act.wait_ge(sem("xn_tp"), (c + 2 * CHUNKS) * 2 + r + 1)
                        copy(xTf[:, r, :], TP[r], "xT_hi")
                    for u in range(CT):
                        t = c * CT + u
                        for n in range(6):
                            act.wait_ge(sem("proj_mm"), t * 6 + n + 1)
                            src = ps[:, 2 + n % 2, :]
                            if n == 1:
                                copy(vb[:, u % 2, :], src, "proj_out")
                                continue
                            if n == 0:
                                act.wait_ge(sem("qk_tp"), t * 5)
                            m, k = (4, 0) if n == 0 else (n - 2, n - 1)
                            act.activation(qk[:, 4 * m:4 * m + 4, :], src.rearrange("p (h d) -> p h d", h=4), ACT.Copy)
                            if k >= 2:
                                act.wait_ge(sem("ss"), t * 5 + k - 1)
                            else:
                                act.wait_ge(sem("ss"), t * 5)
                            act.activation(sqb[:, k % 2, :], src, ACT.Square).then_inc(sem("proj_out"), 1)
                        for n in range(5):
                            act.wait_ge(sem("qk_tp"), t * 5 + n + 1)
                            dst = kTb[:, u % 2, :, :] if n == 0 else qTb[:, 4 * (n - 1):4 * n, :]
                            copy(dst, TP[n % 2].rearrange("p (h q) -> p h q", h=4), "qkT")
                        for g in range(5):
                            if g < 4:
                                act.wait_ge(sem("nmb"), t * 4 + g + 1)
                                if g >= 2:
                                    act.wait_ge(sem("p_tp"), 2 * (t * 4 + g - 1))
                                else:
                                    act.wait_ge(sem("p_tp"), 2 * (t * 4))
                                for h in range(4):
                                    act.activation(prb[:, g % 2, h, :], ps[:, 4 + h // 2, (h % 2) * E:(h % 2 + 1) * E],
                                                   ACT.Exp, bias=nmb[:, g % 2, h:h + 1],
                                                   accum_out=rsb[:, g % 2, h:h + 1]).then_inc(sem("expb"), 1)
                            if g >= 1:
                                act.wait_ge(sem("p_tp"), 2 * (t * 4 + g - 1) + 1)
                                act.wait_ge(sem("pvb"), t * 4 + g - 1)
                                copy(PT[:, 0, :], TP[0], "PT0")
                                act.wait_ge(sem("pvb"), t * 4 + g)
                                if g == 1:
                                    act.wait_ge(sem("wo_mm"), t)
                                copy(oT[:, 4 * g - 4:4 * g, :], ps[:, 6, :].rearrange("p (h q) -> p h q", h=4), "oT")
            if stop >= 4:
                ffn(3 * CHUNKS, 1)

        @block.vector
        def _(dve):
            ch = Chain(dve, sem("dve"))

            def rsqrt(y, v, t):
                ch.link(dve.tensor_scalar(t.bitcast(I32), v.bitcast(I32), 1, None, ALU.logical_shift_right))
                ch.link(dve.tensor_scalar(y.bitcast(I32), t.bitcast(I32), -1.0, RSQRT_SEED, ALU.mult, ALU.add))
                for _ in range(3):
                    ch.link(dve.tensor_tensor(t, y, y, ALU.mult))
                    ch.link(dve.scalar_tensor_tensor(out=t, in0=t, scalar=-0.5, in1=v, op0=ALU.mult, op1=ALU.mult))
                    ch.link(dve.scalar_tensor_tensor(out=y, in0=t, scalar=1.5, in1=y, op0=ALU.add, op1=ALU.mult))

            LN_LINKS = 3 + RSQRT_LINKS

            def layernorm(n, c):
                for t in range(CT):
                    last = dve.bn_stats(stats[:, t, :], X[:, c * CT + t, :])
                ch.link(last)
                dve.memset(rtmp[:, :], 0.0)
                for t in range(CT):
                    last = dve.bn_aggr(mv[:, t, :], stats[:, t, :])
                ch.link(last)
                ch.link(dve.tensor_scalar(var[:, :], mv[:, :, 1], LN_EPS, None, ALU.add))
                rsqrt(rstd[:, :], var[:, :], rtmp[:, :])
                dve.wait_ge(sem("xn_tp"), 2 * n)
                for t in range(CT):
                    last = dve.tensor_scalar(xn[:, t, :], X[:, c * CT + t, :], mv[:, t, 0:1], rstd[:, t:t + 1],
                                             ALU.subtract, ALU.mult)
                last.then_inc(sem("ln_ready"), 1)

            def split_x(n, hi, lo):
                for r in range(2):
                    dve.wait_ge(sem("xT_hi"), 2 * n + r + 1)
                    dve.tensor_tensor(lo[:, r, :], TP[r], hi[:, r, :].bitcast(F32), ALU.subtract).then_inc(sem("xT_lo"), 1)

            for i in range(3):
                dve.wait_ge(sem(f"raw{i}_in"), 32)
                for nib in range(2):
                    for dst, bits in ((mag, 7), (sgn, 8)):
                        o = dst[:, :].bitcast(I32)
                        if nib:
                            last = dve.tensor_scalar(o, raw[i][:, :], 4, bits, ALU.logical_shift_right, ALU.bitwise_and)
                        else:
                            last = dve.tensor_scalar(o, raw[i][:, :], bits, None, ALU.bitwise_and)
                    ch.link(last)
                    ch.link(dve.tensor_scalar(val[:, :], mag[:, :], 2.0, -8.0, ALU.mult, ALU.add))
                    ch.link(dve.scalar_tensor_tensor(out=val[:, :], in0=mag[:, :], scalar=-2.0, in1=val[:, :], op0=ALU.add, op1=ALU.max))
                    ch.link(dve.scalar_tensor_tensor(out=val[:, :], in0=mag[:, :], scalar=0.5, in1=val[:, :], op0=ALU.mult, op1=ALU.max))
                    ch.link(dve.scalar_tensor_tensor(
                        out=sgn[:, :].rearrange("p (s k) -> p s k", k=16), in0=sgn[:, :].bitcast(I32).rearrange("p (s k) -> p s k", k=16),
                        scalar=-4.0, in1=scl[i][:, :].rearrange("p (s k) -> p s k", k=1).broadcast_to([P, P, 16]),
                        op0=ALU.add, op1=ALU.mult))
                    if i:
                        dve.wait_ge(sem("w_tp"), (i * 2 + nib - 2 + 1) * 4)
                    dve.scalar_tensor_tensor(out=deq[nib][:, :], in0=val[:, :], scalar=-0.25, in1=sgn[:, :],
                                             op0=ALU.mult, op1=ALU.mult).then_inc(sem("deq"), 1)
                    if True:
                        for k in range(4):
                            n = (i * 2 + nib) * 4 + k
                            dve.wait_ge(sem("hi_ready"), n + 1)
                            dve.tensor_tensor(w_slot(i, 1, nib, k), w_psum(i, n),
                                              w_slot(i, 0, nib, k).bitcast(F32), ALU.subtract).then_inc(sem("lo_ready"), 1)
            base = ch.k
            assert base == 30

            if stop >= 1:
                dve.wait_ge(sem("x_in"), 16)
                for w, (o, h, i) in enumerate([(wal, wah, sa), (woal, woah, so)]):
                    dve.wait_ge(sem("wa_hi"), w + 1)
                    dve.tensor_tensor(o[:, :, :], i[:, :, :], h[:, :, :].bitcast(F32), ALU.subtract).then_inc(sem("wa_lo"), 1)
                dve.memset(kpad[:, :, :], 0.0)
                dve.memset(qpad[:, :, :, :], 0.0)
                ch.link(dve.memset(vpad[:, :, :], 0.0))
                dve.memset(kpad[:, :, 16:18], 1.0)
                ch.link(dve.memset(vpad[:, :, 16:17], 1.0))
                base += 2
                PER_Q = 1 + 1 + 2
                PER_B = 2 * LN_LINKS + 1 + QUADS * PER_Q
                with dve.Fori(0, B) as b:
                    for a in range(2):
                        ch.at(base + b * PER_B + a * LN_LINKS)
                        layernorm(b * 2 + a, b * 2 + a)
                        assert ch.k == LN_LINKS
                        if a == 0:
                            dve.wait_ge(sem("qkv_mm"), b * 2 * CT)
                        split_x(b * 2 + a, xTh1, xTl1)
                    ch.at(base + b * PER_B + 2 * LN_LINKS)
                    dve.wait_ge(sem("qkv_ready"), b * TB + TB)
                    kk = qkv[:, :, E:E + DA]
                    for blk in (0, 64):
                        last = dve.tensor_scalar(kpad[:, :, blk:blk + DA].bitcast(F32R), kk, 0.25, None, ALU.mult)
                    ch.link(last)
                    for blk in (32, 96):
                        last = dve.scalar_tensor_tensor(out=kpad[:, :, blk:blk + DA].bitcast(F32R), in0=kk, scalar=0.25,
                                                        in1=kpad[:, :, 0:DA], op0=ALU.mult, op1=ALU.subtract)
                    dve.tensor_copy(vpad[:, :, 0:DA], qkv[:, :, E + DA:]).then_inc(sem("kv_pad"), 1)
                    with dve.Fori(0, QUADS) as qd:
                        u = b * QUADS + qd
                        ch.at(base + b * PER_B + 2 * LN_LINKS + 1 + qd * PER_Q)
                        dve.wait_ge(sem("q_tp"), u * 2 * TB)
                        dve.memset(qpad[:, :, :, 16:18], 0.0)
                        src = qkv[:, :, bass.ds(qd * 64, 64)].rearrange("p t (h d) -> p t h d", h=4)
                        for blk in (0, 32):
                            last = dve.tensor_copy(qpad[:, :, :, blk:blk + DA].bitcast(F32R), src)
                        ch.link(last)
                        for blk in (64, 96):
                            last = dve.tensor_tensor(qpad[:, :, :, blk:blk + DA].bitcast(F32R), src, qpad[:, :, :, 0:DA], ALU.subtract)
                        last.then_inc(sem("q_pad"), 1)
                        for n, (i, h0, nh) in enumerate(MAXES):
                            w = (i + 1) * P
                            dve.wait_ge(sem("s_mm"), u * len(MAXES) + n + 1)
                            bank = 2 + 2 * (n % 2)
                            if nh == 2:
                                ins = dve.tensor_reduce(nmax[:, i, h0:h0 + 2], ps[:, bank:bank + 2, 0:w], AX.X, ALU.max, negate=True)
                            else:
                                ins = dve.tensor_reduce(nmax[:, i, h0:h0 + 1], ps[:, bank:bank + 2, :].rearrange("p a b -> p (a b)")[:, 0:w],
                                                        AX.X, ALU.max, negate=True)
                            ins.then_inc(sem("maxed"), 1)
                        dve.wait_ge(sem("maxed"), (u + 1) * len(MAXES))
                        dve.wait_ge(sem("q_tp"), u * 2 * TB + TB)
                        ch.link(dve.tensor_copy(qpad[:, :, :, 16].bitcast(F32R), nmax[:, :, :]))
                        dve.tensor_tensor(qpad[:, :, :, 17].bitcast(F32R), nmax[:, :, :], qpad[:, :, :, 16], ALU.subtract)\
                           .then_inc(sem("m_pad"), 1)
                        for cc in range(2):
                            dve.wait_ge(sem("o_tp"), u * 2 + cc + 1)
                            dve.wait_ge(sem("att"), u * 2 + cc)
                            o = TP[cc].rearrange("p (t h d) -> p t h d", t=CT, h=4)
                            ch.link(dve.reciprocal(rec[:, :, :], o[:, :, :, 16]))
                            dve.tensor_tensor(
                                att[:, cc * CT:(cc + 1) * CT, bass.ds(qd * 64, 64)].rearrange("p t (h d) -> p t h d", h=4),
                                o[:, :, :, 0:DA], rec[:, :, :].rearrange("p t (h d) -> p t h d", d=1).broadcast_to([P, CT, 4, DA]),
                                ALU.mult).then_inc(sem("att"), 1)
                        assert ch.k == PER_Q, ch.k
                    for a in range(2):
                        for r in range(2):
                            dve.wait_ge(sem("att_hi"), b * 4 + a * 2 + r + 1)
                            dve.tensor_tensor(xTl1[:, r, :], TP[r], xTh1[:, r, :].bitcast(F32), ALU.subtract).then_inc(sem("att_lo"), 1)
                        if a == 0:
                            dve.wait_ge(sem("bias_added"), b + 1)
                        for t in range(CT):
                            xt = X[:, b * TB + a * CT + t, :]
                            dve.wait_ge(sem("oproj_mm"), b * TB + a * CT + t + 1)
                            dve.tensor_tensor(xt, xt, ps[:, 6 + t % 2, 0:E], ALU.add).then_inc(sem("x_updated"), 1)
                base += 2 * PER_B
                dve.wait_ge(sem("x_updated"), TILES)

            def ffn(base_chunks, f, chain, updated):
                with dve.Fori(0, CHUNKS) as c:
                    ch.at(chain + c * LN_LINKS)
                    layernorm(c + base_chunks, c)
                    split_x(c + base_chunks, xTh2, xTl2)
                    g = (c + f * CHUNKS) * NT
                    for t in range(NT + 1):
                        if t < NT:
                            dve.wait_ge(sem("gelu"), g + t + 1)
                            dve.wait_ge(sem("up_mm"), g + t + 1)
                            if t >= 2:
                                dve.wait_ge(sem("in_hi"), g + t - 1)
                            dve.tensor_tensor(prod[:, t % 2, :], gel[:, t % 2, :], ps[:, 4 + t % 2, :], ALU.mult)\
                               .then_inc(sem("prod"), 1)
                        if t >= 1:
                            dve.wait_ge(sem("in_hi"), g + t)
                            if t >= 3:
                                dve.wait_ge(sem("down_mm"), g + t - 2)
                            dve.tensor_tensor(inl[:, (t - 1) % 2, :], prod[:, (t - 1) % 2, :],
                                              inh[:, (t - 1) % 2, :].bitcast(F32), ALU.subtract).then_inc(sem("in_lo"), 1)
                    for k in range(2):
                        dve.wait_ge(sem("y_tp"), (c + f * CHUNKS) * 2 + k + 1)
                        xt = X[:, bass.ds(c * CT + 2 * k, 2), :]
                        dve.tensor_tensor(xt, xt, TP[k].rearrange("p (t e) -> p t e", t=2), ALU.add).then_inc(sem("x_updated"), 1)
                    dve.wait_ge(sem("x_updated"), updated + c * 2 + 2)

            if stop >= 2:
                ffn(CHUNKS, 0, base, TILES)
                base += CHUNKS * LN_LINKS

            if stop >= 3:
                dve.wait_ge(sem("tab_in"), 96)
                ch.at(base)
                cs = [tabs[:, n, :, 0:64] for n in range(2)]
                ws = [vb[:, 0, n * DB:(n + 1) * DB].rearrange("p (a d) -> p a d", a=1) for n in range(2)]
                for n in (1, 0):
                    w1, w2 = (ws[n][:, :, k * 64:(k + 1) * 64].broadcast_to([P, TB, 64]) for k in range(2))
                    co, si = tabs[:, 0, :, 0:64], tabs[:, 0, :, 64:128]
                    A, Bt = tabs[:, 2 * n, :, :], tabs[:, 2 * n + 1, :, :]
                    if n == 0:
                        co, si = tabs[:, 1, :, 0:64], tabs[:, 1, :, 64:128]
                    ch.link(dve.tensor_tensor(A[:, :, 0:64], co, w1, ALU.mult))
                    ch.link(dve.tensor_tensor(A[:, :, 64:128], co, w2, ALU.mult))
                    ch.link(dve.scalar_tensor_tensor(out=Bt[:, :, 0:64], in0=si, scalar=-1.0, in1=w2, op0=ALU.mult, op1=ALU.mult))
                    ch.link(dve.tensor_tensor(Bt[:, :, 64:128], si, w1, ALU.mult))
                dve.memset(kTb[:, 1, :, :], 0.0)
                ch.link(dve.memset(vb[:, 1, :], 0.0))
                dve.memset(rqt[:, :], 0.0).then_inc(sem("tables"), 1)
                base += 9
                PER_T = 1 + RSQRT_LINKS + 1 + 4 * 1
                PER_C = LN_LINKS + CT * PER_T
                with dve.Fori(0, B) as b:
                    with dve.Fori(0, 2) as a:
                        c = b * 2 + a
                        ch.at(base + c * PER_C)
                        layernorm(c + 2 * CHUNKS, c)
                        for u in range(CT):
                            t = c * CT + u
                            ch.at(base + c * PER_C + LN_LINKS + u * PER_T)
                            for k in range(5):
                                dve.wait_ge(sem("proj_out"), t * 6 + (1 if k == 0 else k + 2))
                                dve.tensor_reduce(ssb[:, 16:20] if k == 0 else ssb[:, 4 * k - 4:4 * k],
                                                  sqb[:, k % 2, :].rearrange("p (h d) -> p h d", h=4), AX.X, ALU.add)\
                                   .then_inc(sem("ss"), 1)
                            dve.wait_ge(sem("ss"), (t + 1) * 5)
                            ch.link(dve.tensor_scalar(ssb[:, :], ssb[:, :], 1.0 / DB, RMS_EPS, ALU.mult, ALU.add))
                            rsqrt(rqk[:, :], ssb[:, :], rqt[:, :])
                            ti = a * CT + u
                            for n, h0, h1 in ((0, 0, 16), (1, 16, 20)):
                                q = qk[:, h0:h1, :]
                                A, B1, B2 = (tabs[:, 2 * n + s, ti, lo:hi].rearrange("p (a d) -> p a d", a=1)
                                             .broadcast_to([P, h1 - h0, hi - lo]) for s, lo, hi in ((0, 0, 128), (1, 0, 64), (1, 64, 128)))
                                dve.tensor_tensor(rot[:, h0:h1, 0:64], q[:, :, 64:128], B1, ALU.mult)
                                last = dve.tensor_tensor(rot[:, h0:h1, 64:128], q[:, :, 0:64], B2, ALU.mult)
                                if n:
                                    ch.link(last)
                            for n, h0, h1 in ((0, 0, 16), (1, 16, 20)):
                                q = qk[:, h0:h1, :]
                                A = tabs[:, 2 * n, ti, :].rearrange("p (a d) -> p a d", a=1).broadcast_to([P, h1 - h0, DB])
                                last = dve.tensor_tensor(q, q, A, ALU.mult)
                            last.then_inc(sem("rope_parts"), 1)
                            dve.wait_ge(sem("rope_sum"), t + 1)
                            for h0, h1 in ((16, 20), (0, 16)):
                                q = qk[:, h0:h1, :]
                                r = rqk[:, h0:h1].rearrange("p (h d) -> p h d", d=1).broadcast_to([P, h1 - h0, DB])
                                if h0:
                                    dve.tensor_tensor(q, q, r, ALU.mult).then_inc(sem("qk_final"), 1)
                                else:
                                    dve.scalar_tensor_tensor(out=q, in0=q, scalar=float(DB) ** -0.5, in1=r, op0=ALU.mult, op1=ALU.mult)\
                                       .then_inc(sem("qk_final"), 1)
                            for g in range(5):
                                if g < 4:
                                    dve.wait_ge(sem("sb_mm"), t * 4 + g + 1)
                                    dve.tensor_reduce(nmb[:, g % 2, :], ps[:, 4:6, :].rearrange("p a (h k) -> p (a h) k", h=2),
                                                      AX.X, ALU.max, negate=True).then_inc(sem("nmb"), 1)
                                if g >= 1:
                                    dve.wait_ge(sem("p_tp"), 2 * (t * 4 + g - 1) + 2)
                                    dve.wait_ge(sem("pvb"), t * 4 + g - 1)
                                    dve.tensor_copy(PT[:, 1, :], TP[1]).then_inc(sem("PT1"), 1)
                                if g < 4:
                                    dve.wait_ge(sem("expb"), 4 * (t * 4 + g + 1))
                                    ch.link(dve.reciprocal(rcb[:, g % 2, :], rsb[:, g % 2, :]))
                                    dve.tensor_tensor(prb[:, g % 2, :, :], prb[:, g % 2, :, :],
                                                      rcb[:, g % 2, :].rearrange("p (h d) -> p h d", d=1).broadcast_to([P, 4, E]),
                                                      ALU.mult).then_inc(sem("p_final"), 1)
                            assert ch.k == PER_T, (ch.k, PER_T)
                            dve.wait_ge(sem("wo_mm"), t + 1)
                            xt = X[:, t, :]
                            dve.tensor_tensor(xt, xt, ps[:, 7, 0:E], ALU.add).then_inc(sem("x_updated"), 1)
                base += CHUNKS * PER_C
                dve.wait_ge(sem("x_updated"), TILES + 2 * CHUNKS + TILES)
            if stop >= 4:
                ffn(3 * CHUNKS, 1, base, TILES + 2 * CHUNKS + TILES)

        @block.tensor
        def _(pe):
            def tp(o, i, parts=P):
                return pe.transpose(o, i, ident[:, :])

            pe.wait_ge(sem("pool"), POOL_CONST)
            for n in range(20):
                if n == 0:
                    pe.wait_ge(sem("wq_in"), 16)
                if n == 8:
                    pe.wait_ge(sem("wkv_in"), 32)
                if n == 12:
                    pe.wait_ge(sem("wo_in"), 16)
                if n >= 2:
                    pe.wait_ge(sem("wb_ready"), n - 1)
                for k in range(4):
                    if n < 8:
                        r, h = n // 4, (n % 4) * 4 + k
                        src = wqr[:, h, r::2]
                    elif n < 12:
                        r, m = divmod(n - 8, 2)
                        src = wkvr[:, m, k, r::2]
                    else:
                        h, m = (n - 12) * 2 + k // 2, k % 2
                        src = wor[:, m, h, :]
                    last = tp(TP[n % 2][:, k * P:(k + 1) * P], src)
                last.then_inc(sem("wb_tp"), 1)
            for i in range(3):
                for nib in range(2):
                    pe.wait_ge(sem("deq"), i * 2 + nib + 1)
                    for k in range(4):
                        n = (i * 2 + nib) * 4 + k
                        if n >= 2:
                            pe.wait_ge(sem("lo_ready"), n - 1)
                        else:
                            pe.wait_ge(sem("wb_ready"), 20)
                        for m in range(4):
                            if i < 2:
                                src = deq[nib][:, (4 * k + m) * P:(4 * k + m + 1) * P]
                            else:
                                t2, hh = 2 * k + m // 2, m % 2
                                src = deq[nib][:, hh * 1024 + t2 * P:hh * 1024 + (t2 + 1) * P]
                            last = tp(TP[n % 2][:, m * P:(m + 1) * P], src)
                        last.then_inc(sem("w_tp"), 1)

            def transpose_x(n, ready, count):
                pe.wait_ge(sem("ln_ready"), n + 1)
                for r in range(2):
                    for t in range(CT):
                        last = tp(TP[r][:, t * P:(t + 1) * P], xn[:, t, r::2])
                    last.then_inc(sem("xn_tp"), 1)

            def split_mm(o, lh, ll, rh, rl, start, stop):
                pe.matmul(o, ll, rh, start=start, stop=False)
                pe.matmul(o, lh, rl, start=False, stop=False)
                return pe.matmul(o, lh, rh, start=False, stop=stop)

            if stop >= 1:
                pe.wait_ge(sem("wa_lo"), 2)
                with pe.Fori(0, B) as b:
                    for a in range(2):
                        cn = b * 2 + a
                        if a == 0:
                            pe.wait_ge(sem("lo_ready"), 24)
                            pe.wait_ge(sem("att_lo"), b * 4)
                        transpose_x(cn, None, None)
                        pe.wait_ge(sem("xT_lo"), 2 * cn + 2)
                        for t in range(CT):
                            if a == 0 and t < 2:
                                pe.wait_ge(sem("x_updated"), b * TB)
                            else:
                                pe.wait_ge(sem("qkv_ready"), cn * CT + t - 1)
                            tt = slice(t * P, (t + 1) * P)
                            for r in range(2):
                                last = split_mm(ps[:, 6 + t % 2, 0:QKV], xTh1[:, r, tt], xTl1[:, r, tt],
                                                wah[:, r, :], wal[:, r, :], r == 0, r == 1)
                            last.then_inc(sem("qkv_mm"), 1)
                    pe.wait_ge(sem("kv_pad"), b + 1)
                    for h in range(2):
                        for t in range(4):
                            last = tp(TP[h][:, t * P:(t + 1) * P], kpad[:, h * 4 + t, :])
                        last.then_inc(sem("k_tp"), 1)
                    with pe.Fori(0, QUADS) as qd:
                        u = b * QUADS + qd
                        pe.wait_ge(sem("q_pad"), u + 1)
                        pe.wait_ge(sem("att"), u * 2)
                        for i in range(TB):
                            if i < 2:
                                pe.wait_ge(sem("k_ready"), b * 2 + 2)
                            else:
                                pe.wait_ge(sem("q_ready"), u * 2 * TB + i - 1)
                            for h in range(4):
                                last = tp(TP[i % 2][:, h * P:(h + 1) * P], qpad[:, i, h, :])
                            last.then_inc(sem("q_tp"), 1)
                        for n, (i, h0, nh) in enumerate(MAXES):
                            bank = 2 + 2 * (n % 2)
                            if n < 2:
                                pe.wait_ge(sem("q_ready"), u * 2 * TB + TB)
                            else:
                                pe.wait_ge(sem("maxed"), u * len(MAXES) + n - 1)
                            qs = slice(i * P, (i + 1) * P)
                            if n < 2:
                                pe.wait_ge(sem("exp"), u * EXPS)
                            for h in range(h0, h0 + nh):
                                for k0 in range(0, (i + 1) * P, C):
                                    k1 = min((i + 1) * P, k0 + C)
                                    bk = ps[:, bank + (h - h0) + k0 // C, :]
                                    diag = k1 == (i + 1) * P
                                    last = pe.matmul(bk[:, 0:k1 - k0], qTa[:, h, qs], kTa[:, k0:k1], start=True, stop=True)
                                    if diag:
                                        last = pe.matmul(bk[:, k1 - k0 - P:k1 - k0], identb[:, :], causal[:, :],
                                                         start=False, stop=True, skip_group_check=True)
                            last.then_inc(sem("s_mm"), 1)
                        pe.wait_ge(sem("m_pad"), u + 1)
                        for i in range(TB):
                            if i >= 2:
                                pe.wait_ge(sem("q_ready"), u * 2 * TB + TB + i - 1)
                            for h in range(4):
                                last = tp(TP[i % 2][0:32, h * P:(h + 1) * P], qpad[:, i, h, 0:32])
                            last.then_inc(sem("q_tp"), 1)
                        pe.wait_ge(sem("q_ready"), (u + 1) * 2 * TB)

                        def pv(step):
                            cc, j = (0, step) if step < CT else (1, step - CT)
                            w0 = P * max(0, j - CT * cc)
                            pe.wait_ge(sem("exp"), u * EXPS + 2 * step + 2)
                            if j == 0:
                                pe.wait_ge(sem("o_ready"), u * 2 + (cc if cc == 0 else 0))
                            for h in range(4):
                                last = pe.matmul(ps[32 * h:32 * h + 32, 6 + cc, w0:C], vpad[:, j, :],
                                                 prob[:, step % 2, h, 0:C - w0], start=j == 0, stop=j >= CT * cc,
                                                 skip_group_check=True)
                            last.then_inc(sem("pv"), 1)

                        def transpose_o(cc):
                            pe.wait_ge(sem("o_ready"), u * 2 + cc + 1)
                            for t in range(CT):
                                last = tp(TP[cc][:, t * P:(t + 1) * P], OT[:, t * P:(t + 1) * P])
                            last.then_inc(sem("o_tp"), 1)

                        for step in range(STEPS):
                            cc, j = (0, step) if step < CT else (1, step - CT)
                            w0 = P * max(0, j - CT * cc)
                            for v in range(2):
                                n = 2 * step + v
                                if n >= 2:
                                    pe.wait_ge(sem("exp"), u * EXPS + n - 1)
                                for h in range(2):
                                    bk = ps[:, 2 + 2 * (n % 2) + h, 0:C - w0]
                                    diag = j >= CT * cc
                                    last = pe.matmul(bk, kTa[:, j * P:(j + 1) * P], qTa[:, 2 * v + h, cc * C + w0:(cc + 1) * C],
                                                     start=True, stop=True)
                                    if diag:
                                        last = pe.matmul(bk[:, 0:P], identb[:, :], causalT[:, :], start=False, stop=True,
                                                         skip_group_check=True)
                                last.then_inc(sem("sT_mm"), 1)
                            if step >= 1:
                                pv(step - 1)
                            if step == CT + 1:
                                transpose_o(0)
                        pv(STEPS - 1)
                        transpose_o(1)
                    pe.wait_ge(sem("att"), (b + 1) * QUADS * 2)
                    for a in range(2):
                        if a == 1:
                            pe.wait_ge(sem("att_lo"), b * 4 + 2)
                        for r in range(2):
                            for t in range(CT):
                                last = tp(TP[r][:, t * P:(t + 1) * P], att[:, a * CT + t, r::2])
                            last.then_inc(sem("att_tp"), 1)
                        pe.wait_ge(sem("att_lo"), b * 4 + a * 2 + 2)
                        for t in range(CT):
                            n = a * CT + t
                            if n >= 2:
                                pe.wait_ge(sem("x_updated"), b * TB + n - 1)
                            tt = slice(t * P, (t + 1) * P)
                            for r in range(2):
                                last = split_mm(ps[:, 6 + t % 2, 0:E], xTh1[:, r, tt], xTl1[:, r, tt],
                                                woah[:, r, :], woal[:, r, :], r == 0, r == 1)
                            last.then_inc(sem("oproj_mm"), 1)

            def ffn(base, f, updated):
                with pe.Fori(0, CHUNKS) as c:
                    g = (c + f * CHUNKS) * NT
                    pe.wait_ge(sem("x_updated"), updated + 2 * c)
                    transpose_x(c + base, None, None)
                    pe.wait_ge(sem("xT_lo"), (c + base - (CHUNKS if f else 0)) * 2 + 2)

                    def down(t):
                        pe.wait_ge(sem("in_lo"), g + t + 1)
                        if t == 0:
                            pe.wait_ge(sem("y_ready"), c + f * CHUNKS)
                        for hh in range(2):
                            hs = slice(hh * P, (hh + 1) * P)
                            last = split_mm(ps[:, 6 + hh, :], wdh[:, t, hs], wdl[:, t, hs], inh[:, t % 2, :], inl[:, t % 2, :],
                                            t == 0, t == NT - 1)
                        last.then_inc(sem("down_mm"), 1)

                    for t in range(NT):
                        ts = slice(t * P, (t + 1) * P)
                        pe.wait_ge(sem("gelu"), g + max(0, t - 1) if t >= 2 else g)
                        for r in range(2):
                            last = split_mm(ps[:, 2 + t % 2, :], wgh[:, r, ts], wgl[:, r, ts], xTh2[:, r, :], xTl2[:, r, :], r == 0, r == 1)
                        last.then_inc(sem("gate_mm"), 1)
                        pe.wait_ge(sem("prod"), g + max(0, t - 1) if t >= 2 else g)
                        for r in range(2):
                            last = split_mm(ps[:, 4 + t % 2, :], wuh[:, r, ts], wul[:, r, ts], xTh2[:, r, :], xTl2[:, r, :], r == 0, r == 1)
                        last.then_inc(sem("up_mm"), 1)
                        if t >= 1:
                            down(t - 1)
                    down(NT - 1)
                    pe.wait_ge(sem("y_ready"), c + f * CHUNKS + 1)
                    for k in range(2):
                        for m in range(4):
                            t, hh = 2 * k + m // 2, m % 2
                            last = tp(TP[k][:, m * P:(m + 1) * P], yT[:, hh, t * P:(t + 1) * P])
                        last.then_inc(sem("y_tp"), 1)

            if stop >= 2:
                pe.wait_ge(sem("x_updated"), TILES)
                ffn(CHUNKS, 0, TILES)
            if stop >= 3:
                pe.wait_ge(sem("tables"), 1)
                pe.wait_ge(sem("wb_back"), 16)
                with pe.Fori(0, B) as b:
                    with pe.Fori(0, 2) as a:
                        c = b * 2 + a
                        pe.wait_ge(sem("x_updated"), TILES + 2 * CHUNKS + c * CT)
                        pe.wait_ge(sem("PT1"), c * CT * 4)
                        transpose_x(c + 2 * CHUNKS, None, None)
                        pe.wait_ge(sem("xT_hi"), (c + 2 * CHUNKS) * 2 + 2)
                        for u in range(CT):
                            t = c * CT + u
                            for n in range(6):
                                if n >= 2:
                                    pe.wait_ge(sem("proj_out"), t * 6 + n - 1)
                                else:
                                    pe.wait_ge(sem("proj_out"), t * 6)
                                for r in range(2):
                                    w = wkvT[:, r, n * C:(n + 1) * C] if n < 2 else wqT[:, r, (n - 2) * C:(n - 1) * C]
                                    last = pe.matmul(ps[:, 2 + n % 2, :], xTf[:, r, u * P:(u + 1) * P], w, start=r == 0, stop=r == 1)
                                last.then_inc(sem("proj_mm"), 1)
                            for n in range(5):
                                pe.wait_ge(sem("qk_final"), t * 2 + (1 if n == 0 else 2))
                                if n >= 2:
                                    pe.wait_ge(sem("qkT"), t * 5 + n - 1)
                                for k in range(4):
                                    h = 16 + k if n == 0 else 4 * (n - 1) + k
                                    last = tp(TP[n % 2][:, k * P:(k + 1) * P], qk[:, h, :])
                                last.then_inc(sem("qk_tp"), 1)

                            def scores(g):
                                pe.wait_ge(sem("qkT"), t * 5 + g + 2)
                                pe.wait_ge(sem("expb"), 4 * (t * 4 + g))
                                for h in range(4):
                                    o = ps[:, 4 + h // 2, (h % 2) * E:(h % 2 + 1) * E]
                                    pe.matmul(o.rearrange("p (a k) -> p a k", a=2), qTb[:, 4 * g + h, :], kTb[:, :, g, :],
                                              start=True, stop=False)
                                    m = window[:, 2, :] if u % 2 else window[:, 0, :] if u else window[:, 1 - a, :]
                                    last = pe.matmul(o, identb[:, :], m, start=False, stop=True)
                                last.then_inc(sem("sb_mm"), 1)

                            def values(g):
                                pe.wait_ge(sem("p_final"), t * 4 + g + 1)
                                for kt in range(2):
                                    if g == 0:
                                        pe.wait_ge(sem("qkT"), (t + 1) * 5)
                                    else:
                                        pe.wait_ge(sem("PT0" if kt == 0 else "PT1"), t * 4 + g)
                                    for h in range(4):
                                        last = tp(TP[kt][:, h * P:(h + 1) * P], prb[:, g % 2, h, kt * P:(kt + 1) * P])
                                    last.then_inc(sem("p_tp"), 1)
                                pe.wait_ge(sem("oT"), t * 4 + g)
                                for kt in range(2):
                                    pe.wait_ge(sem("PT0" if kt == 0 else "PT1"), t * 4 + g + 1)
                                    last = pe.matmul(ps[:, 6, :], vb[:, kt, g * DB:(g + 1) * DB], PT[:, kt, :], start=kt == 0, stop=kt == 1)
                                last.then_inc(sem("pvb"), 1)

                            scores(0)
                            for g in range(1, 4):
                                scores(g)
                                values(g - 1)
                            values(3)
                            pe.wait_ge(sem("oT"), (t + 1) * 4)
                            pe.wait_ge(sem("x_updated"), TILES + 2 * CHUNKS + t)
                            for h in range(HB):
                                last = pe.matmul(ps[:, 7, 0:E], oT[:, h, :], woT[:, h, :], start=h == 0, stop=h == HB - 1)
                            last.then_inc(sem("wo_mm"), 1)
            if stop >= 4:
                pe.wait_ge(sem("wd_back"), 32)
                ffn(3 * CHUNKS, 1, TILES + 2 * CHUNKS + TILES)



_ORDER = ["L0_attn_a_x", "L0_attn_a_Wq", "L0_attn_a_Wk", "L0_attn_a_Wv", "L0_attn_a_Wo", "L0_attn_a_bo",
          "L0_attn_b_wq", "L0_attn_b_wk", "L0_attn_b_wv", "L0_attn_b_wo", "L0_attn_b_q_norm_w", "L0_attn_b_k_norm_w",
          "L0_ffn_gate_W_packed", "L0_ffn_gate_scales", "L0_ffn_up_W_packed", "L0_ffn_up_scales",
          "L0_ffn_down_W_packed", "L0_ffn_down_scales"]


def kernel(**inputs):
    import numpy as np
    import concourse.bacc as bacc
    from concourse.bass_utils import run_bass_kernel_spmd

    nc = bacc.Bacc("TRN2", target_bir_lowering=False, num_devices=1)
    arrays, args = {}, []

    def put(name, a):
        arrays[name] = a
        args.append(nc.dram_tensor(name, a.shape, mybir.dt.from_np(a.dtype), kind="ExternalInput").ap())

    for name in _ORDER:
        put(name, np.ascontiguousarray(inputs[name]))
    freq = (1.0 / np.float32(10000.0) ** (np.arange(0, DB, 2, dtype=np.float32) / np.float32(DB))).astype(np.float32)
    angle = (np.arange(T, dtype=np.float32)[:, None] * freq[None, :]).astype(np.float32)
    put("rope_cos", np.cos(angle).astype(np.float32))
    put("rope_sin", np.sin(angle).astype(np.float32))
    out = nc.dram_tensor("out", (B, T, E), F32, kind="ExternalOutput").ap()
    build(nc, *args, out)
    r = run_bass_kernel_spmd(nc, [arrays], core_ids=[0])
    return r.results[0]["out"]
```

```python
import concourse.bass as bass
from concourse import mybir
from concourse.alu_op_type import AluOpType as ALU
from contextlib import ExitStack

F32 = mybir.dt.float32
F32R = mybir.dt.float32r
BF16 = mybir.dt.bfloat16
I32 = mybir.dt.int32
ACT = mybir.ActivationFunctionType
AX = mybir.AxisListType

P = 128
E = 256
B, T = 2, 1024
TILES = B * T // P
TB = T // P
CT = 4
CHUNKS = TILES // CT
C = CT * P
HA, DA = 16, 16
QKV = E + 2 * DA
QUADS = HA // 4
HB, KVB, DB = 16, 4, 128
MLP = 2048
NT = MLP // P
UNIT = MLP // 2
BIG = -1.0e30
LN_EPS, RMS_EPS = 1e-5, 1e-6
RSQRT_SEED = float(0x5F3759DF)
POOL_CONST = 19
MAXES = [(i, h, 2) for i in range(CT) for h in (0, 2)] + [(i, h, 1) for i in range(CT, TB) for h in range(4)]
STEPS = CT + TB
EXPS = 2 * STEPS
FFN_NORM, FFN_TP, FFN_SPLIT = 7, 9, 10
RSQRT_LINKS = 2 + 3 * 3
DONE_A = TILES
DONE_F = DONE_A + 2 * CHUNKS
DONE_B = DONE_F + TILES + 1


class Chain:

    def __init__(self, eng, sem):
        self.eng, self.sem, self.base, self.k = eng, sem, 0, 0

    def at(self, base):
        self.base, self.k = base, 0

    def link(self, ins):
        self.k += 1
        ins.then_inc(self.sem, 1)
        self.eng.wait_ge(self.sem, self.base + self.k)


def build(nc, x, Wq, Wk, Wv, Wo, bo, wq, wk, wv, wo, qw, kw, gW, gS, uW, uS, dW, dS, cos, sin, out, stop=9, dbg=None):
    ctx = ExitStack()
    with ctx:
        def sb(name, shape, dt, stack=ctx):
            return stack.enter_context(nc.sbuf_tensor(name, shape, dt))

        sems = {}

        def sem(name):
            if name not in sems:
                sems[name] = ctx.enter_context(nc.semaphore(name))
            return sems[name]

        X = sb("X", [P, TILES + 1, E], F32)
        wgh = sb("wgh", [P, 2, MLP], F32R)
        wgl = sb("wgl", [P, 2, MLP], F32R)
        s = ExitStack()
        wqr = sb("wqr", [P, HB, E], F32, s)
        wor = sb("wor", [P, 2, HB, P], F32, s)
        s.close()
        wuh = sb("wuh", [P, 2, MLP], F32R)
        wul = sb("wul", [P, 2, MLP], F32R)
        ident = sb("ident", [P, P], F32)
        identb = sb("identb", [P, P], BF16)
        causal = sb("causal", [P, P], BF16)
        causalT = sb("causalT", [P, P], BF16)
        window = sb("window", [P, 3, E], BF16)
        stats = sb("stats", [P, CT, 6], F32)
        mv = sb("mv", [P, CT, 2], F32)
        var = sb("var", [P, CT], F32)
        ryy = sb("ryy", [P, CT], F32)
        mean = sb("mean", [P, TILES], F32)
        rstd = sb("rstd", [P, TILES], F32)
        rtmp = sb("rtmp", [P, CT], F32)
        xn = sb("xn", [P, CT, E], F32)
        s = ExitStack()
        raw = [sb(f"raw{i}", [P, MLP], I32, s) for i in range(2)]
        scl = [sb(f"scl{i}", [P, P], F32, s) for i in range(2)]
        s.close()
        s = ExitStack()
        wdh = sb("wdh", [P, NT, E], F32R, s)
        wdl = sb("wdl", [P, NT, E], F32R, s)
        mid = ExitStack()
        late = ExitStack()
        wkvr = sb("wkvr", [P, 2, KVB, E], F32, late)
        late.close()
        raw.append(sb("raw2", [P, MLP], I32, mid))
        mag = sb("mag", [P, 2, UNIT], I32, mid)
        sgn = sb("sgn", [P, 2, UNIT], F32, mid)
        val = sb("val", [P, 2, UNIT], F32, mid)
        deq = sb("deq", [P, 2, UNIT], F32, mid)
        scl.append(sb("scl2", [P, P], F32, mid))
        late = ExitStack()
        wTs = sb("wTs", [P, 10240], F32, late)
        late.close()
        sa = sb("sa", [P, 2, QKV], F32, mid)
        so = sb("so", [P, 2, E], F32, mid)
        mid.close()
        mid = ExitStack()
        kpad = sb("kpad", [P, TB, P], F32, mid)
        OT = sb("OT", [P, C], F32, mid)
        bob = sb("bob", [P, E], F32, mid)
        wah = sb("wah", [P, 2, QKV], F32R, mid)
        wal = sb("wal", [P, 2, QKV], F32R, mid)
        woah = sb("woah", [P, 2, E], F32R, mid)
        woal = sb("woal", [P, 2, E], F32R, mid)
        qkv = sb("qkv", [P, TB, QKV], F32, mid)
        qpad = sb("qpad", [P, TB, 4, P], F32, mid)
        qTa = sb("qTa", [P, 4, T], F32R, mid)
        kTa = sb("kTa", [P, T], F32R, mid)
        vpad = sb("vpad", [P, TB, 32], F32, mid)
        nmax = sb("nmax", [P, TB, 4], F32, mid)
        rec = sb("rec", [P, CT, 4], F32, mid)
        att = sb("att", [P, TB, E], F32, mid)
        both = ExitStack()
        prob = sb("prob", [P, 2, 4, C], F32, both)
        both.close()
        xTh1 = sb("xTh1", [P, 2, C], F32R, mid)
        xTl1 = sb("xTl1", [P, 2, C], F32R, mid)
        mid.close()
        s2 = ExitStack()
        wTb = sb("wTb", [P, 10240], F32, s2)
        mid = ExitStack()
        xTh2 = sb("xTh2", [P, 2, 2, C], F32R, mid)
        xTl2 = sb("xTl2", [P, 2, 2, C], F32R, mid)
        gel = sb("gel", [P, 2, C], F32, mid)
        prod = sb("prod", [P, 2, C], F32, mid)
        inh = sb("inh", [P, 3, C], F32R, mid)
        inl = sb("inl", [P, 3, C], F32R, mid)
        yT = sb("yT", [P, 2, C], F32, mid)
        mid.close()
        mid = ExitStack()
        xT1 = sb("xT1", [P, 2, 2, P], F32, mid)
        qk = sb("qk", [P, 20, DB], F32, mid)
        rot = sb("rot", [P, 20, DB], F32, mid)
        qTb = sb("qTb", [P, HB, P], F32, mid)
        kTb = sb("kTb", [P, 2, KVB, P], F32, mid)
        prb = sb("prb", [P, 2, 4, E], F32, mid)
        sqb = sb("sqb", [P, 2, C], F32, mid)
        ssb = sb("ssb", [P, 20], F32, mid)
        rq = sb("rq", [P, 2, HB], F32, mid)
        rk = sb("rk", [P, KVB], F32, mid)
        rqt = sb("rqt", [P, HB], F32, mid)
        nmx = sb("nmx", [P, 4], F32, mid)
        nmb = sb("nmb", [P, 2, 4], F32, mid)
        rsb = sb("rsb", [P, 2, 4], F32, mid)
        rcb = sb("rcb", [P, 2, 4], F32, mid)
        mid.close()
        s2.close()
        s.close()
        mid = ExitStack()
        tabs = sb("tabs", [P, 4, TB, DB], F32, mid)
        PT = sb("PT", [P, 2, C], F32, mid)
        vb = sb("vb", [P, 2, C], F32, mid)
        oT = sb("oT", [P, HB, P], F32, mid)
        mid.close()

        wqT = wTb[:, 0:4096].rearrange("p (r n) -> p r n", r=2)
        wkvT = wTb[:, 4096:6144].rearrange("p (r n) -> p r n", r=2)
        woT = wTb[:, 6144:10240].rearrange("p (h n) -> p h n", h=HB)

        ps = ctx.enter_context(nc.psum_tensor("ps", [P, 8, 512], F32))
        TP = [ps[:, 0, :], ps[:, 1, :]]

        wb_keep = nc.dram_tensor("wb_keep", (P, 10240), F32, kind="Internal").ap()
        wd_keep = nc.dram_tensor("wd_keep", (P, 2 * NT * E), F32, kind="Internal").ap()

        w_mats = [(wgh, wgl), (wuh, wul), (wdh, wdl)]

        def wb_slot(n):
            return wTs[:, n * 512:(n + 1) * 512]

        def w_slot(i, part, nib, k):
            m = w_mats[i][part]
            return m[:, nib, k * 512:(k + 1) * 512] if i < 2 else m[:, 4 * k + nib:4 * k + nib + 3:2, :]

        def w_psum(i, n):
            o = ps[:, n % 4, :]
            return o if i < 2 else o.rearrange("p (a e) -> p a e", a=2)

        W_UNITS = [(i, nib, j) for i in range(3) for nib in range(2) for j in range(2)]

        def packed(i, j):
            order = "p (j a c) -> p j a c" if i < 2 else "p (a j c) -> p j a c"
            return raw[i][:, :].rearrange(order, j=2, a=2)[:, j]

        def scales(i, j):
            order = "p (j a s) -> p j a s" if i < 2 else "p (a j s) -> p j a s"
            return scl[i][:, :].rearrange(order, j=2, a=2)[:, j]

        WB_ORDER = list(range(8)) + list(range(12, 20)) + list(range(8, 12))

        block = ctx.enter_context(nc.Block())

        @block.sync
        def _(sp):
            def packed_in(i, w, sc):
                sp.dma_start(raw[i][:, :].rearrange("p (t c) -> p t c", c=E),
                             w.rearrange("(t p r) c -> p t (r c)", p=P, r=2)).then_inc(sem(f"raw{i}_in"), 16)
                sp.dma_start(scl[i][:, :].rearrange("p (t c) -> p t c", c=16),
                             sc.rearrange("(t p r) c -> p t (r c)", p=P, r=2)).then_inc(sem(f"raw{i}_in"), 16)
            packed_in(0, gW, gS)
            sp.dma_start(wqr[:, :, :], wq.rearrange("(h p) k -> p h k", p=P)).then_inc(sem("wq_in"), 16)
            sp.dma_start(wor[:, :, :, :], wo.rearrange("(u p) (h d) -> p u h d", p=P, d=P)).then_inc(sem("wo_in"), 16)
            packed_in(1, uW, uS)
            sp.dma_start(wkvr[:, 0, :, :], wk.rearrange("(h p) k -> p h k", p=P)).then_inc(sem("wkv_in"), 16)
            sp.dma_start(wkvr[:, 1, :, :], wv.rearrange("(h p) k -> p h k", p=P)).then_inc(sem("wkv_in"), 16)
            sp.dma_start(X[:, 0:TILES, :], x.rearrange("b (t p) e -> p (b t) e", p=P)).then_inc(sem("x_in"), 16)
            sp.wait_ge(sem("wb_tp"), 20)
            sp.dma_start(raw[2][:, :].rearrange("p (u c) -> p u c", u=2),
                         dW.rearrange("(u p) c -> p u c", u=2)).then_inc(sem("raw2_in"), 16)
            sp.dma_start(scl[2][:, :].rearrange("p (u c) -> p u c", u=2),
                         dS.rearrange("(u p) c -> p u c", u=2)).then_inc(sem("raw2_in"), 16)
            sp.wait_ge(sem("wb_ready"), 20)
            sp.dma_start(wb_keep, wTs[:, :]).then_inc(sem("wb_kept"), 16)
            sp.wait_ge(sem("wb_kept"), 16)
            sp.dma_start(sa[:, :, 0:E], Wq.rearrange("(p r) n -> p r n", r=2)).then_inc(sem("wa_in"), 16)
            sp.dma_start(sa[:, :, E:E + DA], Wk.rearrange("(p r) n -> p r n", r=2)).then_inc(sem("wa_in"), 16)
            sp.dma_start(sa[:, :, E + DA:], Wv.rearrange("(p r) n -> p r n", r=2)).then_inc(sem("wa_in"), 16)
            sp.dma_start(so[:, :, :], Wo.rearrange("(p r) n -> p r n", r=2)).then_inc(sem("wa_in"), 16)
            sp.wait_ge(sem("lo_ready"), 24)
            sp.dma_start(bob[:, :], bo.rearrange("(a n) -> a n", a=1).broadcast_to([P, E])).then_inc(sem("bo_in"), 16)
            sp.dma_start(wd_keep[:, 0:NT * E], wdh[:, :, :].rearrange("p a b -> p (a b)").bitcast(F32)).then_inc(sem("wd_kept"), 16)
            sp.dma_start(wd_keep[:, NT * E:], wdl[:, :, :].rearrange("p a b -> p (a b)").bitcast(F32)).then_inc(sem("wd_kept"), 16)
            if stop >= 3:
                sp.wait_ge(sem("x_updated"), 16)
                sp.dma_start(wTb[:, :], wb_keep).then_inc(sem("wb_back"), 16)
                sp.wait_ge(sem("x_updated"), 16 + 2 * CHUNKS)
                for n in range(2):
                    sp.dma_start(tabs[:, n, :, 0:64], cos.rearrange("(t p) d -> p t d", p=P)).then_inc(sem("tab_in"), 16)
                    sp.dma_start(tabs[:, n, :, 64:128], sin.rearrange("(t p) d -> p t d", p=P)).then_inc(sem("tab_in"), 16)
                sp.dma_start(vb[:, 0, 0:DB], qw.rearrange("(a n) -> a n", a=1).broadcast_to([P, DB])).then_inc(sem("tab_in"), 16)
                sp.dma_start(vb[:, 0, DB:2 * DB], kw.rearrange("(a n) -> a n", a=1).broadcast_to([P, DB])).then_inc(sem("tab_in"), 16)
            if stop >= 4:
                sp.wait_ge(sem("x_updated"), DONE_B)
                sp.wait_ge(sem("wd_kept"), 32)
                sp.wait_ge(sem("proj_out"), 5 + 6 * TILES)
                sp.dma_start(wdh[:, :, :].rearrange("p a b -> p (a b)").bitcast(F32), wd_keep[:, 0:NT * E]).then_inc(sem("wd_back"), 16)
                sp.dma_start(wdl[:, :, :].rearrange("p a b -> p (a b)").bitcast(F32), wd_keep[:, NT * E:]).then_inc(sem("wd_back"), 16)
            done = {0: 0, 1: 16, 2: 16 + 2 * CHUNKS, 3: DONE_B}.get(stop)
            for c in range(CHUNKS):
                sp.wait_ge(sem("x_updated"), done if done is not None else DONE_B + 2 * (c + 1))
                if stop == 0:
                    sp.wait_ge(sem("x_in"), 16)
                b, a = divmod(c, CHUNKS // B)
                sp.dma_start(out[b, a * C:(a + 1) * C, :].rearrange("(t p) e -> p t e", p=P),
                             X[:, c * CT:(c + 1) * CT, :]).then_inc(sem("out_written"), 16)
            sp.wait_ge(sem("out_written"), 16 * CHUNKS)

        @block.gpsimd
        def _(pool):
            def diagonal(m):
                pool.memset(m, 0.0).then_inc(sem("pool"), 1)
                pool.wait_ge(sem("pool"), diagonal.n + 1)
                pool.affine_select(out=m, in_=m, compare_op=ALU.not_equal, fill=1.0, base=0,
                                   pattern=[[-1, P]], channel_multiplier=1).then_inc(sem("pool"), 1)
                diagonal.n += 2
            diagonal.n = 0
            diagonal(ident[:, :])
            diagonal(identb[:, :])

            def mask(m, keep_where, base, step, per_partition):
                pool.memset(m, 0.0).then_inc(sem("pool"), 1)
                pool.wait_ge(sem("pool"), diagonal.n + 1)
                pool.affine_select(out=m, in_=m, compare_op=keep_where, fill=BIG, base=base,
                                   pattern=[[step, P]], channel_multiplier=per_partition).then_inc(sem("pool"), 1)
                diagonal.n += 2
            mask(causal[:, :], ALU.is_ge, 0, -1, 1)
            mask(causalT[:, :], ALU.is_ge, 0, 1, -1)
            mask(window[:, 0, 0:P], ALU.is_ge, 0, -1, 1)
            mask(window[:, 0, P:E], ALU.is_gt, 0, 1, -1)
            mask(window[:, 1, 0:P], ALU.is_ge, 0, -1, 1)
            pool.memset(window[:, 1, P:E], BIG).then_inc(sem("pool"), 1)
            diagonal.n += 1
            mask(window[:, 2, 0:P], ALU.is_gt, 0, 1, -1)
            mask(window[:, 2, P:E], ALU.is_ge, 0, -1, 1)
            assert diagonal.n == POOL_CONST
            for n, (i, nib, j) in enumerate(W_UNITS):
                if nib == 0 and j == 0:
                    pool.wait_ge(sem(f"raw{i}_in"), 32)
                pool.wait_ge(sem("sign"), n + 1)
                sg = sgn[:, n % 2, :].rearrange("p (a s k) -> p a s k", a=2, k=16)
                sc = scales(i, j).rearrange("p a (s k) -> p a s k", k=1).broadcast_to([P, 2, 32, 16])
                pool.tensor_tensor(sg, sg, sc, ALU.mult).then_inc(sem("scaled"), 1)
            if stop >= 1:
                pool.wait_ge(sem("lo_ready"), 24)
                pool.wait_ge(sem("wb_kept"), 16)
                pool.memset(kpad[:, :, :], 0.0)
                pool.memset(vpad[:, :, :], 0.0).then_inc(sem("pads"), 1)
                pool.wait_ge(sem("pads"), 1)
                pool.memset(kpad[:, :, 16:18], 1.0)
                pool.memset(vpad[:, :, 16:17], 1.0)
                pool.memset(qpad[:, :, :, :], 0.0).then_inc(sem("pads"), 1)
                pool.wait_ge(sem("bo_in"), 16)
                for b in range(B):
                    pool.wait_ge(sem("ln_ready"), 2 * (b + 1))
                    v = X[:, b * TB:(b + 1) * TB, :]
                    pool.tensor_tensor(v, v, bob[:, :].rearrange("p (a e) -> p a e", a=1).broadcast_to([P, TB, E]),
                                       ALU.add).then_inc(sem("bias_added"), 1)
            if stop >= 3:
                with pool.Fori(0, CHUNKS) as c:
                    for k in range(4 * CT):
                        pool.wait_ge(sem("rcb"), c * 4 * CT + k + 1)
                        v = prb[:, k % 2, :, :]
                        pool.tensor_tensor(v, v, rcb[:, k % 2, :].rearrange("p (h d) -> p h d", d=1).broadcast_to([P, 4, E]),
                                           ALU.mult).then_inc(sem("p_final"), 1)

        @block.scalar
        def _(act):
            def copy(o, i, s):
                act.activation(o, i, ACT.Copy).then_inc(sem(s), 1)

            def decode(n):
                act.wait_ge(sem("codes"), 2 * n + 2)
                act.activation(sgn[:, n % 2, :], sgn[:, n % 2, :].bitcast(I32), ACT.Copy, bias=1.0, scale=-0.25)\
                   .then_inc(sem("sign"), 1)
                act.activation(val[:, n % 2, :], mag[:, n % 2, :], ACT.Copy, bias=-8.0, scale=2.0).then_inc(sem("val"), 1)

            decode(0)
            for u in range(len(W_UNITS)):
                i, nib, j = W_UNITS[u]
                if u + 1 < len(W_UNITS):
                    decode(u + 1)
                for k in (2 * j, 2 * j + 1):
                    n = 2 * u + k - 2 * j
                    act.wait_ge(sem("w_tp"), n + 1)
                    copy(w_slot(i, 0, nib, k), w_psum(i, n), "hi_ready")
                for n in range(4 * u, min(4 * u + 4, 20)):
                    act.wait_ge(sem("wb_tp"), n + 1)
                    copy(wb_slot(WB_ORDER[n]), ps[:, 4 + n % 4, :], "wb_ready")

            def split_x(n, hi):
                for r in range(2):
                    act.wait_ge(sem("xn_tp"), 2 * n + r + 1)
                    copy(hi[:, r, :], TP[r], "xT_hi")

            if stop >= 1:
                act.wait_ge(sem("wa_in"), 64)
                act.wait_ge(sem("lo_ready"), 24)
                copy(wah[:, :, :], sa[:, :, :], "wa_hi")
                copy(woah[:, :, :], so[:, :, :], "wa_hi")
                with act.Fori(0, B) as b:
                    for a in range(2):
                        act_c = b * 2 + a
                        split_x(act_c, xTh1)
                        for t in range(CT):
                            act.wait_ge(sem("qkv_mm"), act_c * CT + t + 1)
                            copy(qkv[:, a * CT + t, :], ps[:, 6 + t % 2, 0:QKV], "qkv_ready")
                    for h in range(2):
                        act.wait_ge(sem("k_tp"), b * 2 + h + 1)
                        copy(kTa[:, h * C:(h + 1) * C], TP[h], "k_ready")
                    with act.Fori(0, QUADS) as qd:
                        u = b * QUADS + qd
                        for i in range(TB):
                            act.wait_ge(sem("q_tp"), u * 2 * TB + i + 1)
                            copy(qTa[:, :, i * P:(i + 1) * P], TP[i % 2].rearrange("p (h q) -> p h q", h=4), "q_ready")
                        for i in range(TB):
                            act.wait_ge(sem("q_tp"), u * 2 * TB + TB + i + 1)
                            copy(qTa[0:32, :, i * P:(i + 1) * P],
                                 TP[i % 2][0:32, :].rearrange("p (h q) -> p h q", h=4), "q_ready")
                        n = 0
                        for cc in range(2):
                            for j in range(CT * (cc + 1)):
                                step = 4 * cc + j
                                w = C - P * max(0, j - CT * cc)
                                for v in range(2):
                                    act.wait_ge(sem("sT_mm"), u * EXPS + n + 1)
                                    if v == 0 and step >= 2:
                                        act.wait_ge(sem("pv"), u * STEPS + step - 1)
                                    act.activation(prob[:, step % 2, 2 * v:2 * v + 2, 0:w],
                                                   ps[:, 2 + 2 * (n % 2):4 + 2 * (n % 2), 0:w], ACT.Exp)\
                                       .then_inc(sem("exp"), 1)
                                    n += 1
                            act.wait_ge(sem("pv"), u * STEPS + (CT if cc == 0 else STEPS))
                            act.wait_ge(sem("o_tp"), u * 2 + cc)
                            copy(OT[:, :], ps[:, 6 + cc, :], "o_ready")
                    for a in range(2):
                        for r in range(2):
                            act.wait_ge(sem("att_tp"), b * 4 + a * 2 + r + 1)
                            copy(xTh1[:, r, :], TP[r], "att_hi")

            def split_chunk(n, buf):
                for r in range(2):
                    act.wait_ge(sem("xn_tp"), 2 * n + r + 1)
                    copy(xTh2[:, buf, r, :], TP[r], "xT_hi")

            def ffn(f):
                n0 = CHUNKS + f * (CHUNKS + 1)
                split_chunk(n0, 0)
                with act.Fori(0, CHUNKS // 2) as i:
                    g = (i + f * 2) * 2 * NT
                    for st in range(2 * NT):
                        k, t = divmod(st, NT)
                        if st == NT + 2:
                            output(f, i, 0)
                        act.wait_ge(sem("gate_mm"), g + st + 1)
                        if st >= 2:
                            act.wait_ge(sem("prod"), g + st - 1)
                        act.activation(gel[:, st % 2, :], ps[:, 2 + st % 2, :], ACT.Gelu_apprx_tanh).then_inc(sem("gelu"), 1)
                        act.wait_ge(sem("prod"), g + st + 1)
                        if st >= 3:
                            act.wait_ge(sem("down_mm"), g + st - 2)
                        copy(inh[:, st % 3, :], prod[:, st % 2, :], "in_hi")
                        if t == FFN_SPLIT:
                            split_chunk(2 * i + (n0 + k + 1), 1 - k)
                    output(f, i, 1)

            def output(f, i, k):
                c = (i + f * 2) * 2 + k
                act.wait_ge(sem("down_mm"), (c + 1) * NT)
                act.wait_ge(sem("y_tp"), c * 2)
                copy(yT[:, :, :], ps[:, 6:8, :], "y_ready")

            if stop >= 2:
                ffn(0)
            if stop >= 3:
                def tokens(m):
                    act.wait_ge(sem("xn1_tp"), m + 1)
                    copy(xT1[:, TPAR, :, :], TP[0][:, 0:E].rearrange("p (r k) -> p r k", r=2), "xT1")

                def projected(j, m, n, bank):
                    act.wait_ge(sem("proj_mm"), j + 1)
                    src = ps[:, 2 + bank, :]
                    if n == 5:
                        copy(vb[:, VPAR, :], src, "proj_out")
                        return
                    if n == 0:
                        act.wait_ge(sem("qk_tp"), m * 5)
                    h = 4 * (n - 1) if n else HB
                    act.activation(qk[:, h:h + 4, :], src.rearrange("p (h d) -> p h d", h=4), ACT.Copy)
                    act.wait_ge(sem("ss"), m * 5 + max(0, n - 1))
                    act.activation(sqb[:, n % 2, :], src, ACT.Square).then_inc(sem("proj_out"), 1)

                def transposed(m, n):
                    act.wait_ge(sem("qk_tp"), m * 5 + n + 1)
                    dst = kTb[:, MPAR, :, :] if n == 0 else qTb[:, 4 * (n - 1):4 * n, :]
                    copy(dst, TP[n % 2].rearrange("p (h q) -> p h q", h=4), "qkT")

                def prob_half(k):
                    act.wait_ge(sem("p_tp"), k * 2 + 1)
                    act.wait_ge(sem("pvb"), k)
                    copy(PT[:, 0, :], TP[0], "PT0")

                def group_out(k, g):
                    act.wait_ge(sem("pvb"), k + 1)
                    copy(oT[:, 4 * g:4 * g + 4, :], ps[:, 6, :].rearrange("p (h q) -> p h q", h=4), "oT")

                TPAR, MPAR = 0, 0
                tokens(0)
                for n in range(5):
                    projected(n, 0, n, n % 2)
                TPAR = 1
                tokens(1)
                for n in range(5):
                    transposed(0, n)
                with act.Fori(0, CHUNKS) as c:
                    for u in range(CT):
                        t = c * CT + u
                        m = c * CT + (u + 1)
                        TPAR, MPAR, VPAR = u % 2, (u + 1) % 2, u % 2

                        def exps(g):
                            act.wait_ge(sem("nmb"), t * 4 + g + 1)
                            act.wait_ge(sem("p_tp"), 2 * (t * 4 + g))
                            for h in range(4):
                                act.activation(prb[:, g % 2, h, :], ps[:, 4 + h // 2, (h % 2) * E:(h % 2 + 1) * E],
                                               ACT.Exp, bias=nmb[:, g % 2, h:h + 1], scale=rq[:, u % 2, 4 * g + h:4 * g + h + 1],
                                               accum_out=rsb[:, g % 2, h:h + 1]).then_inc(sem("expb"), 1)

                        def project(j, n):
                            projected(t * 6 + (5 + j), m, n, (j + 1) % 2)

                        def finish(g):
                            group_out(t * 4 + g, (g - 1) % 4)
                        exps(0)
                        prob_half(t * 4)
                        finish(0)
                        project(0, 5)
                        project(1, 0)
                        project(2, 1)
                        exps(1)
                        prob_half(t * 4 + 1)
                        project(3, 2)
                        finish(1)
                        project(4, 3)
                        project(5, 4)
                        exps(2)
                        prob_half(t * 4 + 2)
                        tokens(c * CT + (u + 2))
                        finish(2)
                        exps(3)
                        prob_half(t * 4 + 3)
                        transposed(m, 0)
                        transposed(m, 1)
                        finish(3)
                        for n in (2, 3, 4):
                            transposed(m, n)
                prob_half(4 * TILES)
                group_out(4 * TILES, 3)
            if stop >= 4:
                ffn(1)

        @block.vector
        def _(dve):
            ch = Chain(dve, sem("dve"))

            def rsqrt(y, v, t, out=None):
                ch.link(dve.tensor_scalar(t.bitcast(I32), v.bitcast(I32), 1, None, ALU.logical_shift_right))
                ch.link(dve.tensor_scalar(y.bitcast(I32), t.bitcast(I32), -1.0, RSQRT_SEED, ALU.mult, ALU.add))
                for n in range(3):
                    ch.link(dve.tensor_tensor(t, y, y, ALU.mult))
                    ch.link(dve.scalar_tensor_tensor(out=t, in0=t, scalar=-0.5, in1=v, op0=ALU.mult, op1=ALU.mult))
                    ch.link(dve.scalar_tensor_tensor(out=out if n == 2 and out is not None else y,
                                                     in0=t, scalar=1.5, in1=y, op0=ALU.add, op1=ALU.mult))

            LN_LINKS = 3 + RSQRT_LINKS

            def moments(c):
                dve.memset(ryy[:, :], 0.0)
                for t in range(CT):
                    last = dve.bn_stats(stats[:, t, :], X[:, c * CT + t, :])
                ch.link(last)
                dve.memset(rtmp[:, :], 0.0)
                for t in range(CT):
                    last = dve.bn_aggr(mv[:, t, :], stats[:, t, :])
                ch.link(last)
                dve.tensor_scalar(mean[:, bass.ds(c * CT, CT)], mv[:, :, 0], 1.0, None, ALU.mult)
                ch.link(dve.tensor_scalar(var[:, :], mv[:, :, 1], LN_EPS, None, ALU.add))
                rsqrt(ryy[:, :], var[:, :], rtmp[:, :], out=rstd[:, bass.ds(c * CT, CT)])

            def normalise(n, c):
                dve.wait_ge(sem("xn_tp"), 2 * n)
                for t in range(CT):
                    k = c * CT + t
                    last = dve.tensor_scalar(xn[:, t, :], X[:, k, :], mean[:, bass.ds(k, 1)], rstd[:, bass.ds(k, 1)],
                                             ALU.subtract, ALU.mult)
                last.then_inc(sem("ln_ready"), 1)

            def split_x(n, hi, lo):
                for r in range(2):
                    dve.wait_ge(sem("xT_hi"), 2 * n + r + 1)
                    dve.tensor_tensor(lo[:, r, :], TP[r], hi[:, r, :].bitcast(F32), ALU.subtract).then_inc(sem("xT_lo"), 1)

            def codes(n):
                i, nib, j = W_UNITS[n]
                if nib == 0 and j == 0:
                    dve.wait_ge(sem(f"raw{i}_in"), 32)
                if n >= 2:
                    dve.wait_ge(sem("deq"), n - 1)
                for dst, bits in ((mag, 7), (sgn, 8)):
                    o = dst[:, n % 2, :].bitcast(I32).rearrange("p (a c) -> p a c", a=2)
                    if nib:
                        ins = dve.tensor_scalar(o, packed(i, j), 4, bits, ALU.logical_shift_right, ALU.bitwise_and)
                    else:
                        ins = dve.tensor_scalar(o, packed(i, j), bits, None, ALU.bitwise_and)
                    ins.then_inc(sem("codes"), 1)

            def low_parts(u):
                i, nib, j = W_UNITS[u]
                for k in (2 * j, 2 * j + 1):
                    n = 2 * u + k - 2 * j
                    dve.wait_ge(sem("hi_ready"), n + 1)
                    dve.tensor_tensor(w_slot(i, 1, nib, k), w_psum(i, n),
                                      w_slot(i, 0, nib, k).bitcast(F32), ALU.subtract).then_inc(sem("lo_ready"), 1)

            codes(0)
            for n in range(len(W_UNITS)):
                if n + 1 < len(W_UNITS):
                    codes(n + 1)
                m, v = mag[:, n % 2, :], val[:, n % 2, :]
                dve.wait_ge(sem("val"), n + 1)
                ch.link(dve.scalar_tensor_tensor(out=v, in0=m, scalar=-2.0, in1=v, op0=ALU.add, op1=ALU.max))
                ch.link(dve.scalar_tensor_tensor(out=v, in0=m, scalar=0.5, in1=v, op0=ALU.mult, op1=ALU.max))
                if n >= 1:
                    low_parts(n - 1)
                dve.wait_ge(sem("scaled"), n + 1)
                if n >= 2:
                    dve.wait_ge(sem("w_tp"), 2 * (n - 1))
                dve.tensor_tensor(deq[:, n % 2, :], v, sgn[:, n % 2, :], ALU.mult).then_inc(sem("deq"), 1)
            low_parts(len(W_UNITS) - 1)
            base = ch.k

            if stop >= 1:
                dve.wait_ge(sem("x_in"), 16)
                for w, (o, h, i) in enumerate([(wal, wah, sa), (woal, woah, so)]):
                    dve.wait_ge(sem("wa_hi"), w + 1)
                    dve.tensor_tensor(o[:, :, :], i[:, :, :], h[:, :, :].bitcast(F32), ALU.subtract).then_inc(sem("wa_lo"), 1)
                PER_Q = 1 + 1 + 2
                PER_B = 4 * LN_LINKS + 1 + QUADS * PER_Q
                with dve.Fori(0, B) as b:
                    for a in range(2):
                        ch.at(base + b * PER_B + a * LN_LINKS)
                        moments(b * 2 + a)
                        normalise(b * 2 + a, b * 2 + a)
                        assert ch.k == LN_LINKS
                        if a == 0:
                            dve.wait_ge(sem("qkv_mm"), b * 2 * CT)
                        split_x(b * 2 + a, xTh1, xTl1)
                    ch.at(base + b * PER_B + 2 * LN_LINKS)
                    dve.wait_ge(sem("pads"), 2)
                    dve.wait_ge(sem("qkv_ready"), b * TB + TB)
                    kk = qkv[:, :, E:E + DA]
                    for blk in (0, 64):
                        last = dve.tensor_scalar(kpad[:, :, blk:blk + DA].bitcast(F32R), kk, 0.25, None, ALU.mult)
                    ch.link(last)
                    for blk in (32, 96):
                        last = dve.scalar_tensor_tensor(out=kpad[:, :, blk:blk + DA].bitcast(F32R), in0=kk, scalar=0.25,
                                                        in1=kpad[:, :, 0:DA], op0=ALU.mult, op1=ALU.subtract)
                    dve.tensor_copy(vpad[:, :, 0:DA], qkv[:, :, E + DA:]).then_inc(sem("kv_pad"), 1)
                    with dve.Fori(0, QUADS) as qd:
                        u = b * QUADS + qd
                        ch.at(base + b * PER_B + 2 * LN_LINKS + 1 + qd * PER_Q)
                        dve.wait_ge(sem("q_tp"), u * 2 * TB)
                        dve.memset(qpad[:, :, :, 16:18], 0.0)
                        src = qkv[:, :, bass.ds(qd * 64, 64)].rearrange("p t (h d) -> p t h d", h=4)
                        for blk in (0, 32):
                            last = dve.tensor_copy(qpad[:, :, :, blk:blk + DA].bitcast(F32R), src)
                        ch.link(last)
                        for blk in (64, 96):
                            last = dve.tensor_tensor(qpad[:, :, :, blk:blk + DA].bitcast(F32R), src, qpad[:, :, :, 0:DA], ALU.subtract)
                        last.then_inc(sem("q_pad"), 1)
                        for n, (i, h0, nh) in enumerate(MAXES):
                            w = (i + 1) * P
                            dve.wait_ge(sem("s_mm"), u * len(MAXES) + n + 1)
                            bank = 2 + 2 * (n % 2)
                            if nh == 2:
                                ins = dve.tensor_reduce(nmax[:, i, h0:h0 + 2], ps[:, bank:bank + 2, 0:w], AX.X, ALU.max, negate=True)
                            else:
                                ins = dve.tensor_reduce(nmax[:, i, h0:h0 + 1], ps[:, bank:bank + 2, :].rearrange("p a b -> p (a b)")[:, 0:w],
                                                        AX.X, ALU.max, negate=True)
                            ins.then_inc(sem("maxed"), 1)
                        dve.wait_ge(sem("maxed"), (u + 1) * len(MAXES))
                        dve.wait_ge(sem("q_tp"), u * 2 * TB + TB)
                        ch.link(dve.tensor_copy(qpad[:, :, :, 16].bitcast(F32R), nmax[:, :, :]))
                        dve.tensor_tensor(qpad[:, :, :, 17].bitcast(F32R), nmax[:, :, :], qpad[:, :, :, 16], ALU.subtract)\
                           .then_inc(sem("m_pad"), 1)
                        for cc in range(2):
                            dve.wait_ge(sem("o_tp"), u * 2 + cc + 1)
                            dve.wait_ge(sem("att"), u * 2 + cc)
                            o = TP[cc].rearrange("p (t h d) -> p t h d", t=CT, h=4)
                            ch.link(dve.reciprocal(rec[:, :, :], o[:, :, :, 16]))
                            dve.tensor_tensor(
                                att[:, cc * CT:(cc + 1) * CT, bass.ds(qd * 64, 64)].rearrange("p t (h d) -> p t h d", h=4),
                                o[:, :, :, 0:DA], rec[:, :, :].rearrange("p t (h d) -> p t h d", d=1).broadcast_to([P, CT, 4, DA]),
                                ALU.mult).then_inc(sem("att"), 1)
                        assert ch.k == PER_Q, ch.k
                    for a in range(2):
                        for r in range(2):
                            dve.wait_ge(sem("att_hi"), b * 4 + a * 2 + r + 1)
                            dve.tensor_tensor(xTl1[:, r, :], TP[r], xTh1[:, r, :].bitcast(F32), ALU.subtract).then_inc(sem("att_lo"), 1)
                        if a == 0:
                            dve.wait_ge(sem("bias_added"), b + 1)
                        for t in range(CT):
                            xt = X[:, b * TB + a * CT + t, :]
                            dve.wait_ge(sem("oproj_mm"), b * TB + a * CT + t + 1)
                            dve.tensor_tensor(xt, xt, ps[:, 6 + t % 2, 0:E], ALU.add).then_inc(sem("x_updated"), 1)
                        dve.wait_ge(sem("x_updated"), b * TB + (a + 1) * CT)
                        ch.at(base + b * PER_B + 2 * LN_LINKS + 1 + QUADS * PER_Q + a * LN_LINKS)
                        moments(b * 2 + a)
                base += 2 * PER_B
                dve.wait_ge(sem("x_updated"), TILES)

            def ffn(f, chain, updated, moments_too):
                n0 = CHUNKS + f * (CHUNKS + 1)

                def split_chunk(n, buf):
                    for r in range(2):
                        dve.wait_ge(sem("xT_hi"), 2 * n + r + 1)
                        dve.tensor_tensor(xTl2[:, buf, r, :], TP[r], xTh2[:, buf, r, :].bitcast(F32), ALU.subtract)\
                           .then_inc(sem("xT_lo"), 1)

                normalise(n0, 0)
                split_chunk(n0, 0)
                with dve.Fori(0, CHUNKS // 2) as i:
                    ch.at(chain + i * (2 * LN_LINKS))
                    g = (i + f * 2) * 2 * NT

                    def residual(k):
                        for m in range(2):
                            dve.wait_ge(sem("y_tp"), ((i + f * 2) * 2 + k) * 2 + m + 1)
                            xt = X[:, bass.ds(i * 2 * CT + (k * CT + 2 * m), 2), :]
                            dve.tensor_tensor(xt, xt, TP[m].rearrange("p (t e) -> p t e", t=2), ALU.add).then_inc(sem("x_updated"), 1)

                    for st in range(2 * NT):
                        k, t = divmod(st, NT)
                        dve.wait_ge(sem("gelu"), g + st + 1)
                        dve.wait_ge(sem("up_mm"), g + st + 1)
                        dve.tensor_tensor(prod[:, st % 2, :], gel[:, st % 2, :], ps[:, 4 + st % 2, :], ALU.mult)\
                           .then_inc(sem("prod"), 1)
                        dve.wait_ge(sem("in_hi"), g + st + 1)
                        dve.tensor_tensor(inl[:, st % 3, :], prod[:, st % 2, :], inh[:, st % 3, :].bitcast(F32), ALU.subtract)\
                           .then_inc(sem("in_lo"), 1)
                        if st == NT + 3:
                            residual(0)
                        if moments_too and st == NT + 4:
                            dve.wait_ge(sem("x_updated"), updated + i * 4 + 2)
                            moments(i * 2)
                        if t == FFN_NORM:
                            dve.wait_ge(sem("x_updated"), updated + i * 4 + 2 * k)
                            normalise(2 * i + (n0 + k + 1), (i * 2 + (k + 1)) % CHUNKS)
                        if t == FFN_SPLIT:
                            split_chunk(2 * i + (n0 + k + 1), 1 - k)
                    residual(1)
                    dve.wait_ge(sem("x_updated"), updated + i * 4 + 4)
                    if moments_too:
                        moments(i * 2 + 1)

            if stop >= 2:
                ffn(0, base, TILES, True)
                base += CHUNKS * LN_LINKS

            if stop >= 3:
                dve.wait_ge(sem("tab_in"), 96)
                ch.at(base)
                cs = [tabs[:, n, :, 0:64] for n in range(2)]
                ws = [vb[:, 0, n * DB:(n + 1) * DB].rearrange("p (a d) -> p a d", a=1) for n in range(2)]
                for n in (1, 0):
                    w1, w2 = (ws[n][:, :, k * 64:(k + 1) * 64].broadcast_to([P, TB, 64]) for k in range(2))
                    co, si = tabs[:, 0, :, 0:64], tabs[:, 0, :, 64:128]
                    A, Bt = tabs[:, 2 * n, :, :], tabs[:, 2 * n + 1, :, :]
                    if n == 0:
                        co, si = tabs[:, 1, :, 0:64], tabs[:, 1, :, 64:128]
                    ch.link(dve.tensor_tensor(A[:, :, 0:64], co, w1, ALU.mult))
                    ch.link(dve.tensor_tensor(A[:, :, 64:128], co, w2, ALU.mult))
                    ch.link(dve.scalar_tensor_tensor(out=Bt[:, :, 0:64], in0=si, scalar=-1.0, in1=w2, op0=ALU.mult, op1=ALU.mult))
                    ch.link(dve.tensor_tensor(Bt[:, :, 64:128], si, w1, ALU.mult))
                dve.memset(kTb[:, 1, :, :], 0.0)
                ch.link(dve.memset(vb[:, :, :], 0.0))
                dve.memset(X[:, TILES, :], 0.0)
                dve.memset(oT[:, :, :], 0.0)
                dve.memset(prb[:, 1, :, :], 0.0).then_inc(sem("tables"), 1)
                base += 9
                PER_K = 2 + 1 + RSQRT_LINKS
                PER_M = PER_K + 2 * 2 + 1 + RSQRT_LINKS
                PER_C = CT * (PER_M + 1 + 4) + LN_LINKS

                def token_tile(m, x, par):
                    dve.wait_ge(sem("xn1_tp"), m - 1 if not isinstance(m, int) else max(0, m - 1))
                    dve.tensor_scalar(xn[:, par, :], X[:, x, :], mean[:, bass.ds(x, 1)], rstd[:, bass.ds(x, 1)],
                                      ALU.subtract, ALU.mult).then_inc(sem("xn1_ready"), 1)

                def squares(m, n):
                    dve.wait_ge(sem("proj_out"), m * 6 + n + 1)
                    dve.tensor_reduce(ssb[:, 16:20] if n == 0 else ssb[:, 4 * n - 4:4 * n],
                                      sqb[:, n % 2, :].rearrange("p (h d) -> p h d", h=4), AX.X, ALU.add)\
                       .then_inc(sem("ss"), 1)

                def table(n, x, h, lo, hi):
                    return tabs[:, n, x, lo:hi].rearrange("p (a d) -> p a d", a=1).broadcast_to([P, h, hi - lo])

                def rope(x, h0, h1, n):
                    q, o, h = qk[:, h0:h1, :], rot[:, h0:h1, :], h1 - h0
                    dve.tensor_tensor(o[:, :, 0:64], q[:, :, 64:128], table(n + 1, x, h, 0, 64), ALU.mult)
                    ch.link(dve.tensor_tensor(o[:, :, 64:128], q[:, :, 0:64], table(n + 1, x, h, 64, 128), ALU.mult))
                    ch.link(dve.tensor_tensor(q, q, table(n, x, h, 0, DB), ALU.mult))
                    return dve.tensor_tensor(q, q, o, ALU.add)

                def rope_k(x):
                    ch.link(rope(x, HB, 20, 2))

                def rope_q(x, half):
                    rope(x, 8 * half, 8 * half + 8, 0).then_inc(sem("qk_final"), 1)

                def norm_k(m):
                    dve.wait_ge(sem("ss"), m * 5 + 1)
                    ch.link(dve.tensor_scalar(ssb[:, HB:20], ssb[:, HB:20], 1.0 / DB, RMS_EPS, ALU.mult, ALU.add))
                    rsqrt(rk[:, :], ssb[:, HB:20], rqt[:, 0:KVB])
                    q = qk[:, HB:20, :]
                    r = rk[:, :].rearrange("p (h d) -> p h d", d=1).broadcast_to([P, KVB, DB])
                    dve.tensor_tensor(q, q, r, ALU.mult).then_inc(sem("qk_final"), 1)

                def norm_q(m, par):
                    dve.wait_ge(sem("ss"), m * 5 + 5)
                    ch.link(dve.tensor_scalar(ssb[:, 0:HB], ssb[:, 0:HB], RMS_EPS * DB, None, ALU.add))
                    rsqrt(rq[:, par, :], ssb[:, 0:HB], rqt[:, :])

                def prob_half(k):
                    dve.wait_ge(sem("p_tp"), k * 2 + 2)
                    dve.wait_ge(sem("pvb"), k)
                    dve.tensor_copy(PT[:, 1, :], TP[1]).then_inc(sem("PT1"), 1)

                def residual(t, x):
                    dve.wait_ge(sem("wo_mm"), t * 4 + 2)
                    xt = X[:, x, :]
                    dve.tensor_tensor(xt, xt, ps[:, 7, 0:E], ALU.add).then_inc(sem("x_updated"), 1)

                ch.at(base)
                token_tile(0, 0, 0)
                token_tile(1, 1, 1)
                for n in range(5):
                    squares(0, n)
                rope_k(0)
                norm_k(0)
                rope_q(0, 0)
                rope_q(0, 1)
                norm_q(0, 0)
                assert ch.k == PER_M + 1, ch.k
                base += ch.k
                with dve.Fori(0, CHUNKS) as c:
                    ch.at(base + c * PER_C)
                    for u in range(CT):
                        t = c * CT + u
                        m = c * CT + (u + 1)
                        x = m % TB

                        def maxima(g):
                            dve.wait_ge(sem("sb_mm"), t * 4 + g + 1)
                            ch.link(dve.tensor_reduce(nmx[:, :], ps[:, 4:6, :].rearrange("p a (h k) -> p (a h) k", h=2),
                                                      AX.X, ALU.max, negate=True))
                            dve.wait_ge(sem("expb"), 4 * (t * 4 + max(0, g - 1)))
                            dve.tensor_tensor(nmb[:, g % 2, :], nmx[:, :], rq[:, u % 2, 4 * g:4 * g + 4], ALU.mult)\
                               .then_inc(sem("nmb"), 1)

                        def sums(g):
                            dve.wait_ge(sem("expb"), 4 * (t * 4 + g + 1))
                            dve.wait_ge(sem("p_final"), t * 4 + max(0, g - 1))
                            dve.reciprocal(rcb[:, g % 2, :], rsb[:, g % 2, :]).then_inc(sem("rcb"), 1)

                        maxima(0)
                        prob_half(t * 4)
                        sums(0)
                        token_tile(c * CT + (u + 2), (c * CT + (u + 2)) % TILES, u % 2)
                        if u == 1:
                            dve.wait_ge(sem("x_updated"), c * CT + (DONE_F + 1))
                            moments((c + (CHUNKS - 1)) % CHUNKS)
                        squares(m, 0)
                        rope_k(x)
                        maxima(1)
                        prob_half(t * 4 + 1)
                        squares(m, 1)
                        sums(1)
                        residual(t, (t + TILES) % (TILES + 1))
                        norm_k(m)
                        squares(m, 2)
                        rope_q(x, 0)
                        maxima(2)
                        squares(m, 3)
                        prob_half(t * 4 + 2)
                        sums(2)
                        squares(m, 4)
                        rope_q(x, 1)
                        maxima(3)
                        prob_half(t * 4 + 3)
                        sums(3)
                        norm_q(m, (u + 1) % 2)
                    assert ch.k == PER_C, (ch.k, PER_C)
                base += CHUNKS * PER_C
                prob_half(4 * TILES)
                residual(TILES, TILES - 1)
                dve.wait_ge(sem("x_updated"), DONE_B)
                ch.at(base)
                moments(CHUNKS - 1)
                base += LN_LINKS
            if stop >= 4:
                ffn(1, base, DONE_B, False)

        @block.tensor
        def _(pe):
            def tp(o, i, parts=P):
                return pe.transpose(o, i, ident[:, :])

            pe.wait_ge(sem("pool"), 2)
            for u, (i, nib, j) in enumerate(W_UNITS):
                pe.wait_ge(sem("deq"), u + 1)
                for k in (2 * j, 2 * j + 1):
                    n = 2 * u + k - 2 * j
                    if n >= 4:
                        pe.wait_ge(sem("lo_ready"), n - 3)
                    for m in range(4):
                        if i < 2:
                            c0 = (4 * (k - 2 * j) + m) * P
                        else:
                            t2, hh = 2 * k + m // 2, m % 2
                            c0 = hh * 512 + (t2 - 4 * j) * P
                        last = tp(ps[:, n % 4, m * P:(m + 1) * P], deq[:, u % 2, c0:c0 + P])
                    last.then_inc(sem("w_tp"), 1)
                for q in range(4 * u, min(4 * u + 4, 20)):
                    n = WB_ORDER[q]
                    if n == 0:
                        pe.wait_ge(sem("wq_in"), 16)
                    if n == 8:
                        pe.wait_ge(sem("wkv_in"), 32)
                    if n == 12:
                        pe.wait_ge(sem("wo_in"), 16)
                    if q >= 4:
                        pe.wait_ge(sem("wb_ready"), q - 3)
                    for k in range(4):
                        if n < 8:
                            r, h = n // 4, (n % 4) * 4 + k
                            src = wqr[:, h, r::2]
                        elif n < 12:
                            r, m = divmod(n - 8, 2)
                            src = wkvr[:, m, k, r::2]
                        else:
                            h, m = (n - 12) * 2 + k // 2, k % 2
                            src = wor[:, m, h, :]
                        last = tp(ps[:, 4 + q % 4, k * P:(k + 1) * P], src)
                    last.then_inc(sem("wb_tp"), 1)
            pe.wait_ge(sem("pool"), POOL_CONST)

            def transpose_x(n, ready, count):
                pe.wait_ge(sem("ln_ready"), n + 1)
                for r in range(2):
                    for t in range(CT):
                        last = tp(TP[r][:, t * P:(t + 1) * P], xn[:, t, r::2])
                    last.then_inc(sem("xn_tp"), 1)

            def split_mm(o, lh, ll, rh, rl, start, stop):
                pe.matmul(o, ll, rh, start=start, stop=False)
                pe.matmul(o, lh, rl, start=False, stop=False)
                return pe.matmul(o, lh, rh, start=False, stop=stop)

            if stop >= 1:
                pe.wait_ge(sem("wa_lo"), 2)
                with pe.Fori(0, B) as b:
                    for a in range(2):
                        cn = b * 2 + a
                        if a == 0:
                            pe.wait_ge(sem("lo_ready"), 24)
                            pe.wait_ge(sem("att_lo"), b * 4)
                        transpose_x(cn, None, None)
                        pe.wait_ge(sem("xT_lo"), 2 * cn + 2)
                        for t in range(CT):
                            if a == 0 and t < 2:
                                pe.wait_ge(sem("x_updated"), b * TB)
                            else:
                                pe.wait_ge(sem("qkv_ready"), cn * CT + t - 1)
                            tt = slice(t * P, (t + 1) * P)
                            for r in range(2):
                                last = split_mm(ps[:, 6 + t % 2, 0:QKV], xTh1[:, r, tt], xTl1[:, r, tt],
                                                wah[:, r, :], wal[:, r, :], r == 0, r == 1)
                            last.then_inc(sem("qkv_mm"), 1)
                    pe.wait_ge(sem("kv_pad"), b + 1)
                    for h in range(2):
                        for t in range(4):
                            last = tp(TP[h][:, t * P:(t + 1) * P], kpad[:, h * 4 + t, :])
                        last.then_inc(sem("k_tp"), 1)
                    with pe.Fori(0, QUADS) as qd:
                        u = b * QUADS + qd
                        pe.wait_ge(sem("q_pad"), u + 1)
                        pe.wait_ge(sem("att"), u * 2)
                        for i in range(TB):
                            if i < 2:
                                pe.wait_ge(sem("k_ready"), b * 2 + 2)
                            else:
                                pe.wait_ge(sem("q_ready"), u * 2 * TB + i - 1)
                            for h in range(4):
                                last = tp(TP[i % 2][:, h * P:(h + 1) * P], qpad[:, i, h, :])
                            last.then_inc(sem("q_tp"), 1)
                        for n, (i, h0, nh) in enumerate(MAXES):
                            bank = 2 + 2 * (n % 2)
                            if n < 2:
                                pe.wait_ge(sem("q_ready"), u * 2 * TB + TB)
                            else:
                                pe.wait_ge(sem("maxed"), u * len(MAXES) + n - 1)
                            qs = slice(i * P, (i + 1) * P)
                            if n < 2:
                                pe.wait_ge(sem("exp"), u * EXPS)
                            for h in range(h0, h0 + nh):
                                for k0 in range(0, (i + 1) * P, C):
                                    k1 = min((i + 1) * P, k0 + C)
                                    bk = ps[:, bank + (h - h0) + k0 // C, :]
                                    diag = k1 == (i + 1) * P
                                    last = pe.matmul(bk[:, 0:k1 - k0], qTa[:, h, qs], kTa[:, k0:k1], start=True, stop=True)
                                    if diag:
                                        last = pe.matmul(bk[:, k1 - k0 - P:k1 - k0], identb[:, :], causal[:, :],
                                                         start=False, stop=True, skip_group_check=True)
                            last.then_inc(sem("s_mm"), 1)
                        pe.wait_ge(sem("m_pad"), u + 1)
                        for i in range(TB):
                            if i >= 2:
                                pe.wait_ge(sem("q_ready"), u * 2 * TB + TB + i - 1)
                            for h in range(4):
                                last = tp(TP[i % 2][0:32, h * P:(h + 1) * P], qpad[:, i, h, 0:32])
                            last.then_inc(sem("q_tp"), 1)
                        pe.wait_ge(sem("q_ready"), (u + 1) * 2 * TB)

                        def pv(step):
                            cc, j = (0, step) if step < CT else (1, step - CT)
                            w0 = P * max(0, j - CT * cc)
                            pe.wait_ge(sem("exp"), u * EXPS + 2 * step + 2)
                            if j == 0:
                                pe.wait_ge(sem("o_ready"), u * 2 + (cc if cc == 0 else 0))
                            for h in range(4):
                                last = pe.matmul(ps[32 * h:32 * h + 32, 6 + cc, w0:C], vpad[:, j, :],
                                                 prob[:, step % 2, h, 0:C - w0], start=j == 0, stop=j >= CT * cc,
                                                 skip_group_check=True)
                            last.then_inc(sem("pv"), 1)

                        def transpose_o(cc):
                            pe.wait_ge(sem("o_ready"), u * 2 + cc + 1)
                            for t in range(CT):
                                last = tp(TP[cc][:, t * P:(t + 1) * P], OT[:, t * P:(t + 1) * P])
                            last.then_inc(sem("o_tp"), 1)

                        for step in range(STEPS):
                            cc, j = (0, step) if step < CT else (1, step - CT)
                            w0 = P * max(0, j - CT * cc)
                            for v in range(2):
                                n = 2 * step + v
                                if n >= 2:
                                    pe.wait_ge(sem("exp"), u * EXPS + n - 1)
                                for h in range(2):
                                    bk = ps[:, 2 + 2 * (n % 2) + h, 0:C - w0]
                                    diag = j >= CT * cc
                                    last = pe.matmul(bk, kTa[:, j * P:(j + 1) * P], qTa[:, 2 * v + h, cc * C + w0:(cc + 1) * C],
                                                     start=True, stop=True)
                                    if diag:
                                        last = pe.matmul(bk[:, 0:P], identb[:, :], causalT[:, :], start=False, stop=True,
                                                         skip_group_check=True)
                                last.then_inc(sem("sT_mm"), 1)
                            if step >= 1:
                                pv(step - 1)
                            if step == CT + 1:
                                transpose_o(0)
                        pv(STEPS - 1)
                        transpose_o(1)
                    pe.wait_ge(sem("att"), (b + 1) * QUADS * 2)
                    for a in range(2):
                        if a == 1:
                            pe.wait_ge(sem("att_lo"), b * 4 + 2)
                        for r in range(2):
                            for t in range(CT):
                                last = tp(TP[r][:, t * P:(t + 1) * P], att[:, a * CT + t, r::2])
                            last.then_inc(sem("att_tp"), 1)
                        pe.wait_ge(sem("att_lo"), b * 4 + a * 2 + 2)
                        for t in range(CT):
                            n = a * CT + t
                            if n >= 2:
                                pe.wait_ge(sem("x_updated"), b * TB + n - 1)
                            tt = slice(t * P, (t + 1) * P)
                            for r in range(2):
                                last = split_mm(ps[:, 6 + t % 2, 0:E], xTh1[:, r, tt], xTl1[:, r, tt],
                                                woah[:, r, :], woal[:, r, :], r == 0, r == 1)
                            last.then_inc(sem("oproj_mm"), 1)

            def ffn(f, updated):
                n0 = CHUNKS + f * (CHUNKS + 1)
                transpose_x(n0, None, None)
                with pe.Fori(0, CHUNKS // 2) as i:
                    g = (i + f * 2) * 2 * NT

                    def hidden(w_h, w_l, bank, k, t):
                        ts = slice(t * P, (t + 1) * P)
                        for r in range(2):
                            last = split_mm(ps[:, bank, :], w_h[:, r, ts], w_l[:, r, ts], xTh2[:, k, r, :], xTl2[:, k, r, :],
                                            r == 0, r == 1)
                        return last

                    def down(st):
                        k, t = divmod(st, NT)
                        pe.wait_ge(sem("in_lo"), g + st + 1)
                        if t == 0:
                            pe.wait_ge(sem("y_ready"), (i + f * 2) * 2 + k)
                        for hh in range(2):
                            hs = slice(hh * P, (hh + 1) * P)
                            last = split_mm(ps[:, 6 + hh, :], wdh[:, t, hs], wdl[:, t, hs], inh[:, st % 3, :], inl[:, st % 3, :],
                                            t == 0, t == NT - 1)
                        last.then_inc(sem("down_mm"), 1)

                    def output(k):
                        pe.wait_ge(sem("y_ready"), (i + f * 2) * 2 + k + 1)
                        pe.wait_ge(sem("xT_lo"), (2 * i + (n0 + 1 + k)) * 2)
                        for m in range(2):
                            for q in range(4):
                                t, hh = 2 * m + q // 2, q % 2
                                last = tp(TP[m][:, q * P:(q + 1) * P], yT[:, hh, t * P:(t + 1) * P])
                            last.then_inc(sem("y_tp"), 1)

                    for st in range(2 * NT + 2):
                        k, t = divmod(st, NT)
                        if st < 2 * NT:
                            if t == 0:
                                pe.wait_ge(sem("xT_lo"), (2 * i + (n0 + 1 + k)) * 2)
                            pe.wait_ge(sem("gelu"), g + max(0, st - 1))
                            hidden(wgh, wgl, 2 + st % 2, k, t).then_inc(sem("gate_mm"), 1)
                            pe.wait_ge(sem("prod"), g + max(0, st - 1))
                            hidden(wuh, wul, 4 + st % 2, k, t).then_inc(sem("up_mm"), 1)
                        if st >= 2:
                            down(st - 2)
                        if st == NT + 2:
                            output(0)
                        if st < 2 * NT and t == FFN_TP:
                            pe.wait_ge(sem("x_updated"), updated + i * 4 + 2 * k)
                            transpose_x(2 * i + (n0 + 1 + k), None, None)
                    pe.wait_ge(sem("xT_lo"), (2 * i + (n0 + 3)) * 2)
                    output(1)

            if stop >= 2:
                pe.wait_ge(sem("x_updated"), TILES)
                ffn(0, TILES)
            if stop >= 3:
                pe.wait_ge(sem("tables"), 1)
                pe.wait_ge(sem("wb_back"), 16)
                def tokens(m, par):
                    pe.wait_ge(sem("xn1_ready"), m + 1)
                    for r in range(2):
                        last = tp(TP[0][:, r * P:(r + 1) * P], xn[:, par, r::2])
                    last.then_inc(sem("xn1_tp"), 1)

                def project(j, n, par, bank):
                    pe.wait_ge(sem("proj_out"), j - 1 if not isinstance(j, int) else max(0, j - 1))
                    w = wkvT[:, :, 0:C] if n == 0 else wkvT[:, :, C:2 * C] if n == 5 else wqT[:, :, (n - 1) * C:n * C]
                    for r in range(2):
                        last = pe.matmul(ps[:, 2 + bank, :], xT1[:, par, r, :], w[:, r, :], start=r == 0, stop=r == 1)
                    last.then_inc(sem("proj_mm"), 1)

                def transpose_qk(m, n):
                    pe.wait_ge(sem("qk_final"), m * 3 + (1, 2, 2, 3, 3)[n])
                    if n >= 2:
                        pe.wait_ge(sem("qkT"), m * 5 + n - 1)
                    for k in range(4):
                        h = HB + k if n == 0 else 4 * (n - 1) + k
                        last = tp(TP[n % 2][:, k * P:(k + 1) * P], qk[:, h, :])
                    last.then_inc(sem("qk_tp"), 1)

                def transpose_p(k, g, bank_read):
                    pe.wait_ge(sem("p_final"), k)
                    for kt in range(2):
                        s, v = bank_read[kt]
                        pe.wait_ge(sem(s), v)
                        for h in range(4):
                            last = tp(TP[kt][:, h * P:(h + 1) * P], prb[:, g % 2, h, kt * P:(kt + 1) * P])
                        last.then_inc(sem("p_tp"), 1)

                def values(k, g):
                    pe.wait_ge(sem("oT"), k)
                    for kt in range(2):
                        pe.wait_ge(sem("PT0" if kt == 0 else "PT1"), k + 1)
                        last = pe.matmul(ps[:, 6, :], vb[:, kt, g * DB:(g + 1) * DB], PT[:, kt, :], start=kt == 0, stop=kt == 1)
                    last.then_inc(sem("pvb"), 1)

                def wo_part(k, g, read=None):
                    pe.wait_ge(sem("oT"), k)
                    if g == 0:
                        pe.wait_ge(sem("x_updated"), read)
                    for h in range(4 * g, 4 * g + 4):
                        last = pe.matmul(ps[:, 7, 0:E], oT[:, h, :], woT[:, h, :], start=h == 0, stop=h == HB - 1,
                                         skip_group_check=True)
                    last.then_inc(sem("wo_mm"), 1)

                pe.wait_ge(sem("x_updated"), DONE_F)
                tokens(0, 0)
                pe.wait_ge(sem("xT1"), 1)
                for n in range(5):
                    project(n, n, 0, n % 2)
                tokens(1, 1)
                pe.wait_ge(sem("xT1"), 2)
                for n in range(5):
                    transpose_qk(0, n)
                with pe.Fori(0, CHUNKS) as c:
                    for u in range(CT):
                        t = c * CT + u
                        m = c * CT + (u + 1)
                        k = t * 4
                        nx = (u + 1) % 2

                        def scores(g):
                            pe.wait_ge(sem("qkT"), t * 5 + g + 2)
                            pe.wait_ge(sem("expb"), 4 * (k + g))
                            for h in range(4):
                                o = ps[:, 4 + h // 2, (h % 2) * E:(h % 2 + 1) * E]
                                pe.matmul(o.rearrange("p (a k) -> p a k", a=2), qTb[:, 4 * g + h, :], kTb[:, :, g, :],
                                          start=True, stop=False)
                                w = window[:, 2, :] if u % 2 else window[:, 0, :] if u else window[:, 1 - c % 2, :]
                                last = pe.matmul(o, identb[:, :], w, start=False, stop=True)
                            last.then_inc(sem("sb_mm"), 1)

                        def unit(j, n, par):
                            project(t * 6 + (5 + j), n, par, (j + 1) % 2)

                        scores(0)
                        transpose_p(k, 3, [("qkT", t * 5 + 5)] * 2)
                        wo_part(k, 2)
                        unit(0, 5, u % 2)
                        values(k, 3)
                        pe.wait_ge(sem("xT1"), c * CT + (u + 2))
                        unit(1, 0, nx)
                        unit(2, 1, nx)
                        scores(1)
                        transpose_p(k + 1, 0, [("PT0", k + 1), ("PT1", k + 1)])
                        wo_part(k + 1, 3)
                        unit(3, 2, nx)
                        values(k + 1, 0)
                        unit(4, 3, nx)
                        unit(5, 4, nx)
                        scores(2)
                        transpose_p(k + 2, 1, [("PT0", k + 2), ("PT1", k + 2)])
                        wo_part(k + 2, 0, t + (DONE_F + 1))
                        pe.wait_ge(sem("PT0"), k + 3)
                        tokens(c * CT + (u + 2), u % 2)
                        values(k + 2, 1)
                        scores(3)
                        transpose_p(k + 3, 2, [("xT1", c * CT + (u + 3)), ("PT1", k + 3)])
                        wo_part(k + 3, 1)
                        pe.wait_ge(sem("PT0"), k + 4)
                        transpose_qk(m, 0)
                        pe.wait_ge(sem("PT1"), k + 4)
                        transpose_qk(m, 1)
                        values(k + 3, 2)
                        for n in (2, 3, 4):
                            transpose_qk(m, n)
                k = 4 * TILES
                transpose_p(k, 3, [("qkT", TILES * 5 + 5)] * 2)
                wo_part(k, 2)
                values(k, 3)
                wo_part(k + 1, 3)
            if stop >= 4:
                pe.wait_ge(sem("wd_back"), 32)
                pe.wait_ge(sem("x_updated"), DONE_B)
                pe.wait_ge(sem("qkT"), (TILES + 1) * 5)
                ffn(1, DONE_B)

_ORDER = ["L0_attn_a_x", "L0_attn_a_Wq", "L0_attn_a_Wk", "L0_attn_a_Wv", "L0_attn_a_Wo", "L0_attn_a_bo",
          "L0_attn_b_wq", "L0_attn_b_wk", "L0_attn_b_wv", "L0_attn_b_wo", "L0_attn_b_q_norm_w", "L0_attn_b_k_norm_w",
          "L0_ffn_gate_W_packed", "L0_ffn_gate_scales", "L0_ffn_up_W_packed", "L0_ffn_up_scales",
          "L0_ffn_down_W_packed", "L0_ffn_down_scales"]


def kernel(**inputs):
    import numpy as np
    import concourse.bacc as bacc
    from concourse.bass_utils import run_bass_kernel_spmd

    nc = bacc.Bacc("TRN2", target_bir_lowering=False, num_devices=1)
    arrays, args = {}, []

    def put(name, a):
        arrays[name] = a
        args.append(nc.dram_tensor(name, a.shape, mybir.dt.from_np(a.dtype), kind="ExternalInput").ap())

    for name in _ORDER:
        put(name, np.ascontiguousarray(inputs[name]))
    freq = (1.0 / np.float32(10000.0) ** (np.arange(0, DB, 2, dtype=np.float32) / np.float32(DB))).astype(np.float32)
    angle = (np.arange(T, dtype=np.float32)[:, None] * freq[None, :]).astype(np.float32)
    put("rope_cos", np.cos(angle).astype(np.float32))
    put("rope_sin", np.sin(angle).astype(np.float32))
    out = nc.dram_tensor("out", (B, T, E), F32, kind="ExternalOutput").ap()
    build(nc, *args, out)
    r = run_bass_kernel_spmd(nc, [arrays], core_ids=[0])
    return r.results[0]["out"]
```

```python
import concourse.bass as bass
from concourse import mybir
from concourse.alu_op_type import AluOpType as ALU
from contextlib import ExitStack

F32 = mybir.dt.float32
F32R = mybir.dt.float32r
BF16 = mybir.dt.bfloat16
I32 = mybir.dt.int32
ACT = mybir.ActivationFunctionType
AX = mybir.AxisListType

P = 128
E = 256
B, T = 2, 1024
TILES = B * T // P
TB = T // P
CT = 4
CHUNKS = TILES // CT
C = CT * P
HA, DA = 16, 16
QKV = E + 2 * DA
QUADS = HA // 4
HB, KVB, DB = 16, 4, 128
MLP = 2048
NT = MLP // P
UNIT = MLP // 2
FROM = 1
FROM_ONE = ["y_tp", "pvb", "p_tp", "xn_tp", "qkv_mm", "expb", "p_final", "att_lo", "gelu", "prod", "y_ready", "oT",
            "x_updated", "nmb"]
BIG = -1.0e30
LN_EPS, RMS_EPS = 1e-5, 1e-6
RSQRT_SEED = float(0x5F3759DF)
POOL_CONST = 19
STEPS = CT + TB
EXPS = 2 * STEPS
MAXES = [(0, 0, 0, 4), (1, 0, 0, 2), (1, 0, 2, 2)] + [(i, 0, h, 1) for i in (2, 3) for h in range(4)]
MAXES += [(4, 0, h, 1) for h in range(4)] + [(4, 1, 0, 4)]
MAXES += [(5, 0, h, 1) for h in range(4)] + [(5, 1, 0, 2), (5, 1, 2, 2)]
MAXES += [(i, half, h, 1) for i in (6, 7) for half in range(2) for h in range(4)]


R1_AT, LEAD = 4, 1


def attention_plan():
    def maxima(q):
        items = [("T", q, 0), ("T", q, 1)] if q == 0 else []
        for i in range(TB):
            if 1 <= i < TB - 1:
                items.append(("T", q, i + 1))
            units = [("M", q, n) for n, m in enumerate(MAXES) if m[0] == i]
            if i == CT:
                units.insert(2, ("R", q, 0))
            if q + 1 < QUADS:
                if i == TB - 2:
                    units.insert(5, ("P", q + 1, 0))
                if i == TB - 1:
                    units.insert(2, ("T", q + 1, 0))
                    units.insert(5, ("T", q + 1, 1))
            items += units
            if i in (CT - 1, TB - 1):
                items.append(("F", q, i // CT))
        return items

    plan = maxima(0)
    for q in range(1, QUADS + 1):
        items = maxima(q) if q < QUADS else []
        widths = [C - P * max(0, step - CT * (step >= CT) - CT * (step >= CT)) for step in range(STEPS) for v in range(2)]
        units, done = sum(i[0] == "M" for i in items), 0
        for n in range(EXPS):
            step, v = divmod(n, 2)
            plan.append(("S", q - 1, n))
            if n == 2 and q >= 2:
                plan.append(("O", q - 2, 1))
            if n == R1_AT:
                plan.append(("R", q - 1, 1))
            goal = LEAD + units * sum(widths[:n + 1]) / sum(widths)
            while items and (done < goal - 1e-9 or n == EXPS - 1):
                done += items[0][0] == "M"
                plan.append(items.pop(0))
            if v == 1 and step >= 1:
                plan.append(("V", q - 1, step - 1))
                if step == CT:
                    plan.append(("C", q - 1, 0))
                if step == CT + 2:
                    plan.append(("O", q - 1, 0))
        plan += [("V", q - 1, STEPS - 1), ("C", q - 1, 1)]
    plan.append(("O", QUADS - 1, 1))
    return plan


PLAN = attention_plan()


FFN_NORM, FFN_TP, FFN_SPLIT = 7, 9, 10
RSQRT_LINKS = 2 + 3 * 3
DONE_A = TILES
DONE_F = DONE_A + 2 * CHUNKS
DONE_B = DONE_F + TILES + 1


class Chain:

    def __init__(self, eng, sem):
        self.eng, self.sem, self.base, self.k = eng, sem, 0, 0

    def at(self, base):
        self.base, self.k = base, 0

    def link(self, ins):
        self.k += 1
        ins.then_inc(self.sem, 1)
        self.eng.wait_ge(self.sem, self.base + self.k)


def build(nc, x, Wq, Wk, Wv, Wo, bo, wq, wk, wv, wo, qw, kw, gW, gS, uW, uS, dW, dS, cos, sin, out):
    ctx = ExitStack()
    with ctx:
        def sb(name, shape, dt, stack=ctx):
            return stack.enter_context(nc.sbuf_tensor(name, shape, dt))

        sems = {}

        def sem(name):
            if name not in sems:
                sems[name] = ctx.enter_context(nc.semaphore(name))
            return sems[name]

        X = sb("X", [P, TILES + 1, E], F32)
        wgh = sb("wgh", [P, 2, MLP], F32R)
        s = ExitStack()
        wqTh = sb("wqTh", [P, 2, HB * DB], F32R, s)
        s.close()
        wgl = sb("wgl", [P, 2, MLP], F32R)
        s = ExitStack()
        wqr = sb("wqr", [P, HB, E], F32, s)
        wor = sb("wor", [P, 2, HB, P], F32, s)
        s.close()
        s = ExitStack()
        sb("up_high", [P, 2, MLP], F32R, s)
        wkvTh = sb("wkvTh", [P, 2, 2 * KVB * DB], F32R, s)
        xT1h = sb("xT1h", [P, 2, 2, P], F32R, s)
        xT1l = sb("xT1l", [P, 2, 2, P], F32R, s)
        s.close()
        wuh = sb("wuh", [P, 2, MLP], F32R)
        wul = sb("wul", [P, 2, MLP], F32R)
        ident = sb("ident", [P, P], F32)
        identr = sb("identr", [P, P], F32R)
        identb = sb("identb", [P, P], BF16)
        causal = sb("causal", [P, P], BF16)
        causalT = sb("causalT", [P, P], BF16)
        started = sb("started", [P, 16], BF16)
        window = sb("window", [P, 3, E], BF16)
        stats = sb("stats", [P, CT, 6], F32)
        mv = sb("mv", [P, CT, 2], F32)
        var = sb("var", [P, CT], F32)
        ryy = sb("ryy", [P, CT], F32)
        mean = sb("mean", [P, TILES], F32)
        rstd = sb("rstd", [P, TILES], F32)
        rtmp = sb("rtmp", [P, CT], F32)
        s = ExitStack()
        qm = sb("qm", [P, TB, 4, 32], F32R, s)
        s.close()
        xn = sb("xn", [P, CT, E], F32)
        s = ExitStack()
        raw = [sb(f"raw{i}", [P, MLP], I32, s) for i in range(2)]
        scl = [sb(f"scl{i}", [P, P], F32, s) for i in range(2)]
        s.close()
        s = ExitStack()
        wdh = sb("wdh", [P, NT, E], F32R, s)
        late = ExitStack()
        sb("before", [P, NT // 2, E], F32, late)
        kpad = sb("kpad", [P, TB, P], F32, late)
        OT = sb("OT", [P, C], F32, late)
        bob = sb("bob", [P, E], F32, late)
        late.close()
        wdl = sb("wdl", [P, NT, E], F32R, s)
        mid = ExitStack()
        late = ExitStack()
        wkvr = sb("wkvr", [P, 2, KVB, E], F32, late)
        late.close()
        raw.append(sb("raw2", [P, MLP], I32, mid))
        mag = sb("mag", [P, 2, UNIT], I32, mid)
        sgn = sb("sgn", [P, 2, UNIT], F32, mid)
        val = sb("val", [P, 2, UNIT], F32, mid)
        deq = sb("deq", [P, 2, UNIT], F32, mid)
        scl.append(sb("scl2", [P, P], F32, mid))
        late = ExitStack()
        wTs = sb("wTs", [P, 10240], F32, late)
        late.close()
        sa = sb("sa", [P, 2, QKV], F32, mid)
        so = sb("so", [P, 2, E], F32, mid)
        mid.close()
        mid = ExitStack()
        wah = sb("wah", [P, 2, QKV], F32R, mid)
        wal = sb("wal", [P, 2, QKV], F32R, mid)
        woah = sb("woah", [P, 2, E], F32R, mid)
        woal = sb("woal", [P, 2, E], F32R, mid)
        qkv = sb("qkv", [P, TB, QKV], F32, mid)
        qpad = sb("qpad", [P, TB, 4, P], F32R, mid)
        qTa = sb("qTa", [P, 2, 4, T], F32R, mid)
        kTa = sb("kTa", [P, T], F32R, mid)
        vpad = sb("vpad", [P, TB, 32], F32, mid)
        nmax = sb("nmax", [P, TB, 2, 4], F32, mid)
        rec = sb("rec", [P, CT, 4], F32, mid)
        both = ExitStack()
        prob = sb("prob", [P, 2, 4, C], F32, both)
        both.close()
        xTh1 = sb("xTh1", [P, 2, C], F32R, mid)
        xTl1 = sb("xTl1", [P, 2, C], F32R, mid)
        mid.close()
        s2 = ExitStack()
        wqTl = sb("wqTl", [P, 2, HB * DB], F32R, s2)
        wkvTl = sb("wkvTl", [P, 2, 2 * KVB * DB], F32R, s2)
        s2.close()
        s2 = ExitStack()
        wTb = sb("wTb", [P, 10240], F32, s2)
        mid = ExitStack()
        xTh2 = sb("xTh2", [P, 2, 2, C], F32R, mid)
        xTl2 = sb("xTl2", [P, 2, 2, C], F32R, mid)
        gel = sb("gel", [P, 2, C], F32, mid)
        prod = sb("prod", [P, 2, C], F32, mid)
        inh = sb("inh", [P, 3, C], F32R, mid)
        inl = sb("inl", [P, 3, C], F32R, mid)
        yT = sb("yT", [P, 2, C], F32, mid)
        mid.close()
        mid = ExitStack()
        qk = sb("qk", [P, 20, DB], F32, mid)
        rot = sb("rot", [P, 20, DB], F32, mid)
        qTb = sb("qTb", [P, HB, P], F32, mid)
        kTb = sb("kTb", [P, 2, KVB, P], F32, mid)
        prb = sb("prb", [P, 2, 4, E], F32, mid)
        sqb = sb("sqb", [P, 2, C], F32, mid)
        ssb = sb("ssb", [P, 20], F32, mid)
        rq = sb("rq", [P, 2, HB], F32, mid)
        rk = sb("rk", [P, KVB], F32, mid)
        rqt = sb("rqt", [P, HB], F32, mid)
        nmx = sb("nmx", [P, 4], F32, mid)
        first = sb("first", [P, E], BF16, mid)
        nmb = sb("nmb", [P, 2, 4], F32, mid)
        rsb = sb("rsb", [P, 2, 4], F32, mid)
        rcb = sb("rcb", [P, 2, 4], F32, mid)
        mid.close()
        s2.close()
        s.close()
        mid = ExitStack()
        tabs = sb("tabs", [P, 4, TB, DB], F32, mid)
        PT = sb("PT", [P, 2, C], F32, mid)
        vb = sb("vb", [P, 2, C], F32, mid)
        oT = sb("oT", [P, HB, P], F32, mid)
        mid.close()

        wqT = wTb[:, 0:4096].rearrange("p (r n) -> p r n", r=2)
        wkvT = wTb[:, 4096:6144].rearrange("p (r n) -> p r n", r=2)

        def proj_weights(q, kv, n):
            return kv[:, :, 0:C] if n == 0 else kv[:, :, C:2 * C] if n == 5 else q[:, :, (n - 1) * C:n * C]

        woT = wTb[:, 6144:10240].rearrange("p (h n) -> p h n", h=HB)

        ps = ctx.enter_context(nc.psum_tensor("ps", [P, 8, 512], F32))
        TP = [ps[:, 0, :], ps[:, 1, :]]

        wb_keep = nc.dram_tensor("wb_keep", (P, 10240), F32, kind="Internal").ap()
        wlow_keep = nc.dram_tensor("wlow_keep", (P, 2, 2 * MLP), F32, kind="Internal").ap()
        wd_keep = nc.dram_tensor("wd_keep", (P, 2 * NT * E), F32, kind="Internal").ap()

        w_mats = [(wgh, wgl), (wuh, wul), (wdh, wdl)]

        def wb_slot(n):
            return wTs[:, n * 512:(n + 1) * 512]

        def w_slot(i, part, nib, k):
            m = w_mats[i][part]
            return m[:, nib, k * 512:(k + 1) * 512] if i < 2 else m[:, 4 * k + nib:4 * k + nib + 3:2, :]

        def w_psum(i, n):
            o = ps[:, n % 4, :]
            return o if i < 2 else o.rearrange("p (a e) -> p a e", a=2)

        W_UNITS = [(i, nib, j) for i in range(3) for nib in range(2) for j in range(2)]

        def packed(i, j):
            order = "p (j a c) -> p j a c" if i < 2 else "p (a j c) -> p j a c"
            return raw[i][:, :].rearrange(order, j=2, a=2)[:, j]

        def scales(i, j):
            order = "p (j a s) -> p j a s" if i < 2 else "p (a j s) -> p j a s"
            return scl[i][:, :].rearrange(order, j=2, a=2)[:, j]

        WB_ORDER = list(range(8)) + list(range(12, 20)) + list(range(8, 12))

        block = ctx.enter_context(nc.Block())

        @block.sync
        def _(sp):
            def packed_in(i, w, sc):
                sp.dma_start(raw[i][:, :].rearrange("p (t c) -> p t c", c=E),
                             w.rearrange("(t p r) c -> p t (r c)", p=P, r=2)).then_inc(sem(f"raw{i}_in"), 16)
                sp.dma_start(scl[i][:, :].rearrange("p (t c) -> p t c", c=16),
                             sc.rearrange("(t p r) c -> p t (r c)", p=P, r=2)).then_inc(sem(f"raw{i}_in"), 16)
            packed_in(0, gW, gS)
            sp.dma_start(wqr[:, :, :], wq.rearrange("(h p) k -> p h k", p=P)).then_inc(sem("wq_in"), 16)
            sp.dma_start(wor[:, :, :, :], wo.rearrange("(u p) (h d) -> p u h d", p=P, d=P)).then_inc(sem("wo_in"), 16)
            packed_in(1, uW, uS)
            sp.dma_start(wkvr[:, 0, :, :], wk.rearrange("(h p) k -> p h k", p=P)).then_inc(sem("wkv_in"), 16)
            sp.dma_start(wkvr[:, 1, :, :], wv.rearrange("(h p) k -> p h k", p=P)).then_inc(sem("wkv_in"), 16)
            sp.dma_start(X[:, 0:TILES, :], x.rearrange("b (t p) e -> p (b t) e", p=P)).then_inc(sem("x_in"), 16)
            sp.wait_ge(sem("wb_tp"), 20)
            sp.dma_start(raw[2][:, :].rearrange("p (u c) -> p u c", u=2),
                         dW.rearrange("(u p) c -> p u c", u=2)).then_inc(sem("raw2_in"), 16)
            sp.dma_start(scl[2][:, :].rearrange("p (u c) -> p u c", u=2),
                         dS.rearrange("(u p) c -> p u c", u=2)).then_inc(sem("raw2_in"), 16)
            sp.wait_ge(sem("wb_ready"), 20)
            sp.dma_start(wb_keep, wTs[:, :]).then_inc(sem("wb_kept"), 16)
            sp.wait_ge(sem("wb_kept"), 16)
            sp.dma_start(sa[:, :, 0:E], Wq.rearrange("(p r) n -> p r n", r=2)).then_inc(sem("wa_in"), 16)
            sp.dma_start(sa[:, :, E:E + DA], Wk.rearrange("(p r) n -> p r n", r=2)).then_inc(sem("wa_in"), 16)
            sp.dma_start(sa[:, :, E + DA:], Wv.rearrange("(p r) n -> p r n", r=2)).then_inc(sem("wa_in"), 16)
            sp.dma_start(so[:, :, :], Wo.rearrange("(p r) n -> p r n", r=2)).then_inc(sem("wa_in"), 16)
            sp.wait_ge(sem("lo_ready"), 24)
            sp.dma_start(wd_keep[:, NT * E:], wdl[:, :, :].rearrange("p a b -> p (a b)").bitcast(F32)).then_inc(sem("wdl_kept"), 16)
            sp.dma_start(wd_keep[:, 0:NT * E], wdh[:, :, :].rearrange("p a b -> p (a b)").bitcast(F32)).then_inc(sem("wd_kept"), 16)
            for i, m in enumerate((wgl, wul)):
                sp.dma_start(wlow_keep[:, i, :], m[:, :, :].rearrange("p a b -> p (a b)").bitcast(F32)).then_inc(sem("wlow_kept"), 16)
            sp.wait_ge(sem("wdl_kept"), 16)
            sp.dma_start(bob[:, :], bo.rearrange("(a n) -> a n", a=1).broadcast_to([P, E])).then_inc(sem("bo_in"), 16)
            sp.wait_ge(sem("x_updated"), FROM + DONE_A)
            sp.dma_start(wdl[:, NT // 2:, :].rearrange("p a b -> p (a b)").bitcast(F32),
                         wd_keep[:, NT * E + NT // 2 * E:]).then_inc(sem("wdl_back"), 16)
            sp.dma_start(wTb[:, :], wb_keep).then_inc(sem("wb_back"), 16)
            sp.wait_ge(sem("x_updated"), FROM + 16 + 2 * CHUNKS)
            for n in range(2):
                sp.dma_start(tabs[:, n, :, 0:64], cos.rearrange("(t p) d -> p t d", p=P)).then_inc(sem("tab_in"), 16)
                sp.dma_start(tabs[:, n, :, 64:128], sin.rearrange("(t p) d -> p t d", p=P)).then_inc(sem("tab_in"), 16)
            sp.dma_start(PT[:, 0, 0:DB], qw.rearrange("(a n) -> a n", a=1).broadcast_to([P, DB])).then_inc(sem("tab_in"), 16)
            sp.dma_start(PT[:, 0, DB:2 * DB], kw.rearrange("(a n) -> a n", a=1).broadcast_to([P, DB])).then_inc(sem("tab_in"), 16)
            sp.wait_ge(sem("proj_mm"), 5 + 6 * TILES)
            sp.wait_ge(sem("xT1l"), TILES + 2)
            for i, m in enumerate((wgl, wul)):
                sp.dma_start(m[:, :, :].rearrange("p a b -> p (a b)").bitcast(F32), wlow_keep[:, i, :]).then_inc(sem("wlow_again"), 16)
            sp.wait_ge(sem("wd_kept"), 16)
            sp.wait_ge(sem("qk_final"), 3 * (TILES + 1))
            sp.dma_start(wdh[:, :, :].rearrange("p a b -> p (a b)").bitcast(F32), wd_keep[:, 0:NT * E]).then_inc(sem("wdh_again"), 16)
            sp.wait_ge(sem("x_updated"), FROM + DONE_B)
            for q in range(4):
                w = NT // 4 * E
                sp.dma_start(wdl[:, q * NT // 4:(q + 1) * NT // 4, :].rearrange("p a b -> p (a b)").bitcast(F32),
                             wd_keep[:, NT * E + q * w:NT * E + (q + 1) * w]).then_inc(sem(f"wdl_again{q}"), 16)
            for c in range(CHUNKS):
                sp.wait_ge(sem("x_updated"), FROM + DONE_B + 2 * (c + 1))
                b, a = divmod(c, CHUNKS // B)
                sp.dma_start(out[b, a * C:(a + 1) * C, :].rearrange("(t p) e -> p t e", p=P),
                             X[:, c * CT:(c + 1) * CT, :]).then_inc(sem("out_written"), 16)
            sp.wait_ge(sem("out_written"), 16 * CHUNKS)

        @block.gpsimd
        def _(pool):
            def diagonal(m):
                pool.memset(m, 0.0).then_inc(sem("pool"), 1)
                pool.wait_ge(sem("pool"), diagonal.n + 1)
                pool.affine_select(out=m, in_=m, compare_op=ALU.not_equal, fill=1.0, base=0,
                                   pattern=[[-1, P]], channel_multiplier=1).then_inc(sem("pool"), 1)
                diagonal.n += 2
            diagonal.n = 0
            diagonal(ident[:, :])
            diagonal(identb[:, :])
            for n, name in enumerate(FROM_ONE):
                pool.memset(started[:, n:n + 1], 1.0).then_inc(sem(name), FROM)

            def mask(m, keep_where, base, step, per_partition):
                pool.memset(m, 0.0).then_inc(sem("pool"), 1)
                pool.wait_ge(sem("pool"), diagonal.n + 1)
                pool.affine_select(out=m, in_=m, compare_op=keep_where, fill=BIG, base=base,
                                   pattern=[[step, P]], channel_multiplier=per_partition).then_inc(sem("pool"), 1)
                diagonal.n += 2
            mask(causal[:, :], ALU.is_ge, 0, -1, 1)
            mask(causalT[:, :], ALU.is_ge, 0, 1, -1)
            mask(window[:, 0, 0:P], ALU.is_ge, 0, -1, 1)
            mask(window[:, 0, P:E], ALU.is_gt, 0, 1, -1)
            mask(window[:, 1, 0:P], ALU.is_ge, 0, -1, 1)
            pool.memset(window[:, 1, P:E], BIG).then_inc(sem("pool"), 1)
            diagonal.n += 1
            mask(window[:, 2, 0:P], ALU.is_gt, 0, 1, -1)
            mask(window[:, 2, P:E], ALU.is_ge, 0, -1, 1)
            assert diagonal.n == POOL_CONST
            for n, (i, nib, j) in enumerate(W_UNITS):
                if nib == 0 and j == 0:
                    pool.wait_ge(sem(f"raw{i}_in"), 32)
                pool.wait_ge(sem("sign"), n + 1)
                sg = sgn[:, n % 2, :].rearrange("p (a s k) -> p a s k", a=2, k=16)
                sc = scales(i, j).rearrange("p a (s k) -> p a s k", k=1).broadcast_to([P, 2, 32, 16])
                pool.tensor_tensor(sg, sg, sc, ALU.mult).then_inc(sem("scaled"), 1)
            pool.wait_ge(sem("lo_ready"), 24)
            pool.wait_ge(sem("wb_kept"), 16)
            one = ident[:, :].rearrange("p (a b k) -> p a b k", a=1, b=1).broadcast_to([P, TB, 4, P])
            pool.tensor_tensor(qpad[:, :, :, :], one, one, ALU.subtract)
            pool.memset(vpad[:, :, :], 0.0).then_inc(sem("pads"), 1)
            pool.wait_ge(sem("wdl_kept"), 16)
            pool.memset(kpad[:, :, :], 0.0).then_inc(sem("pads"), 1)
            pool.wait_ge(sem("pads"), 2)
            pool.memset(kpad[:, :, 16:18], 1.0)
            pool.memset(vpad[:, :, 16:17], 1.0).then_inc(sem("pads"), 1)
            pool.wait_ge(sem("bo_in"), 16)
            for b in range(B):
                pool.wait_ge(sem("ln_ready"), 2 * (b + 1))
                v = X[:, b * TB:(b + 1) * TB, :]
                pool.tensor_tensor(v, v, bob[:, :].rearrange("p (a e) -> p a e", a=1).broadcast_to([P, TB, E]),
                                   ALU.add).then_inc(sem("bias_added"), 1)
            pool.wait_ge(sem("wb_back"), 16)
            pool.wait_ge(sem("wlow_kept"), 32)
            pool.wait_ge(sem("gate_mm"), CHUNKS * NT)
            pool.wait_ge(sem("up_mm"), CHUNKS * NT)
            for n in range(6):
                pool.tensor_copy(proj_weights(wqTh, wkvTh, n), proj_weights(wqT, wkvT, n)).then_inc(sem("wp_hi"), 1)
            pool.wait_ge(sem("x_updated"), FROM + DONE_F)
            for m in (kTb[:, 1, :, :], vb[:, :, :], X[:, TILES, :], oT[:, :, :], prb[:, 1, :, :]):
                pool.memset(m, 0.0).then_inc(sem("blank"), 1)
            with pool.Fori(0, CHUNKS) as c:
                for k in range(4 * CT):
                    pool.wait_ge(sem("rcb"), c * 4 * CT + k + 1)
                    v = prb[:, k % 2, :, :]
                    pool.tensor_tensor(v, v, rcb[:, k % 2, :].rearrange("p (h d) -> p h d", d=1).broadcast_to([P, 4, E]),
                                       ALU.mult).then_inc(sem("p_final"), 1)

        @block.scalar
        def _(act):
            def copy(o, i, s):
                act.activation(o, i, ACT.Copy).then_inc(sem(s), 1)

            def decode(n):
                act.wait_ge(sem("codes"), 2 * n + 2)
                act.activation(sgn[:, n % 2, :], sgn[:, n % 2, :].bitcast(I32), ACT.Copy, bias=1.0, scale=-0.25)\
                   .then_inc(sem("sign"), 1)
                act.activation(val[:, n % 2, :], mag[:, n % 2, :], ACT.Copy, bias=-8.0, scale=2.0).then_inc(sem("val"), 1)

            decode(0)
            for u in range(len(W_UNITS)):
                i, nib, j = W_UNITS[u]
                if u + 1 < len(W_UNITS):
                    decode(u + 1)
                for k in (2 * j, 2 * j + 1):
                    n = 2 * u + k - 2 * j
                    act.wait_ge(sem("w_tp"), n + 1)
                    copy(w_slot(i, 0, nib, k), w_psum(i, n), "hi_ready")
                for n in range(4 * u, min(4 * u + 4, 20)):
                    act.wait_ge(sem("wb_tp"), n + 1)
                    copy(wb_slot(WB_ORDER[n]), ps[:, 4 + n % 4, :], "wb_ready")

            def split_x(n, hi):
                for r in range(2):
                    act.wait_ge(sem("xn_tp"), FROM + 2 * n + r + 1)
                    copy(hi[:, r, :], TP[r], "xT_hi")

            act.wait_ge(sem("wa_in"), 64)
            act.wait_ge(sem("lo_ready"), 24)
            copy(wah[:, :, :], sa[:, :, :], "wa_hi")
            copy(woah[:, :, :], so[:, :, :], "wa_hi")
            with act.Fori(0, B) as b:
                for a in range(2):
                    act_c = b * 2 + a
                    split_x(act_c, xTh1)
                    for t in range(CT):
                        act.wait_ge(sem("qkv_mm"), FROM + act_c * CT + t + 1)
                        copy(qkv[:, a * CT + t, :], ps[:, 6 + t % 2, 0:QKV], "qkv_ready")
                for h in range(2):
                    act.wait_ge(sem("k_tp"), b * 2 + h + 1)
                    copy(kTa[:, h * C:(h + 1) * C], TP[h], "k_ready")
                copies = b * QUADS * (TB + 2)
                n_copy = 0
                for kind, q, n in PLAN:
                    u = b * QUADS + q
                    if kind == "T":
                        n_copy += 1
                        act.wait_ge(sem("q_tp"), copies + n_copy)
                        copy(qTa[:, q % 2, :, n * P:(n + 1) * P], TP[0].rearrange("p (h q) -> p h q", h=4), "q_ready")
                    elif kind == "R":
                        n_copy += 1
                        act.wait_ge(sem("q_tp"), copies + n_copy)
                        for h in range(4):
                            last = act.activation(qTa[0:32, q % 2, h, n * C:(n + 1) * C], TP[0][32 * h:32 * h + 32, :], ACT.Copy)
                        last.then_inc(sem("q_ready"), 1)
                    elif kind == "S":
                        step, v = divmod(n, 2)
                        cc, j = (0, step) if step < CT else (1, step - CT)
                        w = C - P * max(0, j - CT * cc)
                        act.wait_ge(sem("sT_mm"), u * EXPS + n + 1)
                        if v == 0 and (q or step >= 2):
                            act.wait_ge(sem("pv"), u * STEPS + step - 1)
                        act.activation(prob[:, step % 2, 2 * v:2 * v + 2, 0:w], ps[:, 3 + 2 * v:5 + 2 * v, 0:w], ACT.Exp)\
                           .then_inc(sem("exp"), 1)
                    elif kind == "C":
                        act.wait_ge(sem("pv"), u * STEPS + (CT if n == 0 else STEPS))
                        if q or n:
                            act.wait_ge(sem("o_tp"), u * 2 + n)
                        copy(OT[:, :], ps[:, 7, :], "o_ready")
                for a in range(2):
                    for r in range(2):
                        act.wait_ge(sem("att_tp"), b * 4 + a * 2 + r + 1)
                        copy(xTh1[:, r, :], TP[r], "att_hi")

            def split_chunk(n, buf):
                for r in range(2):
                    act.wait_ge(sem("xn_tp"), FROM + 2 * n + r + 1)
                    copy(xTh2[:, buf, r, :], TP[r], "xT_hi")

            def ffn(f):
                n0 = CHUNKS + f * (CHUNKS + 1)
                split_chunk(n0, 0)
                with act.Fori(0, CHUNKS // 2) as i:
                    g = (i + f * 2) * 2 * NT
                    for st in range(2 * NT):
                        k, t = divmod(st, NT)
                        if st == NT + 2:
                            output(f, i, 0)
                        act.wait_ge(sem("gate_mm"), g + st + 1)
                        if st >= 2:
                            act.wait_ge(sem("prod"), FROM + g + st - 1)
                        act.activation(gel[:, st % 2, :], ps[:, 2 + st % 2, :], ACT.Gelu_apprx_tanh).then_inc(sem("gelu"), 1)
                        act.wait_ge(sem("prod"), FROM + g + st + 1)
                        if st >= 3:
                            act.wait_ge(sem("down_mm"), g + st - 2)
                        copy(inh[:, st % 3, :], prod[:, st % 2, :], "in_hi")
                        if t == FFN_SPLIT:
                            split_chunk(2 * i + (n0 + k + 1), 1 - k)
                    output(f, i, 1)

            def output(f, i, k):
                c = (i + f * 2) * 2 + k
                act.wait_ge(sem("down_mm"), (c + 1) * NT)
                act.wait_ge(sem("y_tp"), FROM + c * 2)
                copy(yT[:, :, :], ps[:, 6:8, :], "y_ready")

            ffn(0)
            def tokens(m, par):
                act.wait_ge(sem("xn1_tp"), m + 1)
                copy(xT1h[:, par, :, :], TP[0][:, 0:E].rearrange("p (r k) -> p r k", r=2), "xT1")

            def projected(j, m, n, bank, par=0):
                act.wait_ge(sem("proj_mm"), j + 1)
                src = ps[:, 2 + bank, :]
                if n == 5:
                    copy(vb[:, par, :], src, "proj_out")
                    return
                if n == 0:
                    act.wait_ge(sem("qk_tp"), m * 5)
                h = 4 * (n - 1) if n else HB
                act.activation(qk[:, h:h + 4, :], src.rearrange("p (h d) -> p h d", h=4), ACT.Copy)
                act.wait_ge(sem("ss"), m * 5 + max(0, n - 1))
                act.activation(sqb[:, n % 2, :], src, ACT.Square).then_inc(sem("proj_out"), 1)

            def transposed(m, n, par):
                act.wait_ge(sem("qk_tp"), m * 5 + n + 1)
                dst = kTb[:, par, :, :] if n == 0 else qTb[:, 4 * (n - 1):4 * n, :]
                copy(dst, TP[n % 2].rearrange("p (h q) -> p h q", h=4), "qkT")

            def prob_half(k):
                act.wait_ge(sem("p_tp"), FROM + k * 2 + 1)
                act.wait_ge(sem("pvb"), FROM + k)
                copy(PT[:, 0, :], TP[0], "PT0")

            def group_out(k, g):
                act.wait_ge(sem("pvb"), FROM + k + 1)
                copy(oT[:, 4 * g:4 * g + 4, :], ps[:, 6, :].rearrange("p (h q) -> p h q", h=4), "oT")

            tokens(0, 0)
            for n in range(5):
                projected(n, 0, n, n % 2)
            tokens(1, 1)
            for n in range(5):
                transposed(0, n, 0)
            with act.Fori(0, CHUNKS) as c:
                for u in range(CT):
                    t = c * CT + u
                    m = c * CT + (u + 1)
                    nx = (u + 1) % 2

                    def exps(g):
                        act.wait_ge(sem("nmb"), FROM + t * 4 + g + 1)
                        for h in range(4):
                            act.activation(prb[:, g % 2, h, :], prb[:, g % 2, h, :],
                                           ACT.Exp, bias=nmb[:, g % 2, h:h + 1], scale=-1.0,
                                           accum_out=rsb[:, g % 2, h:h + 1]).then_inc(sem("expb"), 1)

                    def project(j, n):
                        projected(t * 6 + (5 + j), m, n, (j + 1) % 2, u % 2)

                    def finish(g):
                        group_out(t * 4 + g, (g - 1) % 4)
                    prob_half(t * 4)
                    exps(0)
                    finish(0)
                    project(0, 5)
                    project(1, 0)
                    project(2, 1)
                    prob_half(t * 4 + 1)
                    exps(1)
                    project(3, 2)
                    finish(1)
                    project(4, 3)
                    prob_half(t * 4 + 2)
                    exps(2)
                    project(5, 4)
                    tokens(c * CT + (u + 2), u % 2)
                    finish(2)
                    prob_half(t * 4 + 3)
                    exps(3)
                    transposed(m, 0, nx)
                    transposed(m, 1, nx)
                    finish(3)
                    for n in (2, 3, 4):
                        transposed(m, n, nx)
            prob_half(4 * TILES)
            group_out(4 * TILES, 3)
            ffn(1)

        @block.vector
        def _(dve):
            ch = Chain(dve, sem("dve"))

            def rsqrt(y, v, t, out=None):
                ch.link(dve.tensor_scalar(t.bitcast(I32), v.bitcast(I32), 1, None, ALU.logical_shift_right))
                ch.link(dve.tensor_scalar(y.bitcast(I32), t.bitcast(I32), -1.0, RSQRT_SEED, ALU.mult, ALU.add))
                for n in range(3):
                    ch.link(dve.tensor_tensor(t, y, y, ALU.mult))
                    ch.link(dve.scalar_tensor_tensor(out=t, in0=t, scalar=-0.5, in1=v, op0=ALU.mult, op1=ALU.mult))
                    ch.link(dve.scalar_tensor_tensor(out=out if n == 2 and out is not None else y,
                                                     in0=t, scalar=1.5, in1=y, op0=ALU.add, op1=ALU.mult))

            LN_LINKS = 3 + RSQRT_LINKS

            def moments(c):
                dve.memset(ryy[:, :], 0.0)
                for t in range(CT):
                    last = dve.bn_stats(stats[:, t, :], X[:, c * CT + t, :])
                ch.link(last)
                dve.memset(rtmp[:, :], 0.0)
                for t in range(CT):
                    last = dve.bn_aggr(mv[:, t, :], stats[:, t, :])
                ch.link(last)
                dve.tensor_scalar(mean[:, bass.ds(c * CT, CT)], mv[:, :, 0], 1.0, None, ALU.mult)
                ch.link(dve.tensor_scalar(var[:, :], mv[:, :, 1], LN_EPS, None, ALU.add))
                rsqrt(ryy[:, :], var[:, :], rtmp[:, :], out=rstd[:, bass.ds(c * CT, CT)])

            def normalise(n, c):
                dve.wait_ge(sem("xn_tp"), FROM + 2 * n)
                for t in range(CT):
                    k = c * CT + t
                    last = dve.tensor_scalar(xn[:, t, :], X[:, k, :], mean[:, bass.ds(k, 1)], rstd[:, bass.ds(k, 1)],
                                             ALU.subtract, ALU.mult)
                last.then_inc(sem("ln_ready"), 1)

            def split_x(n, hi, lo):
                for r in range(2):
                    dve.wait_ge(sem("xT_hi"), 2 * n + r + 1)
                    dve.tensor_tensor(lo[:, r, :], TP[r], hi[:, r, :].bitcast(F32), ALU.subtract).then_inc(sem("xT_lo"), 1)

            def codes(n):
                i, nib, j = W_UNITS[n]
                if nib == 0 and j == 0:
                    dve.wait_ge(sem(f"raw{i}_in"), 32)
                if n >= 2:
                    dve.wait_ge(sem("deq"), n - 1)
                for dst, bits in ((mag, 7), (sgn, 8)):
                    o = dst[:, n % 2, :].bitcast(I32).rearrange("p (a c) -> p a c", a=2)
                    if nib:
                        ins = dve.tensor_scalar(o, packed(i, j), 4, bits, ALU.logical_shift_right, ALU.bitwise_and)
                    else:
                        ins = dve.tensor_scalar(o, packed(i, j), bits, None, ALU.bitwise_and)
                    ins.then_inc(sem("codes"), 1)

            def low_parts(u):
                i, nib, j = W_UNITS[u]
                for k in (2 * j, 2 * j + 1):
                    n = 2 * u + k - 2 * j
                    dve.wait_ge(sem("hi_ready"), n + 1)
                    dve.tensor_tensor(w_slot(i, 1, nib, k), w_psum(i, n),
                                      w_slot(i, 0, nib, k).bitcast(F32), ALU.subtract).then_inc(sem("lo_ready"), 1)

            codes(0)
            for n in range(len(W_UNITS)):
                if n + 1 < len(W_UNITS):
                    codes(n + 1)
                m, v = mag[:, n % 2, :], val[:, n % 2, :]
                dve.wait_ge(sem("val"), n + 1)
                ch.link(dve.scalar_tensor_tensor(out=v, in0=m, scalar=-2.0, in1=v, op0=ALU.add, op1=ALU.max))
                ch.link(dve.scalar_tensor_tensor(out=v, in0=m, scalar=0.5, in1=v, op0=ALU.mult, op1=ALU.max))
                if n >= 1:
                    low_parts(n - 1)
                dve.wait_ge(sem("scaled"), n + 1)
                if n >= 2:
                    dve.wait_ge(sem("w_tp"), 2 * (n - 1))
                dve.tensor_tensor(deq[:, n % 2, :], v, sgn[:, n % 2, :], ALU.mult).then_inc(sem("deq"), 1)
            low_parts(len(W_UNITS) - 1)
            base = ch.k

            dve.wait_ge(sem("x_in"), 16)
            for w, (o, h, i) in enumerate([(wal, wah, sa), (woal, woah, so)]):
                dve.wait_ge(sem("wa_hi"), w + 1)
                dve.tensor_tensor(o[:, :, :], i[:, :, :], h[:, :, :].bitcast(F32), ALU.subtract).then_inc(sem("wa_lo"), 1)
            ch.link(dve.tensor_copy(identr[:, :], ident[:, :]))
            base += 1
            PER_Q = 1 + 1 + 2 + 2
            PER_B = 2 * LN_LINKS + 2 + QUADS * PER_Q
            ch.at(base)
            moments(0)
            normalise(0, 0)
            moments(1)
            base += 2 * LN_LINKS
            with dve.Fori(0, B) as b:
                ch.at(base + b * PER_B)
                for a in range(2):
                    if a == 1:
                        normalise(b * 2 + 1, b * 2 + 1)
                    if a == 0:
                        dve.wait_ge(sem("qkv_mm"), FROM + b * 2 * CT)
                    split_x(b * 2 + a, xTh1, xTl1)
                dve.wait_ge(sem("pads"), 3)
                dve.wait_ge(sem("qkv_ready"), b * TB + TB)
                kk = qkv[:, :, E:E + DA]
                for blk in (0, 64):
                    last = dve.tensor_scalar(kpad[:, :, blk:blk + DA].bitcast(F32R), kk, 0.25, None, ALU.mult)
                ch.link(last)
                for blk in (32, 96):
                    last = dve.scalar_tensor_tensor(out=kpad[:, :, blk:blk + DA].bitcast(F32R), in0=kk, scalar=0.25,
                                                    in1=kpad[:, :, 0:DA], op0=ALU.mult, op1=ALU.subtract)
                dve.tensor_copy(vpad[:, :, 0:DA], qkv[:, :, E + DA:]).then_inc(sem("kv_pad"), 1)
                one = ident[:, :].rearrange("p (a h k) -> p a h k", a=1, h=4).broadcast_to([P, TB, 4, 32])
                ch.link(dve.tensor_tensor(qm[:, :, :, :], one, one, ALU.subtract))

                def queries(q):
                    return qkv[:, :, q * 64:(q + 1) * 64].rearrange("p t (h d) -> p t h d", h=4)

                def pad(q):
                    for blk in (0, 32):
                        last = dve.tensor_copy(qpad[:, :, :, blk:blk + DA], queries(q))
                    ch.link(last)
                    for blk in (64, 96):
                        last = dve.tensor_tensor(qpad[:, :, :, blk:blk + DA], queries(q),
                                                 qpad[:, :, :, 0:DA].bitcast(F32), ALU.subtract)
                    last.then_inc(sem("q_pad"), 1)

                pad(0)
                copies = b * QUADS * (TB + 2)
                n_tp = 0
                for kind, q, n in PLAN:
                    u = b * QUADS + q
                    if kind in "TR":
                        n_tp += 1
                    if (kind, q, n) == ("R", QUADS - 1, 1):
                        for a in range(2):
                            dve.wait_ge(sem("x_updated"), FROM + b * TB)
                            moments((b * 2 + (2 + a)) % CHUNKS)
                        dve.wait_ge(sem("q_tp"), copies + n_tp)
                        normalise(b * 2 + 2, (b * 2 + 2) % CHUNKS)
                    if kind == "P":
                        dve.wait_ge(sem("q_tp"), copies + n_tp)
                        pad(q)
                    elif kind == "M":
                        i, half, h0, nh = MAXES[n]
                        w = min(C, (i + 1) * P - half * C)
                        dve.wait_ge(sem("s_mm"), u * len(MAXES) + n + 1)
                        dve.tensor_reduce(nmax[:, i, half, h0:h0 + nh],
                                          ps[:, 1 + n % 2, 0:nh * w].rearrange("p (h k) -> p h k", h=nh),
                                          AX.X, ALU.max, negate=True).then_inc(sem("maxed"), 1)
                    elif kind == "F":
                        tt = slice(n * CT, (n + 1) * CT)
                        dve.wait_ge(sem("maxed"), u * len(MAXES) + (11 if n == 0 else len(MAXES)))
                        dve.wait_ge(sem("q_tp"), copies + n_tp)
                        src = qkv[:, tt, q * 64:(q + 1) * 64].rearrange("p t (h d) -> p t h d", h=4)
                        dve.tensor_copy(qm[:, tt, :, 0:DA], src)
                        if n == 1:
                            ch.link(dve.tensor_tensor(nmax[:, tt, 0, :], nmax[:, tt, 0, :], nmax[:, tt, 1, :], ALU.min))
                        ch.link(dve.tensor_copy(qm[:, tt, :, 16], nmax[:, tt, 0, :]))
                        dve.tensor_tensor(qm[:, tt, :, 17], nmax[:, tt, 0, :], qm[:, tt, :, 16].bitcast(F32), ALU.subtract)\
                           .then_inc(sem("m_pad"), 1)
                    elif kind == "O":
                        dve.wait_ge(sem("o_tp"), u * 2 + n + 1)
                        if q or n:
                            dve.wait_ge(sem("att"), u * 2 + n)
                        o = TP[0].rearrange("p (t h d) -> p t h d", t=CT, h=4)
                        ch.link(dve.reciprocal(rec[:, :, :], o[:, :, :, 16]))
                        dve.tensor_tensor(
                            qkv[:, n * CT:(n + 1) * CT, q * 64:(q + 1) * 64].rearrange("p t (h d) -> p t h d", h=4),
                            o[:, :, :, 0:DA], rec[:, :, :].rearrange("p t (h d) -> p t h d", d=1).broadcast_to([P, CT, 4, DA]),
                            ALU.mult).then_inc(sem("att"), 1)
                assert ch.k == PER_B, ch.k
                for a in range(2):
                    for r in range(2):
                        dve.wait_ge(sem("att_hi"), b * 4 + a * 2 + r + 1)
                        dve.tensor_tensor(xTl1[:, r, :], TP[r], xTh1[:, r, :].bitcast(F32), ALU.subtract).then_inc(sem("att_lo"), 1)
                    if a == 0:
                        dve.wait_ge(sem("bias_added"), b + 1)
                    for t in range(CT):
                        xt = X[:, b * TB + a * CT + t, :]
                        dve.wait_ge(sem("oproj_mm"), b * TB + a * CT + t + 1)
                        dve.tensor_tensor(xt, xt, ps[:, 6 + t % 2, 0:E], ALU.add).then_inc(sem("x_updated"), 1)
            base += 2 * PER_B
            dve.wait_ge(sem("x_updated"), FROM + TILES)

            def ffn(f, chain, updated, moments_too):
                n0 = CHUNKS + f * (CHUNKS + 1)

                def split_chunk(n, buf):
                    for r in range(2):
                        dve.wait_ge(sem("xT_hi"), 2 * n + r + 1)
                        dve.tensor_tensor(xTl2[:, buf, r, :], TP[r], xTh2[:, buf, r, :].bitcast(F32), ALU.subtract)\
                           .then_inc(sem("xT_lo"), 1)

                split_chunk(n0, 0)
                if f == 1:
                    dve.wait_ge(sem("x_updated"), FROM + updated)
                    ch.at(chain)
                    moments(CHUNKS - 1)
                with dve.Fori(0, CHUNKS // 2) as i:
                    ch.at(chain + i * (3 * LN_LINKS))
                    g = (i + f * 2) * 2 * NT

                    def residual(k):
                        for m in range(2):
                            dve.wait_ge(sem("y_tp"), FROM + ((i + f * 2) * 2 + k) * 2 + m + 1)
                            xt = X[:, bass.ds(i * 2 * CT + (k * CT + 2 * m), 2), :]
                            dve.tensor_tensor(xt, xt, TP[m].rearrange("p (t e) -> p t e", t=2), ALU.add).then_inc(sem("x_updated"), 1)

                    for st in range(2 * NT):
                        k, t = divmod(st, NT)
                        dve.wait_ge(sem("gelu"), FROM + g + st + 1)
                        dve.wait_ge(sem("up_mm"), g + st + 1)
                        dve.tensor_tensor(prod[:, st % 2, :], gel[:, st % 2, :], ps[:, 4 + st % 2, :], ALU.mult)\
                           .then_inc(sem("prod"), 1)
                        dve.wait_ge(sem("in_hi"), g + st + 1)
                        dve.tensor_tensor(inl[:, st % 3, :], prod[:, st % 2, :], inh[:, st % 3, :].bitcast(F32), ALU.subtract)\
                           .then_inc(sem("in_lo"), 1)
                        if st == NT + 3:
                            residual(0)
                        if moments_too and st == NT + 4:
                            dve.wait_ge(sem("x_updated"), FROM + updated + i * 4 + 2)
                            moments(i * 2)
                        if moments_too and st in (5, 11):
                            dve.wait_ge(sem("x_updated"), FROM + updated + i * 4)
                            moments((i * 2 + (2 if st == 11 else 3)) % CHUNKS)
                        if t == FFN_NORM:
                            dve.wait_ge(sem("x_updated"), FROM + updated + i * 4 + 2 * k)
                            normalise(2 * i + (n0 + k + 1), (i * 2 + (k + 1)) % CHUNKS)
                        if t == FFN_SPLIT:
                            split_chunk(2 * i + (n0 + k + 1), 1 - k)
                    residual(1)
                    dve.wait_ge(sem("x_updated"), FROM + updated + i * 4 + 4)

            ffn(0, base, TILES, True)
            base += CHUNKS // 2 * 3 * LN_LINKS

            PER_K = 2 + 1 + RSQRT_LINKS
            PER_M = PER_K + 2 * 2 + 2 + RSQRT_LINKS
            PER_C = CT * (PER_M + 1) + 1 + LN_LINKS

            def token_tile(m, x, par):
                dve.wait_ge(sem("xn1_tp"), m - 1 if not isinstance(m, int) else max(0, m - 1))
                dve.tensor_scalar(xn[:, par, :], X[:, x, :], mean[:, bass.ds(x, 1)], rstd[:, bass.ds(x, 1)],
                                  ALU.subtract, ALU.mult).then_inc(sem("xn1_ready"), 1)

            def squares(m, n):
                dve.wait_ge(sem("proj_out"), m * 6 + n + 1)
                dve.tensor_reduce(ssb[:, 16:20] if n == 0 else ssb[:, 4 * n - 4:4 * n],
                                  sqb[:, n % 2, :].rearrange("p (h d) -> p h d", h=4), AX.X, ALU.add)\
                   .then_inc(sem("ss"), 1)

            def table(n, x, h, lo, hi):
                return tabs[:, n, x, lo:hi].rearrange("p (a d) -> p a d", a=1).broadcast_to([P, h, hi - lo])

            def rope(x, h0, h1, n):
                q, o, h = qk[:, h0:h1, :], rot[:, h0:h1, :], h1 - h0
                dve.tensor_tensor(o[:, :, 0:64], q[:, :, 64:128], table(n + 1, x, h, 0, 64), ALU.mult)
                ch.link(dve.tensor_tensor(o[:, :, 64:128], q[:, :, 0:64], table(n + 1, x, h, 64, 128), ALU.mult))
                ch.link(dve.tensor_tensor(q, q, table(n, x, h, 0, DB), ALU.mult))
                return dve.tensor_tensor(q, q, o, ALU.add)

            def rope_k(x):
                ch.link(rope(x, HB, 20, 2))

            def rope_q(x, half):
                rope(x, 8 * half, 8 * half + 8, 0).then_inc(sem("qk_final"), 1)

            def norm_k(m):
                dve.wait_ge(sem("ss"), m * 5 + 1)
                ch.link(dve.tensor_scalar(ssb[:, HB:20], ssb[:, HB:20], 1.0 / DB, RMS_EPS, ALU.mult, ALU.add))
                rsqrt(rk[:, :], ssb[:, HB:20], rqt[:, 0:KVB])
                q = qk[:, HB:20, :]
                r = rk[:, :].rearrange("p (h d) -> p h d", d=1).broadcast_to([P, KVB, DB])
                dve.tensor_tensor(q, q, r, ALU.mult).then_inc(sem("qk_final"), 1)

            def norm_q(m, par):
                dve.wait_ge(sem("ss"), m * 5 + 5)
                ch.link(dve.tensor_scalar(ssb[:, 0:HB], ssb[:, 0:HB], RMS_EPS * DB, None, ALU.add))
                rsqrt(rq[:, par, :], ssb[:, 0:HB], rqt[:, :])
                ch.link(dve.tensor_scalar(rq[:, par, :], rq[:, par, :], -1.0, None, ALU.mult))

            def prob_half(k):
                dve.wait_ge(sem("p_tp"), FROM + k * 2 + 2)
                dve.wait_ge(sem("pvb"), FROM + k)
                dve.tensor_copy(PT[:, 1, :], TP[1]).then_inc(sem("PT1"), 1)

            def residual(t, x):
                dve.wait_ge(sem("wo_mm"), t * 4 + 2)
                xt = X[:, x, :]
                dve.tensor_tensor(xt, xt, ps[:, 7, 0:E], ALU.add).then_inc(sem("x_updated"), 1)

            def weight_low(n):
                dve.wait_ge(sem("wp_hi"), n + 1)
                dve.tensor_tensor(proj_weights(wqTl, wkvTl, n), proj_weights(wqT, wkvT, n),
                                  proj_weights(wqTh, wkvTh, n).bitcast(F32), ALU.subtract).then_inc(sem("wp_lo"), 1)

            def tokens_low(m, par):
                dve.wait_ge(sem("xT1"), m + 1)
                dve.tensor_tensor(xT1l[:, par, :, :], TP[0][:, 0:E].rearrange("p (r k) -> p r k", r=2),
                                  xT1h[:, par, :, :].bitcast(F32), ALU.subtract).then_inc(sem("xT1l"), 1)

            ch.at(base)
            token_tile(0, 0, 0)
            weight_low(0)
            tokens_low(0, 0)
            token_tile(1, 1, 1)
            for n in (1, 2, 3, 4):
                weight_low(n)
            dve.wait_ge(sem("tab_in"), 96)
            ws = [PT[:, 0, n * DB:(n + 1) * DB].rearrange("p (a d) -> p a d", a=1) for n in range(2)]
            for n in (1, 0):
                w1, w2 = (ws[n][:, :, k * 64:(k + 1) * 64].broadcast_to([P, TB, 64]) for k in range(2))
                co, si = tabs[:, 0, :, 0:64], tabs[:, 0, :, 64:128]
                A, Bt = tabs[:, 2 * n, :, :], tabs[:, 2 * n + 1, :, :]
                if n == 0:
                    co, si = tabs[:, 1, :, 0:64], tabs[:, 1, :, 64:128]
                ch.link(dve.tensor_tensor(A[:, :, 0:64], co, w1, ALU.mult))
                ch.link(dve.tensor_tensor(A[:, :, 64:128], co, w2, ALU.mult))
                ch.link(dve.scalar_tensor_tensor(out=Bt[:, :, 0:64], in0=si, scalar=-1.0, in1=w2, op0=ALU.mult, op1=ALU.mult))
                ch.link(dve.tensor_tensor(Bt[:, :, 64:128], si, w1, ALU.mult))
                for k in ((0, 1) if n else (2, 3, 4)):
                    squares(0, k)
                if n == 0:
                    weight_low(5)
                    tokens_low(1, 1)
            rope_k(0)
            norm_k(0)
            rope_q(0, 0)
            rope_q(0, 1)
            norm_q(0, 0)
            assert ch.k == PER_M + 1 + 8, ch.k
            base += ch.k
            with dve.Fori(0, CHUNKS) as c:
                ch.at(base + c * PER_C)
                ch.link(dve.tensor_copy(first[:, :], window[:, 1 - c % 2, :]))
                for u in range(CT):
                    t = c * CT + u
                    m = c * CT + (u + 1)
                    x = m % TB

                    def maxima(g):
                        dve.wait_ge(sem("expb"), FROM + 4 * (t * 4 + max(0, g - 1)))
                        dve.wait_ge(sem("p_tp"), FROM + 2 * (t * 4 + g))
                        dve.wait_ge(sem("sb_mm"), t * 4 + g + 1)
                        dve.memset(nmx[:, :], 0.0)
                        w = window[:, 2, :] if u % 2 else window[:, 0, :] if u else first[:, :]
                        for h in range(4):
                            last = dve.tensor_tensor_reduce(
                                prb[:, g % 2, h, :], ps[:, 4 + h // 2, (h % 2) * E:(h % 2 + 1) * E], w,
                                rq[:, u % 2, 4 * g + h:4 * g + h + 1], 3.0e38, ALU.add, ALU.min, nmb[:, g % 2, h:h + 1])
                        last.then_inc(sem("nmb"), 1)

                    def sums(g):
                        dve.wait_ge(sem("expb"), FROM + 4 * (t * 4 + g + 1))
                        dve.wait_ge(sem("p_final"), FROM + t * 4 + max(0, g - 1))
                        dve.reciprocal(rcb[:, g % 2, :], rsb[:, g % 2, :]).then_inc(sem("rcb"), 1)

                    maxima(0)
                    prob_half(t * 4)
                    sums(0)
                    token_tile(c * CT + (u + 2), (c * CT + (u + 2)) % TILES, u % 2)
                    if u == 1:
                        dve.wait_ge(sem("x_updated"), FROM + c * CT + (DONE_F + 1))
                        moments((c + (CHUNKS - 1)) % CHUNKS)
                    squares(m, 0)
                    maxima(1)
                    prob_half(t * 4 + 1)
                    rope_k(x)
                    squares(m, 1)
                    sums(1)
                    residual(t, (t + TILES) % (TILES + 1))
                    norm_k(m)
                    squares(m, 2)
                    maxima(2)
                    prob_half(t * 4 + 2)
                    squares(m, 3)
                    sums(2)
                    rope_q(x, 0)
                    tokens_low(c * CT + (u + 2), u % 2)
                    squares(m, 4)
                    maxima(3)
                    prob_half(t * 4 + 3)
                    rope_q(x, 1)
                    sums(3)
                    norm_q(m, (u + 1) % 2)
                assert ch.k == PER_C, (ch.k, PER_C)
            base += CHUNKS * PER_C
            dve.wait_ge(sem("xn1_tp"), TILES + 2)
            normalise(CHUNKS + (CHUNKS + 1), 0)
            prob_half(4 * TILES)
            residual(TILES, TILES - 1)
            ffn(1, base, DONE_B, False)

        @block.tensor
        def _(pe):
            def tp(o, i):
                return pe.transpose(o, i, ident[:, :])

            pe.wait_ge(sem("pool"), 2)
            for u, (i, nib, j) in enumerate(W_UNITS):
                pe.wait_ge(sem("deq"), u + 1)
                for k in (2 * j, 2 * j + 1):
                    n = 2 * u + k - 2 * j
                    if n >= 4:
                        pe.wait_ge(sem("lo_ready"), n - 3)
                    for m in range(4):
                        if i < 2:
                            c0 = (4 * (k - 2 * j) + m) * P
                        else:
                            t2, hh = 2 * k + m // 2, m % 2
                            c0 = hh * 512 + (t2 - 4 * j) * P
                        last = tp(ps[:, n % 4, m * P:(m + 1) * P], deq[:, u % 2, c0:c0 + P])
                    last.then_inc(sem("w_tp"), 1)
                for q in range(4 * u, min(4 * u + 4, 20)):
                    n = WB_ORDER[q]
                    if n == 0:
                        pe.wait_ge(sem("wq_in"), 16)
                    if n == 8:
                        pe.wait_ge(sem("wkv_in"), 32)
                    if n == 12:
                        pe.wait_ge(sem("wo_in"), 16)
                    if q >= 4:
                        pe.wait_ge(sem("wb_ready"), q - 3)
                    for k in range(4):
                        if n < 8:
                            r, h = n // 4, (n % 4) * 4 + k
                            src = wqr[:, h, r::2]
                        elif n < 12:
                            r, m = divmod(n - 8, 2)
                            src = wkvr[:, m, k, r::2]
                        else:
                            h, m = (n - 12) * 2 + k // 2, k % 2
                            src = wor[:, m, h, :]
                        last = tp(ps[:, 4 + q % 4, k * P:(k + 1) * P], src)
                    last.then_inc(sem("wb_tp"), 1)
            pe.wait_ge(sem("pool"), POOL_CONST)

            def transpose_x(n):
                pe.wait_ge(sem("ln_ready"), n + 1)
                for r in range(2):
                    for t in range(CT):
                        last = tp(TP[r][:, t * P:(t + 1) * P], xn[:, t, r::2])
                    last.then_inc(sem("xn_tp"), 1)

            def split_mm(o, lh, ll, rh, rl, start, stop):
                pe.matmul(o, ll, rh, start=start, stop=False)
                pe.matmul(o, lh, rl, start=False, stop=False)
                return pe.matmul(o, lh, rh, start=False, stop=stop)

            pe.wait_ge(sem("wa_lo"), 2)
            with pe.Fori(0, B) as b:
                for a in range(2):
                    cn = b * 2 + a
                    if a == 0:
                        pe.wait_ge(sem("lo_ready"), 24)
                        pe.wait_ge(sem("att_lo"), FROM + b * 4)
                    transpose_x(cn)
                    pe.wait_ge(sem("xT_lo"), 2 * cn + 2)
                    for t in range(CT):
                        if a == 0 and t < 2:
                            pe.wait_ge(sem("x_updated"), FROM + b * TB)
                        else:
                            pe.wait_ge(sem("qkv_ready"), cn * CT + t - 1)
                        tt = slice(t * P, (t + 1) * P)
                        for r in range(2):
                            last = split_mm(ps[:, 6 + t % 2, 0:QKV], xTh1[:, r, tt], xTl1[:, r, tt],
                                            wah[:, r, :], wal[:, r, :], r == 0, r == 1)
                        last.then_inc(sem("qkv_mm"), 1)
                pe.wait_ge(sem("kv_pad"), b + 1)
                for h in range(2):
                    for t in range(4):
                        last = tp(TP[h][:, t * P:(t + 1) * P], kpad[:, h * 4 + t, :])
                    last.then_inc(sem("k_tp"), 1)
                pe.wait_ge(sem("k_ready"), b * 2 + 2)
                copies = b * QUADS * (TB + 2)
                n_copy = 0
                bank0 = None
                tile_copied = {}
                for kind, q, n in PLAN:
                    u = b * QUADS + q
                    if kind in "TRO" and bank0:
                        pe.wait_ge(sem(bank0[0]), bank0[1])
                    if kind == "T":
                        if n == 0:
                            pe.wait_ge(sem("q_pad"), u + 1)
                        for h in range(4):
                            last = pe.transpose(TP[0][:, h * P:(h + 1) * P].bitcast(F32R), qpad[:, n, h, :], identr[:, :])
                        last.then_inc(sem("q_tp"), 1)
                    elif kind == "R":
                        pe.wait_ge(sem("m_pad"), u * 2 + n + 1)
                        for t in range(CT):
                            last = pe.transpose(TP[0][:, t * P:(t + 1) * P].bitcast(F32R),
                                                qm[:, n * CT + t, :, :].rearrange("p h k -> p (h k)"), identr[:, :])
                        last.then_inc(sem("q_tp"), 1)
                    if kind in "TR":
                        n_copy += 1
                        bank0 = ("q_ready", copies + n_copy)
                        tile_copied[kind, q, n] = copies + n_copy
                    elif kind == "M":
                        i, half, h0, nh = MAXES[n]
                        w = min(C, (i + 1) * P - half * C)
                        pe.wait_ge(sem("q_ready"), tile_copied["T", q, i])
                        if q or n >= 2:
                            pe.wait_ge(sem("maxed"), u * len(MAXES) + n - 1)
                        for h in range(h0, h0 + nh):
                            bk = ps[:, 1 + n % 2, (h - h0) * w:(h - h0 + 1) * w]
                            diag = half * C + w == (i + 1) * P
                            last = pe.matmul(bk, qTa[:, q % 2, h, i * P:(i + 1) * P], kTa[:, half * C:half * C + w],
                                             start=True, stop=True)
                            if diag:
                                last = pe.matmul(bk[:, w - P:w], identb[:, :], causal[:, :],
                                                 start=False, stop=True, skip_group_check=True)
                        last.then_inc(sem("s_mm"), 1)
                    elif kind == "S":
                        step, v = divmod(n, 2)
                        cc, j = (0, step) if step < CT else (1, step - CT)
                        w0 = P * max(0, j - CT * cc)
                        pe.wait_ge(sem("q_ready"), tile_copied["R", q, cc])
                        if q or n >= 2:
                            pe.wait_ge(sem("exp"), u * EXPS + n - 1)
                        for h in range(2):
                            bk = ps[:, 3 + 2 * v + h, 0:C - w0]
                            last = pe.matmul(bk, kTa[:, j * P:(j + 1) * P], qTa[:, q % 2, 2 * v + h, cc * C + w0:(cc + 1) * C],
                                             start=True, stop=True)
                            if j >= CT * cc:
                                last = pe.matmul(bk[:, 0:P], identb[:, :], causalT[:, :], start=False, stop=True,
                                                 skip_group_check=True)
                        last.then_inc(sem("sT_mm"), 1)
                    elif kind == "V":
                        cc, j = (0, n) if n < CT else (1, n - CT)
                        w0 = P * max(0, j - CT * cc)
                        pe.wait_ge(sem("exp"), u * EXPS + 2 * n + 2)
                        if j == 0 and (q or cc):
                            pe.wait_ge(sem("o_ready"), u * 2 + cc)
                        for h in range(4):
                            last = pe.matmul(ps[32 * h:32 * h + 32, 7, w0:C], vpad[:, j, :],
                                             prob[:, n % 2, h, 0:C - w0], start=j == 0, stop=j >= CT * cc,
                                             skip_group_check=True)
                        last.then_inc(sem("pv"), 1)
                    elif kind == "O":
                        pe.wait_ge(sem("o_ready"), u * 2 + n + 1)
                        for t in range(CT):
                            last = tp(TP[0][:, t * P:(t + 1) * P], OT[:, t * P:(t + 1) * P])
                        last.then_inc(sem("o_tp"), 1)
                        bank0 = ("att", u * 2 + n + 1)
                pe.wait_ge(sem("att"), (b + 1) * QUADS * 2)
                for a in range(2):
                    if a == 1:
                        pe.wait_ge(sem("att_lo"), FROM + b * 4 + 2)
                    for r in range(2):
                        for t in range(CT):
                            last = tp(TP[r][:, t * P:(t + 1) * P], qkv[:, a * CT + t, r:E:2])
                        last.then_inc(sem("att_tp"), 1)
                    pe.wait_ge(sem("att_lo"), FROM + b * 4 + a * 2 + 2)
                    for t in range(CT):
                        n = a * CT + t
                        if n >= 2:
                            pe.wait_ge(sem("x_updated"), FROM + b * TB + n - 1)
                        tt = slice(t * P, (t + 1) * P)
                        for r in range(2):
                            last = split_mm(ps[:, 6 + t % 2, 0:E], xTh1[:, r, tt], xTl1[:, r, tt],
                                            woah[:, r, :], woal[:, r, :], r == 0, r == 1)
                        last.then_inc(sem("oproj_mm"), 1)

            def ffn(f, updated):
                n0 = CHUNKS + f * (CHUNKS + 1)
                transpose_x(n0)
                if f == 1:
                    pe.wait_ge(sem("wlow_again"), 32)
                    pe.wait_ge(sem("wdh_again"), 16)
                    pe.wait_ge(sem("proj_out"), 5 + 6 * TILES)
                with pe.Fori(0, CHUNKS // 2) as i:
                    g = (i + f * 2) * 2 * NT

                    def hidden(w_h, w_l, bank, k, t):
                        ts = slice(t * P, (t + 1) * P)
                        for r in range(2):
                            last = split_mm(ps[:, bank, :], w_h[:, r, ts], w_l[:, r, ts], xTh2[:, k, r, :], xTl2[:, k, r, :],
                                            r == 0, r == 1)
                        return last

                    def down(st):
                        k, t = divmod(st, NT)
                        if f == 0 and st == NT // 2:
                            pe.wait_ge(sem("wdl_back"), 16)
                        if f == 1 and st == 0:
                            pe.wait_ge(sem("x_updated"), FROM + DONE_B)
                        if f == 1 and st < NT and st % 4 == 0:
                            pe.wait_ge(sem(f"wdl_again{st // 4}"), 16)
                        pe.wait_ge(sem("in_lo"), g + st + 1)
                        if t == 0:
                            pe.wait_ge(sem("y_ready"), FROM + (i + f * 2) * 2 + k)
                        for hh in range(2):
                            hs = slice(hh * P, (hh + 1) * P)
                            last = split_mm(ps[:, 6 + hh, :], wdh[:, t, hs], wdl[:, t, hs], inh[:, st % 3, :], inl[:, st % 3, :],
                                            t == 0, t == NT - 1)
                        last.then_inc(sem("down_mm"), 1)

                    def output(k):
                        pe.wait_ge(sem("y_ready"), FROM + (i + f * 2) * 2 + k + 1)
                        pe.wait_ge(sem("xT_lo"), (2 * i + (n0 + 1 + k)) * 2)
                        for m in range(2):
                            for q in range(4):
                                t, hh = 2 * m + q // 2, q % 2
                                last = tp(TP[m][:, q * P:(q + 1) * P], yT[:, hh, t * P:(t + 1) * P])
                            last.then_inc(sem("y_tp"), 1)

                    for st in range(2 * NT + 2):
                        k, t = divmod(st, NT)
                        if st < 2 * NT:
                            if t == 0:
                                pe.wait_ge(sem("xT_lo"), (2 * i + (n0 + 1 + k)) * 2)
                            pe.wait_ge(sem("gelu"), FROM + g + max(0, st - 1))
                            hidden(wgh, wgl, 2 + st % 2, k, t).then_inc(sem("gate_mm"), 1)
                            pe.wait_ge(sem("prod"), FROM + g + max(0, st - 1))
                            hidden(wuh, wul, 4 + st % 2, k, t).then_inc(sem("up_mm"), 1)
                        if st >= 2:
                            down(st - 2)
                        if st == NT + 2:
                            output(0)
                        if st < 2 * NT and t == FFN_TP:
                            pe.wait_ge(sem("x_updated"), FROM + updated + i * 4 + 2 * k)
                            transpose_x(2 * i + (n0 + 1 + k))
                    pe.wait_ge(sem("xT_lo"), (2 * i + (n0 + 3)) * 2)
                    output(1)

            pe.wait_ge(sem("x_updated"), FROM + TILES)
            ffn(0, TILES)
            pe.wait_ge(sem("wb_back"), 16)
            def tokens(m, par):
                pe.wait_ge(sem("xn1_ready"), m + 1)
                for r in range(2):
                    last = tp(TP[0][:, r * P:(r + 1) * P], xn[:, par, r::2])
                last.then_inc(sem("xn1_tp"), 1)

            def project(j, n, par, bank):
                pe.wait_ge(sem("proj_out"), j - 1 if not isinstance(j, int) else max(0, j - 1))
                wh, wl = proj_weights(wqTh, wkvTh, n), proj_weights(wqTl, wkvTl, n)
                for r in range(2):
                    last = split_mm(ps[:, 2 + bank, :], xT1h[:, par, r, :], xT1l[:, par, r, :], wh[:, r, :], wl[:, r, :],
                                    r == 0, r == 1)
                last.then_inc(sem("proj_mm"), 1)

            def transpose_qk(m, n):
                pe.wait_ge(sem("qk_final"), m * 3 + (1, 2, 2, 3, 3)[n])
                if n >= 2:
                    pe.wait_ge(sem("qkT"), m * 5 + n - 1)
                for k in range(4):
                    h = HB + k if n == 0 else 4 * (n - 1) + k
                    last = tp(TP[n % 2][:, k * P:(k + 1) * P], qk[:, h, :])
                last.then_inc(sem("qk_tp"), 1)

            def transpose_p(k, g, bank_read):
                pe.wait_ge(sem("p_final"), FROM + k)
                for kt in range(2):
                    s, v = bank_read[kt]
                    pe.wait_ge(sem(s), v)
                    for h in range(4):
                        last = tp(TP[kt][:, h * P:(h + 1) * P], prb[:, g % 2, h, kt * P:(kt + 1) * P])
                    last.then_inc(sem("p_tp"), 1)

            def values(k, g):
                pe.wait_ge(sem("oT"), FROM + k)
                for kt in range(2):
                    pe.wait_ge(sem("PT0" if kt == 0 else "PT1"), k + 1)
                    last = pe.matmul(ps[:, 6, :], vb[:, kt, g * DB:(g + 1) * DB], PT[:, kt, :], start=kt == 0, stop=kt == 1)
                last.then_inc(sem("pvb"), 1)

            def wo_part(k, g, read=None):
                pe.wait_ge(sem("oT"), FROM + k)
                if g == 0:
                    pe.wait_ge(sem("x_updated"), FROM + read)
                for h in range(4 * g, 4 * g + 4):
                    last = pe.matmul(ps[:, 7, 0:E], oT[:, h, :], woT[:, h, :], start=h == 0, stop=h == HB - 1,
                                     skip_group_check=True)
                last.then_inc(sem("wo_mm"), 1)

            pe.wait_ge(sem("x_updated"), FROM + DONE_F)
            tokens(0, 0)
            pe.wait_ge(sem("xT1l"), 1)
            for n in range(5):
                pe.wait_ge(sem("wp_lo"), n + 1)
                project(n, n, 0, n % 2)
            tokens(1, 1)
            pe.wait_ge(sem("xT1l"), 2)
            pe.wait_ge(sem("wp_lo"), 6)
            pe.wait_ge(sem("blank"), 5)
            for n in range(5):
                transpose_qk(0, n)
            with pe.Fori(0, CHUNKS) as c:
                for u in range(CT):
                    t = c * CT + u
                    m = c * CT + (u + 1)
                    k = t * 4
                    nx = (u + 1) % 2

                    def scores(g):
                        pe.wait_ge(sem("qkT"), t * 5 + g + 2)
                        pe.wait_ge(sem("nmb"), FROM + k + g)
                        for h in range(4):
                            o = ps[:, 4 + h // 2, (h % 2) * E:(h % 2 + 1) * E]
                            last = pe.matmul(o.rearrange("p (a k) -> p a k", a=2), qTb[:, 4 * g + h, :], kTb[:, :, g, :],
                                             start=True, stop=True)
                        last.then_inc(sem("sb_mm"), 1)

                    def unit(j, n, par):
                        project(t * 6 + (5 + j), n, par, (j + 1) % 2)

                    scores(0)
                    transpose_p(k, 3, [("qkT", t * 5 + 5)] * 2)
                    wo_part(k, 2)
                    unit(0, 5, u % 2)
                    values(k, 3)
                    pe.wait_ge(sem("xT1l"), c * CT + (u + 2))
                    unit(1, 0, nx)
                    unit(2, 1, nx)
                    scores(1)
                    transpose_p(k + 1, 0, [("PT0", k + 1), ("PT1", k + 1)])
                    wo_part(k + 1, 3)
                    unit(3, 2, nx)
                    values(k + 1, 0)
                    unit(4, 3, nx)
                    scores(2)
                    transpose_p(k + 2, 1, [("PT0", k + 2), ("PT1", k + 2)])
                    wo_part(k + 2, 0, t + (DONE_F + 1))
                    unit(5, 4, nx)
                    pe.wait_ge(sem("PT0"), k + 3)
                    tokens(c * CT + (u + 2), u % 2)
                    values(k + 2, 1)
                    scores(3)
                    transpose_p(k + 3, 2, [("xT1l", c * CT + (u + 3)), ("PT1", k + 3)])
                    wo_part(k + 3, 1)
                    pe.wait_ge(sem("PT0"), k + 4)
                    transpose_qk(m, 0)
                    pe.wait_ge(sem("PT1"), k + 4)
                    transpose_qk(m, 1)
                    values(k + 3, 2)
                    for n in (2, 3, 4):
                        transpose_qk(m, n)
            k = 4 * TILES
            transpose_p(k, 3, [("qkT", TILES * 5 + 5)] * 2)
            wo_part(k, 2)
            values(k, 3)
            wo_part(k + 1, 3)
            ffn(1, DONE_B)

_ORDER = ["L0_attn_a_x", "L0_attn_a_Wq", "L0_attn_a_Wk", "L0_attn_a_Wv", "L0_attn_a_Wo", "L0_attn_a_bo",
          "L0_attn_b_wq", "L0_attn_b_wk", "L0_attn_b_wv", "L0_attn_b_wo", "L0_attn_b_q_norm_w", "L0_attn_b_k_norm_w",
          "L0_ffn_gate_W_packed", "L0_ffn_gate_scales", "L0_ffn_up_W_packed", "L0_ffn_up_scales",
          "L0_ffn_down_W_packed", "L0_ffn_down_scales"]


def kernel(**inputs):
    import numpy as np
    import concourse.bacc as bacc
    from concourse.bass_utils import run_bass_kernel_spmd

    nc = bacc.Bacc("TRN2", target_bir_lowering=False, num_devices=1)
    arrays, args = {}, []

    def put(name, a):
        arrays[name] = a
        args.append(nc.dram_tensor(name, a.shape, mybir.dt.from_np(a.dtype), kind="ExternalInput").ap())

    for name in _ORDER:
        put(name, np.ascontiguousarray(inputs[name]))
    freq = (1.0 / np.float32(10000.0) ** (np.arange(0, DB, 2, dtype=np.float32) / np.float32(DB))).astype(np.float32)
    angle = (np.arange(T, dtype=np.float32)[:, None] * freq[None, :]).astype(np.float32)
    put("rope_cos", np.cos(angle).astype(np.float32))
    put("rope_sin", np.sin(angle).astype(np.float32))
    out = nc.dram_tensor("out", (B, T, E), F32, kind="ExternalOutput").ap()
    build(nc, *args, out)
    r = run_bass_kernel_spmd(nc, [arrays], core_ids=[0])
    return r.results[0]["out"]
```
